# Optimizing a Trainium2 kernel written in Bass

```python
import numpy as np
import jax
import jax.numpy as jnp

def _softmax(x, axis=-1):
    return jax.nn.softmax(x, axis=axis)

def _gelu(x):
    return jax.nn.gelu(x, approximate=True)

def _silu(x):
    return jax.nn.silu(x)

def _sigmoid(x):
    return jax.nn.sigmoid(x)

def _layernorm(x, axis=-1, eps=1e-05):
    m = jnp.mean(x, axis=axis, keepdims=True)
    v = jnp.var(x, axis=axis, keepdims=True)
    return (x - m) / jnp.sqrt(v + eps)

def _scatter_add(tgt, idx, src, axis=0):
    return tgt.at[idx].add(src)

def _segment_sum(src, seg, n):
    return jax.ops.segment_sum(src, seg, n)
kernel_name = 'mk_gnn_preln_d2_gnn_r32_084715'

def setup_inputs(seed: int=0):
    np.random.seed(seed)
    _w = jnp.asarray

    def _rec_inputs():
        import jax
        import jax.numpy as jnp
        _gk = jax.random.key(seed)
        x = -0.000202 + 1 * jax.random.normal(jax.random.fold_in(_gk, 1), (3125, 128), jnp.float32)
        src = jax.random.randint(jax.random.fold_in(_gk, 2), (100000,), 0, 3125, jnp.int32)
        dst = jax.random.randint(jax.random.fold_in(_gk, 3), (100000,), 0, 3125, jnp.int32)
        _o = jnp.argsort(dst, stable=True)
        src = src[_o]
        dst = dst[_o]
        edge_type_200 = jax.random.randint(jax.random.fold_in(_gk, 13), (100000,), 0, 200, jnp.int32)
        edge_weight1 = jax.random.uniform(jax.random.fold_in(_gk, 14), (100000, 1), jnp.float32, 0.0, 0.999998)
        return (x, src, dst, edge_type_200, edge_weight1)
    x, src, dst, edge_type_200, edge_weight1 = _rec_inputs()

    def _L0_gnn_setup():
        import jax, jax.numpy as jnp
        import numpy as np
        N, E, H, O, R, B = (50000, 18750, 128, 128, 200, 8)

        def _rel_layer(h, src, dst, etype, norm, V, comp, loop_w, bias, activation):
            c = comp[etype]
            num_bases, out_dim = (V.shape[0], V.shape[2])
            m = jnp.zeros((src.shape[0], out_dim), h.dtype)
            for b in range(num_bases):
                xb = h @ V[b]
                m = m + c[:, b, None] * xb[src]
            m = m * norm
            agg = jax.ops.segment_sum(m, dst, num_segments=h.shape[0])
            out = agg + bias + h @ loop_w
            return jax.nn.relu(out) if activation else out
        key = jax.random.key(seed)
        ks = jax.random.split(key, 13)
        s = 1.0 / np.sqrt(H).astype(np.float32)
        sb = 1.0 / np.sqrt(B).astype(np.float32)
        return {'feats': jax.random.normal(ks[0], (N, H), jnp.float32), 'src': jax.random.randint(ks[1], (E,), 0, N, jnp.int32), 'dst': jax.random.randint(ks[2], (E,), 0, N, jnp.int32), 'etype': jax.random.randint(ks[3], (E,), 0, R, jnp.int32), 'norm': jax.random.uniform(ks[4], (E, 1), jnp.float32), 'V1': jax.random.normal(ks[5], (B, H, H), jnp.float32) * s, 'comp1': jax.random.normal(ks[6], (R, B), jnp.float32) * sb, 'loop1': jax.random.normal(ks[7], (H, H), jnp.float32) * s, 'bias1': jnp.zeros((H,), jnp.float32), 'V2': jax.random.normal(ks[8], (B, H, O), jnp.float32) * s, 'comp2': jax.random.normal(ks[9], (R, B), jnp.float32) * sb, 'loop2': jax.random.normal(ks[10], (H, O), jnp.float32) * s, 'bias2': jnp.zeros((O,), jnp.float32)}
    _L0_gnn_all = _L0_gnn_setup()
    _L0_gnn_in = {k: v for k, v in _L0_gnn_all.items() if k in ('V1', 'comp1', 'loop1', 'bias1', 'V2', 'comp2', 'loop2', 'bias2')}
    del _L0_gnn_all

    def _L1_gnn_setup():
        import jax, jax.numpy as jnp
        import numpy as np
        N_NODES = 3125
        N_EDGES = 50000
        IN_DIM = 128
        HID_DIM = 128

        def _gcn_norm(edge_index, num_nodes):
            loops = jnp.arange(num_nodes, dtype=edge_index.dtype)
            src = jnp.concatenate([edge_index[0], loops])
            dst = jnp.concatenate([edge_index[1], loops])
            deg = jax.ops.segment_sum(jnp.ones_like(dst, dtype=jnp.float32), dst, num_segments=num_nodes)
            dinv = jnp.where(deg > 0, jax.lax.rsqrt(deg), 0.0)
            norm = dinv[src] * dinv[dst]
            return (src, dst, norm)

        def _gcn_conv(x, W, b, src, dst, norm, num_nodes):
            h = x @ W
            msg = h[src] * norm[:, None]
            out = jax.ops.segment_sum(msg, dst, num_segments=num_nodes)
            return out + b
        key = jax.random.key(seed)
        k_x, k_e, k_w1, k_w2 = jax.random.split(key, 4)
        x = jax.random.normal(k_x, (N_NODES, IN_DIM), dtype=jnp.float32)
        edge_index = jax.random.randint(k_e, (2, N_EDGES), 0, N_NODES, dtype=jnp.int64)
        s1 = 1.0 / np.sqrt(IN_DIM)
        s2 = 1.0 / np.sqrt(HID_DIM)
        W1 = jax.random.uniform(k_w1, (IN_DIM, HID_DIM), jnp.float32, -s1, s1)
        b1 = jnp.zeros((HID_DIM,), jnp.float32)
        W2 = jax.random.uniform(k_w2, (HID_DIM, HID_DIM), jnp.float32, -s2, s2)
        b2 = jnp.zeros((HID_DIM,), jnp.float32)
        return {'x': x, 'edge_index': edge_index, 'W1': W1, 'b1': b1, 'W2': W2, 'b2': b2}
    _L1_gnn_all = _L1_gnn_setup()
    _L1_gnn_in = {k: v for k, v in _L1_gnn_all.items() if k in ('W1', 'b1', 'W2', 'b2')}
    del _L1_gnn_all
    return {'x': x, 'src': src, 'dst': dst, 'edge_type_200': edge_type_200, 'edge_weight1': edge_weight1, 'L0_gnn_V1': _L0_gnn_in['V1'], 'L0_gnn_comp1': _L0_gnn_in['comp1'], 'L0_gnn_loop1': _L0_gnn_in['loop1'], 'L0_gnn_bias1': _L0_gnn_in['bias1'], 'L0_gnn_V2': _L0_gnn_in['V2'], 'L0_gnn_comp2': _L0_gnn_in['comp2'], 'L0_gnn_loop2': _L0_gnn_in['loop2'], 'L0_gnn_bias2': _L0_gnn_in['bias2'], 'L1_gnn_W1': _L1_gnn_in['W1'], 'L1_gnn_b1': _L1_gnn_in['b1'], 'L1_gnn_W2': _L1_gnn_in['W2'], 'L1_gnn_b2': _L1_gnn_in['b2']}

def reference(x, src, dst, edge_type_200, edge_weight1, L0_gnn_V1, L0_gnn_comp1, L0_gnn_loop1, L0_gnn_bias1, L0_gnn_V2, L0_gnn_comp2, L0_gnn_loop2, L0_gnn_bias2, L1_gnn_W1, L1_gnn_b1, L1_gnn_W2, L1_gnn_b2):
    import jax
    import jax.numpy as jnp

    def _L0_gnn_ref(feats, src, dst, etype, norm, V1, comp1, loop1, bias1, V2, comp2, loop2, bias2):
        import jax, jax.numpy as jnp
        import numpy as np
        N, E, H, O, R, B = (50000, 18750, 128, 128, 200, 8)

        def _rel_layer(h, src, dst, etype, norm, V, comp, loop_w, bias, activation):
            c = comp[etype]
            num_bases, out_dim = (V.shape[0], V.shape[2])
            m = jnp.zeros((src.shape[0], out_dim), h.dtype)
            for b in range(num_bases):
                xb = h @ V[b]
                m = m + c[:, b, None] * xb[src]
            m = m * norm
            agg = jax.ops.segment_sum(m, dst, num_segments=h.shape[0])
            out = agg + bias + h @ loop_w
            return jax.nn.relu(out) if activation else out
        h = _rel_layer(feats, src, dst, etype, norm, V1, comp1, loop1, bias1, True)
        h = _rel_layer(h, src, dst, etype, norm, V2, comp2, loop2, bias2, False)
        return h

    def _L1_gnn_ref(x, edge_index, W1, b1, W2, b2):
        import jax, jax.numpy as jnp
        import numpy as np
        N_NODES = 3125
        N_EDGES = 50000
        IN_DIM = 128
        HID_DIM = 128

        def _gcn_norm(edge_index, num_nodes):
            loops = jnp.arange(num_nodes, dtype=edge_index.dtype)
            src = jnp.concatenate([edge_index[0], loops])
            dst = jnp.concatenate([edge_index[1], loops])
            deg = jax.ops.segment_sum(jnp.ones_like(dst, dtype=jnp.float32), dst, num_segments=num_nodes)
            dinv = jnp.where(deg > 0, jax.lax.rsqrt(deg), 0.0)
            norm = dinv[src] * dinv[dst]
            return (src, dst, norm)

        def _gcn_conv(x, W, b, src, dst, norm, num_nodes):
            h = x @ W
            msg = h[src] * norm[:, None]
            out = jax.ops.segment_sum(msg, dst, num_segments=num_nodes)
            return out + b
        n = x.shape[0]
        src, dst, norm = _gcn_norm(edge_index, n)
        h = _gcn_conv(x, W1, b1, src, dst, norm, n)
        h = jax.nn.relu(h)
        return _gcn_conv(h, W2, b2, src, dst, norm, n)
    edge_index = jnp.stack([src, dst])
    h = jnp.maximum(_layernorm(x, axis=-1), 0.0)
    x = x + _L0_gnn_ref(h, src, dst, edge_type_200, edge_weight1, L0_gnn_V1, L0_gnn_comp1, L0_gnn_loop1, L0_gnn_bias1, L0_gnn_V2, L0_gnn_comp2, L0_gnn_loop2, L0_gnn_bias2)
    h = jnp.maximum(_layernorm(x, axis=-1), 0.0)
    x = x + _L1_gnn_ref(h, edge_index, L1_gnn_W1, L1_gnn_b1, L1_gnn_W2, L1_gnn_b2)
    return x

_drawn_inputs = setup_inputs


def setup_inputs(seed=0):
    import zlib

    import numpy as np

    out = dict(_drawn_inputs(seed))
    spreads = {'L0_gnn_bias1': (0.0, 0.1),
     'L0_gnn_bias2': (0.0, 0.483),
     'L1_gnn_b1': (0.0, 0.8),
     'L1_gnn_b2': (0.0, 0.439)}
    factors = {'L1_gnn_W1': 5.214, 'L1_gnn_W2': 3.276}
    for name, (base, spread) in spreads.items():
        noise = np.random.default_rng([zlib.crc32(name.encode()), seed]).standard_normal(out[name].shape)
        drawn = base * np.exp(spread * noise) if base else spread * noise
        out[name] = jnp.asarray(drawn.astype(out[name].dtype))
    for name, factor in factors.items():
        out[name] = (out[name] * factor).astype(out[name].dtype)
    return out
```

```python
from contextlib import ExitStack

import concourse.bass as bass
import numpy as np
from concourse import mybir

ALU = mybir.AluOpType
ACT = mybir.ActivationFunctionType
AX = mybir.AxisListType
F32, F16, BF16, I32 = mybir.dt.float32, mybir.dt.float16, mybir.dt.bfloat16, mybir.dt.int32

P = 128
N, D, E, R, NB = 3125, 128, 100000, 200, 8
GROUPS = -(-N // P)
LAST_ROWS = N - (GROUPS - 1) * P
TILES = 784
RAW = 7
WIN = 16
WPG = P // WIN
WINDOWS = GROUPS * WPG
SPAN = 6
CHUNK = 16
RING = 4 * CHUNK
CHUNKS = TILES // CHUNK
SRC_BLOCKS = GROUPS
AW = SRC_BLOCKS * WIN
ET = 8
ET_CHUNKS = TILES // ET
RH = R // 2
PAD_DST = 4000
EPS = 1e-5


def after(eng, sem, value):
    if isinstance(value, int) and value <= 0:
        return
    eng.wait_ge(sem, value)


class Chain:

    def __init__(self, eng, sem, base=0):
        self.eng, self.sem, self.at = eng, sem, base

    def link(self, ins):
        self.at = self.at + 1
        ins.then_inc(self.sem, 1)
        self.eng.wait_ge(self.sem, self.at)


def flat(ap):
    return ap.rearrange("p a b -> p (a b)")


def one(ap, g):
    if isinstance(g, int):
        return ap[:, g, :]
    return ap[:, bass.ds(g, 1), :].rearrange("p a b -> p (a b)")


def prepare(nc, io, t):
    x, src, dst, norm = io["x"], io["src"], io["dst"], io["edge_weight1"]
    with ExitStack() as ctx:
        sb = lambda n, s, d: ctx.enter_context(nc.sbuf_tensor("pre_" + n, s, d))
        sem = lambda n: ctx.enter_context(nc.semaphore("pre_" + n))
        raw_src, raw_dst = sb("raw_src", [P, RAW, P], I32), sb("raw_dst", [P, RAW, P], I32)
        raw_norm = sb("raw_norm", [P, RAW, P], F32)
        src_f, dst_f = sb("src_f", [P, RAW, P], F32), sb("dst_f", [P, RAW, P], F32)
        stats, mv = sb("stats", [P, GROUPS, 6], F32), sb("mv", [P, GROUPS, 2], F32)
        rstd = sb("rstd", [P, GROUPS], F32)
        t_max, t_min, tile_id = sb("t_max", [P, RAW], F32), sb("t_min", [P, RAW], F32), sb("tile_id", [P, RAW], F32)
        win_lo, ring_lo = sb("win_lo", [P, WINDOWS], F32), sb("ring_lo", [P, WINDOWS], F32)
        kk = sb("kk", [P, 8], F32)
        before = sb("before", [P, RAW, WINDOWS], BF16)
        va, vb = sb("va", [P, RAW, WINDOWS], F32), sb("vb", [P, RAW, WINDOWS], F32)
        vc = sb("vc", [P, RAW, WINDOWS], F32)
        first = sb("first", [P, WINDOWS], F32)
        r1, r2 = sb("r1", [P, WINDOWS], F32), sb("r2", [P, WINDOWS], F32)
        bad, bad2 = sb("bad", [P, 1], F32), sb("bad2", [P, 1], F32)
        pos_f = sb("pos_f", [P, WINDOWS, 8], F32)
        ones_bf = sb("ones_bf", [P, P], BF16)
        ia, ib, dst_i = sb("ia", [P, TILES], I32), sb("ib", [P, TILES], I32), sb("dst_i", [P, TILES], I32)
        fa, fb = sb("fa", [P, TILES], F32), sb("fb", [P, TILES], F32)
        comp = sb("comp", [RH, 2, 2 * NB], F32)
        rest = sb("rest", [RH, 2, 2 * NB], F32)

        ps = lambda n: ctx.enter_context(nc.psum_tensor("pre_" + n, [P, 512], F32))
        ps_src, ps_dst, ps_norm = [ps("s0"), ps("s1")], [ps("d0"), ps("d1")], [ps("n0"), ps("n1")]
        ps_first, ps_bad = ps("ps_first"), ps("ps_bad")

        pads_set, consts_set = sem("pads_set"), sem("consts_set")
        x_in, src_in, dst_in, norm_in = sem("x_in"), sem("src_in"), sem("dst_in"), sem("norm_in")
        w_in, comp_in = sem("w_in"), sem("comp_in")
        ve, ve_ln = sem("vector_chain"), sem("centred")
        var_ready, sd_ready, h_ready, h_out = sem("var_ready"), sem("sd_ready"), sem("h_ready"), sem("h_out")
        srcf_ready, dstf_ready, src_t, dst_t, norm_t = (sem(n) for n in ("srcf", "dstf", "src_t", "dst_t", "norm_t"))
        before_ready, first_done, bad_ready, bad_done = (sem(n) for n in ("before", "first_done", "bad_ready", "bad_done"))
        full = (RAW - 1) * P * P
        rows = (E - full) // P
        tail = E - full - rows * P

        block = ctx.enter_context(nc.Block())

        def edge_loads(eng, raw, flat_dram, done):
            eng.dma_start(raw[:, 0:RAW - 1, :], flat_dram[0:full].rearrange("(c q e) -> q c e", q=P, e=P)).then_inc(done, 16)
            eng.dma_start(raw[0:rows, RAW - 1, :], flat_dram[full:full + rows * P].rearrange("(q e) -> q e", e=P)).then_inc(done, 16)
            eng.dma_start(raw[rows:rows + 1, RAW - 1, 0:tail], flat_dram[full + rows * P:E].rearrange("(q e) -> q e", q=1)).then_inc(done, 16)

        @block.sync
        def _(sp):
            sp.dma_start(t.X[:, 0:GROUPS - 1, :], x[0:(GROUPS - 1) * P, :].rearrange("(g p) d -> p g d", p=P)).then_inc(x_in, 16)
            sp.wait_ge(pads_set, 4)
            sp.dma_start(t.X[0:LAST_ROWS, GROUPS - 1, :], x[(GROUPS - 1) * P:N, :]).then_inc(x_in, 16)
            edge_loads(sp, raw_dst, dst, dst_in)
            edge_loads(sp, raw_norm, norm.rearrange("e a -> (e a)"), norm_in)
            for i, name in enumerate(("L0_gnn_V1", "L0_gnn_V2")):
                sp.dma_start(t.V[i][:, :, :], io[name].rearrange("b d o -> d b o")).then_inc(w_in, 16)
            for i, name in enumerate(("L0_gnn_loop1", "L0_gnn_loop2", "L1_gnn_W1", "L1_gnn_W2")):
                sp.dma_start(t.W[i][:, :], io[name]).then_inc(w_in, 16)
            for i, name in enumerate(("L0_gnn_bias1", "L0_gnn_bias2")):
                sp.dma_start(t.bias_row[i][:, :], io[name].rearrange("(a n) -> a n", a=1)).then_inc(w_in, 16)
            for i, name in enumerate(("L1_gnn_b1", "L1_gnn_b2")):
                sp.dma_start(t.bias_all[i][:, :], io[name].rearrange("(a n) -> a n", a=1).to_broadcast([P, D])).then_inc(w_in, 16)
            sp.wait_ge(h_ready, 1)
            sp.dma_start(t.h1_dram.rearrange("(g p) d -> p g d", p=P), t.H[:, :, :]).then_inc(h_out, 16)
            sp.wait_ge(w_in, 10 * 16)
            sp.wait_ge(h_out, 16)

        @block.scalar
        def _(act):
            for l, name in enumerate(("L0_gnn_comp1", "L0_gnn_comp2")):
                for h in range(2):
                    act.dma_start(comp[:, h, l * NB:(l + 1) * NB], io[name][h * RH:(h + 1) * RH, :]).then_inc(comp_in, 16)
            act.wait_ge(pads_set, 4)
            edge_loads(act, raw_src, src, src_in)
            act.wait_ge(var_ready, 1)
            nc.scalar.activation(rstd[:, :], rstd[:, :], ACT.Sqrt).then_inc(sd_ready, 1)
            act.wait_ge(ve_ln, 1)
            nc.scalar.activation(t.H[:, :, :], t.H[:, :, :], ACT.Relu).then_inc(h_ready, 1)

        @block.gpsimd
        def _(pool):
            g = nc.gpsimd
            g.memset(t.X[:, GROUPS - 1, :], 0.0).then_inc(pads_set, 1)
            g.memset(raw_src[:, RAW - 1, :], 0).then_inc(pads_set, 1)
            g.memset(raw_dst[:, RAW - 1, :], PAD_DST).then_inc(pads_set, 1)
            g.memset(raw_norm[:, RAW - 1, :], 0.0).then_inc(pads_set, 1)
            g.memset(t.ident[:, :], 0.0).then_inc(consts_set, 1)
            g.memset(t.ones[:, :], 1.0).then_inc(consts_set, 1)
            g.memset(ones_bf[:, :], 1.0).then_inc(consts_set, 1)
            g.memset(t.ones16[:, :], 1.0).then_inc(consts_set, 1)
            pool.wait_ge(consts_set, 4)
            g.affine_select(out=t.ident[:, :], in_=t.ident[:, :], compare_op=ALU.not_equal, fill=1.0, base=0,
                            pattern=[[-1, P]], channel_multiplier=1).then_inc(consts_set, 1)
            io_ = lambda out, pattern, base=0, cm=0: g.iota(out, pattern=pattern, base=base, channel_multiplier=cm,
                                                           allow_small_or_imprecise_dtypes=True).then_inc(consts_set, 1)
            io_(win_lo[:, :], [[WIN, WINDOWS]])
            io_(tile_id[:, :], [[P, RAW]], cm=1)
            io_(ring_lo[:, :], [[CHUNK, WINDOWS // 4], [0, 4]], base=-CHUNK)
            io_(kk[:, :], [[1, 8]])
            io_(t.neg_win[:, :], [[-WIN, WINDOWS]])
            io_(t.win512[:, :], [[512, WINDOWS]])
            io_(t.iota16[:, :], [[1, WIN]])
            io_(t.iota400[:, :], [[1, AW]])
            io_(t.iota128[:, :], [[1, P]])
            io_(t.type_id[:, :], [[RH, 2]], cm=1)
            io_(t.group_lo[:, :], [[P, GROUPS]])

        @block.tensor
        def _(pe):
            m = nc.tensor
            pe.wait_ge(before_ready, 1)
            for c in range(RAW):
                ins = m.matmul(ps_first[:, 0:WINDOWS], ones_bf[:, :], before[:, c, :], start=(c == 0), stop=(c == RAW - 1))
            ins.then_inc(first_done, 1)

            def turn(blocks, ps_pair, done):
                for c in range(RAW):
                    ins = m.transpose(ps_pair[c // 4][:, c % 4 * P:(c % 4 + 1) * P], blocks[:, c, :], t.ident[:, :])
                ins.then_inc(done, 1)

            pe.wait_ge(srcf_ready, 1)
            turn(src_f, ps_src, src_t)
            pe.wait_ge(dstf_ready, 1)
            turn(dst_f, ps_dst, dst_t)
            pe.wait_ge(norm_in, 48)
            turn(raw_norm, ps_norm, norm_t)
            pe.wait_ge(bad_ready, 1)
            m.matmul(ps_bad[:, 0:1], t.ones[:, :], bad[:, :], start=True, stop=True).then_inc(bad_done, 1)

        @block.vector
        def _(dve):
            v = nc.vector
            k = Chain(dve, ve)
            dve.wait_ge(x_in, 32)
            for g in range(GROUPS):
                ins = v.bn_stats(stats[:, g, :], t.X[:, g, :])
            k.link(ins)
            for g in range(GROUPS):
                ins = v.bn_aggr(mv[:, g, :], stats[:, g, :])
            k.link(ins)
            v.tensor_scalar(rstd[:, :], mv[:, :, 1], EPS, None, ALU.add).then_inc(var_ready, 1)
            dve.wait_ge(dst_in, 48)
            v.tensor_copy(dst_f[:, :, :], raw_dst[:, :, :]).then_inc(dstf_ready, 1)
            dve.wait_ge(sd_ready, 1)
            k.link(v.reciprocal(rstd[:, :], rstd[:, :]))
            for g in range(GROUPS):
                ins = v.tensor_scalar(t.H[:, g, :], t.X[:, g, :], mv[:, g, 0:1], rstd[:, g:g + 1], ALU.subtract, ALU.mult)
            ins.then_inc(ve_ln, 1)
            dve.wait_ge(src_in, 48)
            v.tensor_copy(src_f[:, :, :], raw_src[:, :, :]).then_inc(srcf_ready, 1)
            dve.wait_ge(dstf_ready, 1)
            v.tensor_reduce(t_max[:, :], dst_f[:, :, :], AX.X, ALU.max)
            k.link(v.tensor_reduce(t_min[:, :], dst_f[:, :, :], AX.X, ALU.min))
            dve.wait_ge(consts_set, 16)
            wide = [P, RAW, WINDOWS]
            v.tensor_tensor(before[:, :, :], t_max[:, :].unsqueeze(2).to_broadcast(wide),
                            win_lo[:, :].unsqueeze(1).to_broadcast(wide), ALU.is_lt).then_inc(before_ready, 1)
            k.link(v.scalar_tensor_tensor(out=va[:, :, :], in0=win_lo[:, :].unsqueeze(1).to_broadcast(wide), scalar=float(WIN),
                                          in1=t_min[:, :].unsqueeze(2).to_broadcast(wide), op0=ALU.add, op1=ALU.is_gt))
            dve.wait_ge(before_ready, 1)
            k.link(v.tensor_tensor(va[:, :, :], va[:, :, :], before[:, :, :], ALU.subtract))
            dve.wait_ge(first_done, 1)
            k.link(v.tensor_scalar(first[:, :], ps_first[:, 0:WINDOWS], float(TILES - SPAN), None, ALU.min))
            k.link(v.tensor_tensor(vb[:, :, :], first[:, :].unsqueeze(1).to_broadcast(wide),
                                   tile_id[:, :].unsqueeze(2).to_broadcast(wide), ALU.subtract))
            k.link(v.tensor_scalar(vc[:, :, :], vb[:, :, :], 0.0, None, ALU.is_gt))
            k.link(v.scalar_tensor_tensor(out=vc[:, :, :], in0=vb[:, :, :], scalar=float(1 - SPAN), in1=vc[:, :, :],
                                          op0=ALU.is_lt, op1=ALU.add))
            k.link(v.tensor_tensor(va[:, :, :], va[:, :, :], vc[:, :, :], ALU.mult))
            k.link(v.tensor_reduce(bad[:, :], va[:, :, :], AX.XY, ALU.add))
            k.link(v.tensor_tensor(r1[:, :], first[:, :], ring_lo[:, :], ALU.is_lt))
            k.link(v.scalar_tensor_tensor(out=r2[:, :], in0=first[:, :], scalar=float(SPAN - 3 * CHUNK), in1=ring_lo[:, :],
                                          op0=ALU.add, op1=ALU.is_gt))
            k.link(v.tensor_tensor(r1[:, :], r1[:, :], r2[:, :], ALU.add))
            k.link(v.tensor_reduce(bad2[:, :], r1[:, :], AX.X, ALU.add))
            v.tensor_tensor(bad[:, :], bad[:, :], bad2[:, :], ALU.add).then_inc(bad_ready, 1)
            k.link(v.tensor_tensor(pos_f[:, :, :], first[:, :].unsqueeze(2).to_broadcast([P, WINDOWS, 8]),
                                   kk[:, :].unsqueeze(1).to_broadcast([P, WINDOWS, 8]), ALU.add))
            k.link(v.tensor_copy(t.pos[:, :, :], pos_f[0:1, :, :]))
            k.link(v.tensor_single_scalar(t.pos[:, :, :], t.pos[:, :, :], RING - 1, ALU.bitwise_and))
            k.link(v.tensor_copy(t.first[:, :], first[0:1, :]))
            cut = 4 * P

            def column(out, pair):
                v.tensor_copy(out[:, 0:cut], pair[0][:, :])
                k.link(v.tensor_copy(out[:, cut:TILES], pair[1][:, 0:TILES - cut]))

            dve.wait_ge(src_t, 1)
            column(t.idx, ps_src)
            dve.wait_ge(dst_t, 1)
            column(t.dst, ps_dst)
            column(dst_i, ps_dst)
            dve.wait_ge(norm_t, 1)
            column(t.norm, ps_norm)
            k.link(v.tensor_single_scalar(ia[:, :], t.idx[:, :], P - 1, ALU.bitwise_and))
            k.link(v.tensor_copy(t.src_lo[:, :], ia[:, :]))
            k.link(v.tensor_single_scalar(ib[:, :], t.idx[:, :], 7, ALU.logical_shift_right))
            k.link(v.tensor_copy(fa[:, :], ib[:, :]))
            k.link(v.tensor_single_scalar(ia[:, :], dst_i[:, :], WIN - 1, ALU.bitwise_and))
            k.link(v.tensor_copy(fb[:, :], ia[:, :]))
            k.link(v.tensor_scalar(t.key[:, :], t.dst[:, :], 32.0, None, ALU.mult))
            k.link(v.scalar_tensor_tensor(out=t.key[:, :], in0=fa[:, :], scalar=16.0, in1=t.key[:, :], op0=ALU.mult, op1=ALU.add))
            k.link(v.scalar_tensor_tensor(out=t.key[:, :], in0=fb[:, :], scalar=-31.0, in1=t.key[:, :], op0=ALU.mult, op1=ALU.add))
            dve.wait_ge(comp_in, 64)
            k.link(v.tensor_copy(t.comp[:, 0, :, :], comp[:, :, :]))
            k.link(v.tensor_tensor(rest[:, :, :], comp[:, :, :], t.comp[:, 0, :, :], ALU.subtract))
            k.link(v.tensor_copy(t.comp[:, 1, :, :], rest[:, :, :]))
            k.link(v.tensor_tensor(rest[:, :, :], rest[:, :, :], t.comp[:, 1, :, :], ALU.subtract))
            k.link(v.tensor_copy(t.comp[:, 2, :, :], rest[:, :, :]))
            dve.wait_ge(bad_done, 1)
            k.link(v.tensor_scalar(t.slow[:, :], ps_bad[0:1, 0:1], 0.0, None, ALU.is_gt))


class Coefficients:

    def __init__(self, nc, io, t, ctx, name):
        self.nc, self.io, self.t = nc, io, t
        sem = lambda n: ctx.enter_context(nc.semaphore(f"{name}_{n}"))
        self.etype = ctx.enter_context(nc.sbuf_tensor(f"{name}_types", [RH, 2, ET * P], I32))
        self.onehot = ctx.enter_context(nc.sbuf_tensor(f"{name}_onehot", [RH, 2, 2, ET * P], BF16))
        self.ps = ctx.enter_context(nc.psum_tensor(f"{name}_ps", [P, 512], F32))
        self.etype_in = [sem("types_in0"), sem("types_in1")]
        self.onehot_ready, self.product_done, self.coef_ready = sem("onehot_ready"), sem("product_done"), sem("coef_ready")

    def load(self, eng, m, s):
        after(eng, self.onehot_ready, m - 1)
        count = ET * P if not isinstance(m, int) else min(ET * P, E - m * ET * P)
        rows = self.io["edge_type_200"].rearrange("(a n) -> a n", a=1)
        eng.dma_start(self.etype[:, s, 0:count], rows[:, bass.ds(m * ET * P, count)].to_broadcast([RH, count]))\
           .then_inc(self.etype_in[s], 16)

    def make_onehot(self, eng, m, half_m, s):
        after(eng, self.product_done, m - 1)
        eng.wait_ge(self.etype_in[s], (half_m + 1) * 16)
        for h in range(2):
            ins = self.nc.vector.tensor_scalar(self.onehot[:, s, h, :], self.etype[:, s, :], self.t.type_id[0:RH, h:h + 1],
                                               None, ALU.is_equal)
        ins.then_inc(self.onehot_ready, 1)

    def multiply(self, eng, m, s):
        after(eng, self.coef_ready, m)
        eng.wait_ge(self.onehot_ready, m + 1)
        for e in range(ET):
            for h in range(2):
                for part in range(3):
                    ins = self.nc.tensor.matmul(self.ps[:, e * 2 * NB:(e + 1) * 2 * NB], self.onehot[:, s, h, e * P:(e + 1) * P],
                                                self.t.comp[:, part, h, :], start=(h == 0 and part == 0),
                                                stop=(h == 1 and part == 2))
        ins.then_inc(self.product_done, 1)

    def scale(self, eng, m):
        eng.wait_ge(self.product_done, m + 1)
        shape = [P, 2, ET, NB]
        self.nc.vector.tensor_tensor(self.t.coef[:, :, bass.ds(m * ET, ET), :],
                                     self.ps[:, 0:ET * 2 * NB].rearrange("p (e l b) -> p l e b", l=2, b=NB),
                                     self.t.norm[:, bass.ds(m * ET, ET)].unsqueeze(1).unsqueeze(3).to_broadcast(shape),
                                     ALU.mult).then_inc(self.coef_ready, 1)


class Finish:

    def __init__(self, nc, t, ctx, name, layer):
        self.nc, self.t, self.layer = nc, t, layer
        sb = lambda n, s, d: ctx.enter_context(nc.sbuf_tensor(f"{name}_{n}", s, d))
        sem = lambda n: ctx.enter_context(nc.semaphore(f"{name}_{n}"))
        self.sem_passed = sem("passed")
        self.ZT = sb("ZT", [P, NB, P], F32)
        self.h_stage, self.hT = sb("h_stage", [P, P], F32), sb("hT", [P, P], F32)
        self.ps_h = ctx.enter_context(nc.psum_tensor(f"{name}_ps_h", [P, 512], F32))
        self.ps_o = ctx.enter_context(nc.psum_tensor(f"{name}_ps_o", [P, 512], F32))
        self.staged, self.turned, self.hT_ready = sem("staged"), sem("turned"), sem("hT_ready")
        self.out_done, self.h_new, self.rows_out = sem("out_done"), sem("h_new"), sem("rows_out")
        if layer == 1:
            self.xs, self.hn, self.r = sb("xs", [P, P], F32), sb("hn", [P, P], F32), sb("r", [P, P], F32)
            self.hp, self.parts = sb("hp", [P, P], F32), sb("parts", [P, 3, P], BF16)
            self.stats, self.mv, self.sd = sb("stats", [P, 6], F32), sb("mv", [P, 2], F32), sb("sd", [P, 1], F32)
            self.xs_ready, self.xs_kept, self.var_ready, self.sd_ready = sem("xs_ready"), sem("xs_kept"), sem("var_ready"), sem("sd_ready")
            self.hn_ready, self.hn_turned, self.hnT_ready = sem("hn_ready"), sem("hn_turned"), sem("hnT_ready")
            self.w1_done, self.parts_ready, self.parts_kept = sem("w1_done"), sem("parts_ready"), sem("parts_kept")
            self.chain = sem("chain")

    def hold(self, act, sem, value):
        if isinstance(value, int) and value <= 0:
            return
        act.wait_ge(sem, value)
        act.sem_inc(self.sem_passed, 1)

    def act_stage(self, act, g):
        self.hold(act, self.turned, g)
        self.nc.scalar.activation(self.h_stage[:, :], one(self.t.H, g), ACT.Copy).then_inc(self.staged, 1)
        self.hold(act, self.out_done if self.layer == 0 else self.w1_done, g)
        self.hold(act, self.turned, g + 1)
        self.nc.scalar.activation(self.hT[:, :], self.ps_h[:, 0:P], ACT.Copy).then_inc(self.hT_ready, 1)

    def pe_turn(self, pe, g):
        after(pe, self.hT_ready, g)
        if self.layer == 1:
            after(pe, self.hnT_ready, g)
        pe.wait_ge(self.staged, g + 1)
        self.nc.tensor.transpose(self.ps_h[:, 0:P], self.h_stage[:, :], self.t.ident[:, :]).then_inc(self.turned, 1)

    def pe_out(self, pe, g):
        t, m = self.t, self.nc.tensor
        after(pe, self.h_new if self.layer == 0 else self.parts_ready, g)
        pe.wait_ge(self.hT_ready, g + 1)
        for b in range(NB):
            m.matmul(self.ps_o[:, 0:P], self.ZT[:, b, :], t.V[self.layer][:, b, :], start=(b == 0), stop=False)
        m.matmul(self.ps_o[:, 0:P], self.hT[:, :], t.W[self.layer][:, :], start=False, stop=False)
        m.matmul(self.ps_o[:, 0:P], t.ones[0:1, :], t.bias_row[self.layer][:, :], start=False, stop=True)\
         .then_inc(self.out_done, 1)
        if self.layer == 1:
            pe.wait_ge(self.hn_ready, g + 1)
            m.transpose(self.ps_h[:, P:2 * P], self.hn[:, :], t.ident[:, :]).then_inc(self.hn_turned, 1)
            pe.wait_ge(self.hnT_ready, g + 1)
            m.matmul(self.ps_o[:, P:2 * P], self.hT[:, :], t.W[2][:, :], start=True, stop=True).then_inc(self.w1_done, 1)

    def act_out(self, act, g, rows_dram):
        t, s = self.t, self.nc.scalar
        if self.layer == 0:
            self.hold(act, self.out_done, g + 1)
            s.activation(one(t.H, g), self.ps_o[:, 0:P], ACT.Relu).then_inc(self.h_new, 1)
            self.hold(act, self.h_new, g + 1)
            act.dma_start(rows_dram[bass.ds(g * P, P), :], one(t.H, g)).then_inc(self.rows_out, 16)
            return
        self.hold(act, self.xs_ready, g + 1)
        s.activation(one(t.X, g), self.xs[:, :], ACT.Copy).then_inc(self.xs_kept, 1)
        self.hold(act, self.var_ready, g + 1)
        s.activation(self.sd[:, :], self.mv[:, 1:2], ACT.Sqrt).then_inc(self.sd_ready, 1)
        self.hold(act, self.hn_turned, g + 1)
        s.activation(self.hT[:, :], self.ps_h[:, P:2 * P], ACT.Copy).then_inc(self.hnT_ready, 1)
        self.hold(act, self.parts_ready, g + 1)
        s.activation(one(t.HP[0], g), self.hp[:, :], ACT.Copy).then_inc(self.parts_kept, 1)
        out = t.S[0][:, bass.ds(g, 1), :, :].rearrange("p a b c -> p (a b) c")
        s.activation(out, self.parts[:, :, :], ACT.Copy).then_inc(self.parts_kept, 1)
        if rows_dram is not None:
            self.hold(act, self.parts_kept, 2 * (g + 1))
            act.dma_start(rows_dram[bass.ds(g * P, P), :], one(t.HP[0], g)).then_inc(self.rows_out, 16)

    def dve_out(self, dve, g):
        t, v = self.t, self.nc.vector
        k = Chain(dve, self.chain, 8 * g)
        after(dve, self.xs_kept, g)
        dve.wait_ge(self.out_done, g + 1)
        v.tensor_tensor(self.xs[:, :], self.ps_o[:, 0:P], one(t.X, g), ALU.add).then_inc(self.xs_ready, 1)
        dve.wait_ge(self.xs_ready, g + 1)
        k.link(v.bn_stats(self.stats[:, :], self.xs[:, :]))
        dve.sem_inc(self.sem_passed, 1)
        k.link(v.bn_aggr(self.mv[:, :], self.stats[:, :]))
        v.tensor_scalar(self.mv[:, 1:2], self.mv[:, 1:2], EPS, None, ALU.add).then_inc(self.var_ready, 1)
        dve.wait_ge(self.sd_ready, g + 1)
        k.link(v.reciprocal(self.sd[:, :], self.sd[:, :]))
        k.link(v.tensor_scalar(self.r[:, :], self.xs[:, :], self.mv[:, 0:1], self.sd[:, :], ALU.subtract, ALU.mult))
        v.tensor_scalar(self.hn[:, :], self.r[:, :], 0.0, None, ALU.max).then_inc(self.hn_ready, 1)
        after(dve, self.parts_kept, 2 * g)
        dve.wait_ge(self.w1_done, g + 1)
        k.link(v.tensor_scalar(self.hp[:, :], self.ps_o[:, P:2 * P], t.dinv[:, bass.ds(g, 1)], None, ALU.mult))
        split(v, k, self.hp, self.r, self.parts, self.parts_ready)


def split(v, k, whole, r, parts, done):
    k.link(v.tensor_scalar(parts[:, 0, :], whole[:, :], 1.0, None, ALU.mult))
    k.link(v.tensor_tensor(r[:, :], whole[:, :], parts[:, 0, :], ALU.subtract))
    k.link(v.tensor_scalar(parts[:, 1, :], r[:, :], 1.0, None, ALU.mult))
    v.tensor_tensor(parts[:, 2, :], r[:, :], parts[:, 1, :], ALU.subtract).then_inc(done, 1)


def relational_layer(nc, io, t, layer, rows_in, rows_out):
    name = f"rel{layer}"
    build = layer == 0
    with ExitStack() as ctx:
        sb = lambda n, s, d: ctx.enter_context(nc.sbuf_tensor(f"{name}_{n}", s, d))
        sem = lambda n: ctx.enter_context(nc.semaphore(f"{name}_{n}"))
        ps = lambda n: ctx.enter_context(nc.psum_tensor(f"{name}_{n}", [P, 512], F32))
        idx = [sb(f"idx{i}", [P, CHUNK], I32) for i in range(2)]
        match = [sb(f"match{i}", [P, SPAN, WIN], F32) for i in range(2)]
        C = [sb(f"C{i}", [P, SPAN, NB, WIN], F32) for i in range(2)]
        Z = [sb(f"Z{i}", [P, P], F32) for i in range(2)]
        fin = Finish(nc, t, ctx, name, layer)
        ps_z = [ps("ps_z0"), ps("ps_z1")]
        ps_t = ps("ps_t")
        idx_ready = sem("idx_ready")
        ring_even, ring_odd = sem("ring_even"), sem("ring_odd")
        z_done, t_done = sem("z_done"), sem("t_done")
        match_ready, c_ready, z_ready, zt_ready = sem("match_ready"), sem("c_ready"), sem("z_ready"), sem("zt_ready")
        passed = sem("waits_passed")
        ring = t.ring
        if build:
            co = Coefficients(nc, io, t, ctx, name)
            M = [sb(f"M{i}", [P, SPAN, AW], BF16) for i in range(2)]
            lo = [sb(f"lo{i}", [P, SPAN, P], BF16) for i in range(2)]
            A = sb("A", [P, 2, SRC_BLOCKS, P], F16)
            ps_a = [ps("ps_a0"), ps("ps_a1")]
            m_ready, a_done, a_kept, deg_done = sem("m_ready"), sem("a_done"), sem("a_kept"), sem("deg_done")
            deg_kept = sem("deg_kept")
            a_out = sem("a_out")
        else:
            deg_plus = sb("deg_plus", [P, GROUPS], F32)
            root_ready = sem("root_ready")
        block = ctx.enter_context(nc.Block())

        def hold(eng, s, value):
            if isinstance(value, int) and value <= 0:
                return
            eng.wait_ge(s, value)
            eng.sem_inc(passed, 1)

        def groups(eng, body):
            body(0)
            with eng.Fori(1, GROUPS - 2) as g:
                body(g)
            body(GROUPS - 2)
            body(GROUPS - 1)

        def slab(g):
            return A[:, bass.ds(g % 2, 1), :, :].rearrange("p a b n -> p (a b n)")

        def chunks_next(g):
            if not build or (isinstance(g, int) and g == GROUPS - 1):
                return 0
            if isinstance(g, int) and g == GROUPS - 2:
                return ET_CHUNKS - 4 * (GROUPS - 1)
            return 4

        @block.gpsimd
        def _(pool):
            g_ = nc.gpsimd

            def chunk(c, half_c, s):
                if not isinstance(c, int) or c >= 4:
                    hold(pool, z_done, (c - 2) * 4)
                landed = (ring_even, ring_odd)[s % 2]
                hold(pool, landed, CHUNK * 16 * half_c)
                g_.tensor_copy(idx[s % 2][:, :], t.idx[:, bass.ds(c * CHUNK, CHUNK)]).then_inc(idx_ready, 1)
                hold(pool, idx_ready, c + 1)
                for i in range(CHUNK):
                    g_.indirect_dma_start(ring[:, s * CHUNK + i, :], None, rows_in,
                                          bass.IndirectOffsetOnAxis(ap=idx[s % 2][:, i:i + 1], axis=0)).then_inc(landed, 16)

            for s in range(4):
                chunk(s, s // 2, s)
            with pool.Fori(1, CHUNKS // 4) as m:
                for s in range(4):
                    chunk(m * 4 + s, m * 2 + s // 2, s)
            chunk(CHUNKS - 1, (CHUNKS - 1) // 2, 0)

        if build:
            @block.sync
            def _(sp):
                for m in range(4):
                    co.load(sp, m, m % 2)

                def group(g):
                    for i in range(chunks_next(g)):
                        co.load(sp, (g + 1) * 4 + i, i % 2)
                groups(sp, group)

        @block.vector
        def _(dve):
            v = nc.vector
            if build:
                for m in range(4):
                    co.make_onehot(dve, m, m // 2, m % 2)
                    co.scale(dve, m)
            else:
                v.tensor_scalar(deg_plus[:, :], t.deg[:, :], 1.0, None, ALU.add).then_inc(root_ready, 1)
                dve.wait_ge(root_ready, 2)
                v.reciprocal(t.dinv[:, :], deg_plus[:, :]).then_inc(root_ready, 1)
                dve.wait_ge(root_ready, 3)
            regs = [dve.alloc_register(f"{name}_first{i}") for i in range(WPG)]

            def window(g, i, start):
                j, s = g * WPG + i, i % 2
                tiles = bass.ds(start, SPAN)
                shape = [P, SPAN, WIN]
                v.scalar_tensor_tensor(out=match[s][:, :, :], in0=t.dst[:, tiles].unsqueeze(2).to_broadcast(shape),
                                       scalar=t.neg_win[:, bass.ds(j, 1)],
                                       in1=t.iota16[:, :].unsqueeze(1).to_broadcast(shape),
                                       op0=ALU.add, op1=ALU.is_equal).then_inc(match_ready, 1)
                if build:
                    after(dve, a_done, j - 1)
                    for k in range(SPAN):
                        tile = bass.ds(start + k, 1)
                        v.tensor_scalar(M[s][:, k, :], t.iota400[:, :], t.win512[:, bass.ds(j, 1)], t.key[:, tile],
                                        ALU.add, ALU.is_equal)
                        ins = v.tensor_scalar(lo[s][:, k, :], t.iota128[:, :], t.src_lo[:, tile], None, ALU.is_equal)
                    ins.then_inc(m_ready, 1)
                after(dve, z_done, j - 1)
                dve.wait_ge(match_ready, j + 1)
                shape = [P, SPAN, NB, WIN]
                v.tensor_tensor(C[s][:, :, :, :], match[s][:, :, :].unsqueeze(2).to_broadcast(shape),
                                t.coef[:, layer, tiles, :].unsqueeze(3).to_broadcast(shape), ALU.mult).then_inc(c_ready, 1)

            def group(g):
                dve.load(regs, t.first[0:1, bass.ds(g * WPG, WPG)])
                starts = [dve.snap(r, min_val=0, max_val=TILES - SPAN) for r in regs]
                if build:
                    have = min((g + 1) * 4, ET_CHUNKS) if isinstance(g, int) else (g + 1) * 4
                    dve.wait_ge(co.coef_ready, have)
                for i in range(WPG):
                    extra = i // 2 < chunks_next(g)
                    m = (g + 1) * 4 + i // 2
                    if extra and i % 2 == 0:
                        co.make_onehot(dve, m, (g + 1) * 2 + i // 4, i // 2 % 2)
                    window(g, i, starts[i])
                    if build and i == 0 and not (isinstance(g, int) and g == 0):
                        keep_deg(g - 1)
                    if extra and i % 2 == 1:
                        co.scale(dve, m)
                if not build:
                    fin.dve_out(dve, g)

            def keep_deg(g):
                dve.wait_ge(deg_done, g + 1)
                v.tensor_scalar(t.deg[:, bass.ds(g, 1)], fin.ps_h[:, 2 * P:2 * P + 1], 1.0, None, ALU.mult).then_inc(deg_kept, 1)

            groups(dve, group)
            if build:
                keep_deg(GROUPS - 1)

        @block.tensor
        def _(pe):
            m_ = nc.tensor
            if build:
                for m in range(4):
                    co.multiply(pe, m, m % 2)
            regs = [pe.alloc_register(f"{name}_pos{i}") for i in range(SPAN)]

            def turn(g, i):
                j = g * WPG + i
                pe.wait_ge(z_ready, j + 1)
                after(pe, zt_ready, j)
                m_.transpose(ps_t[:, 0:P], Z[i % 2][:, :], t.ident[:, :]).then_inc(t_done, 1)

            def group(g):
                if build:
                    after(pe, deg_kept, g)
                fin.pe_turn(pe, g)
                for i in range(WPG):
                    j, s = g * WPG + i, i % 2
                    pe.load(regs, t.pos[0:1, bass.ds(j, 1), 0:SPAN].rearrange("p a b -> p (a b)"))
                    at = [pe.snap(r, min_val=0, max_val=RING - 1) for r in regs]
                    if i == 0:
                        pe.wait_ge(ring_even, (g + 1) * (16 * CHUNK))
                        pe.wait_ge(ring_odd, (g + 1) * (16 * CHUNK) if not (isinstance(g, int) and g == GROUPS - 1) else g * (16 * CHUNK))
                    if i == WPG // 2 and not (isinstance(g, int) and g == GROUPS - 1):
                        pe.wait_ge(ring_even, (g + 2) * (16 * CHUNK))
                    after(pe, z_ready, j - 1)
                    pe.wait_ge(c_ready, j + 1)
                    for k in range(SPAN):
                        ins = m_.matmul(ps_z[s][:, 0:P], C[s][:, k, :, :].rearrange("p b w -> p (b w)"), one(ring, at[k]),
                                        start=(k == 0), stop=(k == SPAN - 1))
                    ins.then_inc(z_done, 1)
                    if build:
                        after(pe, a_kept, j - 1)
                        pe.wait_ge(m_ready, j + 1)
                        for k in range(SPAN):
                            ins = m_.matmul(ps_a[s][:, 0:AW], lo[s][:, k, :], M[s][:, k, :], start=(k == 0), stop=(k == SPAN - 1))
                        ins.then_inc(a_done, 1)
                        if i % 2 == 0 and i // 2 < chunks_next(g):
                            co.multiply(pe, (g + 1) * 4 + i // 2, i // 2 % 2)
                    if i:
                        turn(g, i - 1)
                turn(g, WPG - 1)
                pe.wait_ge(zt_ready, (g + 1) * WPG)
                fin.pe_out(pe, g)
                if build:
                    pe.wait_ge(a_kept, (g + 1) * WPG)
                    blocks = slab(g)
                    for b in range(SRC_BLOCKS):
                        ins = m_.matmul(fin.ps_h[:, 2 * P:2 * P + 1], blocks[:, b * P:(b + 1) * P], t.ones16[:, 0:1],
                                        start=(b == 0), stop=(b == SRC_BLOCKS - 1))
                    ins.then_inc(deg_done, 1)
            groups(pe, group)

        @block.scalar
        def _(act):
            s_ = nc.scalar
            if not build:
                act.wait_ge(root_ready, 1)
                s_.activation(deg_plus[:, :], deg_plus[:, :], ACT.Sqrt).then_inc(root_ready, 1)

            def keep_zt(g, i):
                j = g * WPG + i
                hold(act, t_done, j + 1)
                if i == 0:
                    hold(act, fin.out_done, g)
                s_.activation(fin.ZT[:, :, i * WIN:(i + 1) * WIN],
                              ps_t[:, 0:P].rearrange("p (b w) -> p b w", b=NB), ACT.Copy).then_inc(zt_ready, 1)

            def group(g):
                fin.act_stage(act, g)
                for i in range(WPG):
                    j, s = g * WPG + i, i % 2
                    hold(act, z_done, j + 1)
                    hold(act, t_done, j - 1)
                    s_.activation(Z[s][:, :], ps_z[s][:, 0:P], ACT.Copy).then_inc(z_ready, 1)
                    if build:
                        if i == 0:
                            hold(act, deg_done, g)
                        hold(act, a_done, j + 1)
                        s_.activation(slab(g).rearrange("p (b n) -> p b n", n=P)[:, :, i * WIN:(i + 1) * WIN],
                                      ps_a[s][:, 0:AW].rearrange("p (b w) -> p b w", w=WIN), ACT.Copy).then_inc(a_kept, 1)
                    if i:
                        keep_zt(g, i - 1)
                keep_zt(g, WPG - 1)
                if build:
                    hold(act, a_out, g * 16)
                    hold(act, a_kept, (g + 1) * WPG)
                    act.dma_start(t.A_dram[bass.ds(g, 1), :, :].rearrange("a p n -> (a p) n"), slab(g)).then_inc(a_out, 16)
                fin.act_out(act, g, rows_out)
            groups(act, group)
            if build:
                act.wait_ge(a_out, 16 * GROUPS)
            if rows_out is not None:
                act.wait_ge(fin.rows_out, 16 * GROUPS)


SLOTS = 5


def dense_layer(nc, t, layer, out):
    name = f"gcn{layer}"
    last = layer == 1
    with ExitStack() as ctx:
        sb = lambda n, s, d: ctx.enter_context(nc.sbuf_tensor(f"{name}_{n}", s, d))
        sem = lambda n: ctx.enter_context(nc.semaphore(f"{name}_{n}"))
        ps = lambda n: ctx.enter_context(nc.psum_tensor(f"{name}_{n}", [P, 512], F32))
        A = [sb(f"A{s}", [P, SRC_BLOCKS, P], F16) for s in range(SLOTS)]
        z = [sb(f"z{s}", [P, P], F32) for s in range(SLOTS)]
        ps_g = [ps(f"ps_g{s}") for s in range(SLOTS)]
        tail = DenseTail(nc, t, ctx, name, last)
        a_in = [sem(f"a_in{s}") for s in range(SLOTS)]
        agg_done = sem("agg_done")
        chain = sem("chain")
        z_out = [sem(f"z_out{s}") for s in range(SLOTS)]
        block = ctx.enter_context(nc.Block())

        def slots(eng, body):
            rounds = GROUPS // SLOTS
            for s in range(SLOTS):
                body(s, s, 0)
            with eng.Fori(1, rounds - 1) as m:
                for s in range(SLOTS):
                    body(m * SLOTS + s, s, m)
            for s in range(SLOTS):
                body((rounds - 1) * SLOTS + s, s, rounds - 1)

        @block.sync
        def _(sp):
            def load(g, s, m):
                after(sp, agg_done, g - (SLOTS - 1))
                sp.dma_start(A[s][:, :, :].rearrange("p b n -> p (b n)"),
                             t.A_dram[bass.ds(g, 1), :, :].rearrange("a p n -> (a p) n")).then_inc(a_in[s], 16)
            slots(sp, load)

        @block.tensor
        def _(pe):
            def group(g, s, m):
                pe.wait_ge(a_in[s], (m + 1) * 16)
                after(pe, tail.z_ready, g - (SLOTS - 1))
                for b in range(SRC_BLOCKS):
                    ins = nc.tensor.matmul(ps_g[s][:, 0:3 * P], A[s][:, b, :], t.S[layer][:, b, :, :].rearrange("p c n -> p (c n)"),
                                           start=(b == 0), stop=(b == SRC_BLOCKS - 1))
                ins.then_inc(agg_done, 1)
                if not last:
                    tail.pe_turn(pe, g - 1, z[(s - 1) % SLOTS])
                    tail.pe_multiply(pe, g - 2)
            slots(pe, group)
            if not last:
                tail.pe_turn(pe, GROUPS - 1, z[(GROUPS - 1) % SLOTS])
                tail.pe_multiply(pe, GROUPS - 2)
                tail.pe_multiply(pe, GROUPS - 1)

        @block.scalar
        def _(act):
            def group(g, s, m):
                if last:
                    tail.store(act, g, z[s], out, z_out[s])
                else:
                    tail.act(act, g)
            slots(act, group)
            if last:
                for s in range(SLOTS):
                    act.wait_ge(z_out[s], (GROUPS // SLOTS) * 16)

        @block.vector
        def _(dve):
            v = nc.vector

            def group(g, s, m):
                dve.wait_ge(agg_done, g + 1)
                if last:
                    after(dve, z_out[s], m * 16)
                k = Chain(dve, chain, 3 * g if last else 2 * g)
                k.link(v.tensor_reduce(z[s][:, :], ps_g[s][:, 0:3 * P].rearrange("p (c n) -> p n c", c=3), AX.X, ALU.add))
                tail.combine(dve, v, k, g, z[s])
                if not last:
                    tail.dve_split(dve, g - 2)
            slots(dve, group)
            if not last:
                tail.dve_split(dve, GROUPS - 2)
                tail.dve_split(dve, GROUPS - 1)



class DenseTail:

    def __init__(self, nc, t, ctx, name, last):
        self.nc, self.t, self.last = nc, t, last
        sem = lambda n: ctx.enter_context(nc.semaphore(f"{name}_{n}"))
        self.z_ready, self.passed = sem("z_ready"), sem("waits_passed")
        self.layer = 1 if last else 0
        if not last:
            sb = lambda n, s, d: ctx.enter_context(nc.sbuf_tensor(f"{name}_{n}", s, d))
            ps = lambda n: ctx.enter_context(nc.psum_tensor(f"{name}_{n}", [P, 512], F32))
            self.zT, self.hp, self.r = sb("zT", [P, P], F32), sb("hp", [P, P], F32), sb("r", [P, P], F32)
            self.parts = sb("parts", [P, 3, P], BF16)
            self.ps_t, self.ps_o = ps("ps_t"), ps("ps_o")
            self.turned, self.zT_ready, self.w_done = sem("turned"), sem("zT_ready"), sem("w_done")
            self.parts_ready, self.parts_kept, self.chain = sem("parts_ready"), sem("parts_kept"), sem("split_chain")

    def combine(self, dve, v, k, g, z):
        t = self.t
        k.link(v.tensor_tensor(z[:, :], z[:, :], one(t.HP[self.layer], g), ALU.add))
        ins = v.scalar_tensor_tensor(out=z[:, :], in0=z[:, :], scalar=t.dinv[:, bass.ds(g, 1)],
                                     in1=t.bias_all[self.layer][:, :], op0=ALU.mult, op1=ALU.add)
        if self.last:
            k.link(ins)
            v.tensor_tensor(z[:, :], z[:, :], one(t.X, g), ALU.add).then_inc(self.z_ready, 1)
        else:
            ins.then_inc(self.z_ready, 1)

    def pe_turn(self, pe, g, z):
        if isinstance(g, int) and g < 0:
            return
        after(pe, self.zT_ready, g)
        pe.wait_ge(self.z_ready, g + 1)
        self.nc.tensor.transpose(self.ps_t[:, 0:P], z[:, :], self.t.ident[:, :]).then_inc(self.turned, 1)

    def hold(self, act, sem, value):
        if isinstance(value, int) and value <= 0:
            return
        act.wait_ge(sem, value)
        act.sem_inc(self.passed, 1)

    def store(self, act, g, z, out, done):
        rows = LAST_ROWS if isinstance(g, int) and g == GROUPS - 1 else P
        self.hold(act, self.z_ready, g + 1)
        act.dma_start(out[bass.ds(g * P, rows), :], z[0:rows, :]).then_inc(done, 16)

    def act(self, act, g):
        hold = lambda sem, value: self.hold(act, sem, value)
        t, s = self.t, self.nc.scalar
        hold(self.w_done, g)
        hold(self.turned, g + 1)
        s.activation(self.zT[:, :], self.ps_t[:, 0:P], ACT.Relu).then_inc(self.zT_ready, 1)
        hold(self.parts_ready, g + 1)
        s.activation(one(t.HP[1], g), self.hp[:, :], ACT.Copy).then_inc(self.parts_kept, 1)
        out = t.S[1][:, bass.ds(g, 1), :, :].rearrange("p a b c -> p (a b) c")
        s.activation(out, self.parts[:, :, :], ACT.Copy).then_inc(self.parts_kept, 1)

    def pe_multiply(self, pe, g):
        if isinstance(g, int) and g < 0:
            return
        pe.wait_ge(self.zT_ready, g + 1)
        after(pe, self.parts_ready, g)
        self.nc.tensor.matmul(self.ps_o[:, 0:P], self.zT[:, :], self.t.W[3][:, :], start=True, stop=True).then_inc(self.w_done, 1)

    def dve_split(self, dve, g):
        if isinstance(g, int) and g < 0:
            return
        v = self.nc.vector
        after(dve, self.parts_kept, 2 * g)
        dve.wait_ge(self.w_done, g + 1)
        k = Chain(dve, self.chain, 4 * g)
        k.link(v.tensor_scalar(self.hp[:, :], self.ps_o[:, 0:P], self.t.dinv[:, bass.ds(g, 1)], None, ALU.mult))
        split(v, k, self.hp, self.r, self.parts, self.parts_ready)


def any_order_coefficients(nc, io, t):
    with ExitStack() as ctx:
        co = Coefficients(nc, io, t, ctx, "any_coef")
        block = ctx.enter_context(nc.Block())

        def chunks(eng, step):
            for m in range(2):
                step(m, 0, m)
            with eng.Fori(1, ET_CHUNKS // 2 - 1) as pair:
                for s in range(2):
                    step(pair * 2 + s, pair, s)
            for m in range(ET_CHUNKS - 2, ET_CHUNKS):
                step(m, m // 2, m % 2)

        @block.sync
        def _(sp):
            chunks(sp, lambda m, half_m, s: co.load(sp, m, s))

        @block.tensor
        def _(pe):
            chunks(pe, lambda m, half_m, s: co.multiply(pe, m, s))

        @block.vector
        def _(dve):
            def step(m, half_m, s):
                co.make_onehot(dve, m, half_m, s)
                co.scale(dve, m)
            chunks(dve, step)


class AnyOrder:

    def __init__(self, nc, t, ctx, name, rows_in):
        self.nc, self.t, self.rows_in, self.name = nc, t, rows_in, name
        sb = lambda n, s, d: ctx.enter_context(nc.sbuf_tensor(f"{name}_{n}", s, d))
        sem = lambda n: ctx.enter_context(nc.semaphore(f"{name}_{n}"))
        self.idx, self.rows = sb("idx", [P, 1], I32), sb("rows", [P, D], F32)
        self.match = sb("match", [P, P], F32)
        self.idx_ready, self.landed, self.done, self.passed = sem("idx_ready"), sem("landed"), sem("done"), sem("pool_waits_passed")
        self.match_ready, self.factor_ready, self.sum_ready = sem("match_ready"), sem("factor_ready"), sem("sum_ready")
        self.cleared, self.dve_passed = sem("cleared"), sem("dve_waits_passed")

    def gather(self, pool):
        with pool.Fori(0, GROUPS) as g:
            with pool.Fori(0, TILES) as tile:
                n = g * TILES + tile
                pool.wait_ge(self.done, n + 1)
                pool.sem_inc(self.passed, 1)
                self.nc.gpsimd.tensor_copy(self.idx[:, :], self.t.idx[:, bass.ds(tile, 1)]).then_inc(self.idx_ready, 1)
                pool.wait_ge(self.idx_ready, n + 1)
                pool.sem_inc(self.passed, 1)
                self.nc.gpsimd.indirect_dma_start(self.rows[:, :], None, self.rows_in,
                                                  bass.IndirectOffsetOnAxis(ap=self.idx[:, 0:1], axis=0)).then_inc(self.landed, 16)

    def one_hot(self, dve, g, tile, n):
        dve.wait_ge(self.done, n + 1)
        self.nc.vector.tensor_scalar(self.match[:, :], self.t.iota128[:, :], self.t.group_lo[:, bass.ds(g, 1)],
                                     self.t.dst[:, bass.ds(tile, 1)], ALU.add, ALU.is_equal).then_inc(self.match_ready, 1)
        dve.wait_ge(self.match_ready, n + 1)


def any_order_relational(nc, t, layer, rows_in, rows_out):
    name = f"any_rel{layer}"
    with ExitStack() as ctx:
        ps = lambda n: ctx.enter_context(nc.psum_tensor(f"{name}_{n}", [P, 512], F32))
        C = ctx.enter_context(nc.sbuf_tensor(f"{name}_C", [P, NB, P], F32))
        fin = Finish(nc, t, ctx, name, layer)
        way = AnyOrder(nc, t, ctx, name, rows_in)
        ps_z = [ps("ps_z0"), ps("ps_z1")]
        ps_d = ps("ps_d")
        if layer == 1:
            root_ready = ctx.enter_context(nc.semaphore(f"{name}_root_ready"))
        block = ctx.enter_context(nc.Block())
        HB = NB // 2

        @block.gpsimd
        def _(pool):
            way.gather(pool)

        @block.tensor
        def _(pe):
            m_ = nc.tensor
            pe.sem_inc(way.done, 1)
            with pe.Fori(0, GROUPS) as g:
                pe.wait_ge(fin.staged, g + 1)
                m_.transpose(fin.ps_h[:, 0:P], fin.h_stage[:, :], t.ident[:, :]).then_inc(fin.turned, 1)
                with pe.Fori(0, TILES) as tile:
                    n = g * TILES + tile
                    pe.wait_ge(way.landed, (n + 1) * 16)
                    pe.wait_ge(way.factor_ready, n + 1)
                    if layer == 0:
                        m_.matmul(ps_d[:, 0:1], way.match[:, :], t.ones[:, 0:1], start=True, stop=True)
                    for h in range(2):
                        ins = m_.matmul(ps_z[h][:, :], way.rows[:, :], C[:, h * HB:(h + 1) * HB, :].rearrange("p b n -> p (b n)"),
                                        start=True, stop=True)
                    ins.then_inc(way.done, 1)
                pe.wait_ge(way.sum_ready, g + 1)
                fin.pe_out(pe, g)

        @block.scalar
        def _(act):
            if layer == 1:
                act.wait_ge(root_ready, 1)
                nc.scalar.activation(t.dinv[:, :], t.dinv[:, :], ACT.Sqrt).then_inc(root_ready, 1)
            with act.Fori(0, GROUPS) as g:
                nc.scalar.activation(fin.h_stage[:, :], one(t.H, g), ACT.Copy).then_inc(fin.staged, 1)
                fin.hold(act, fin.turned, g + 1)
                nc.scalar.activation(fin.hT[:, :], fin.ps_h[:, 0:P], ACT.Copy).then_inc(fin.hT_ready, 1)
                fin.act_out(act, g, rows_out)
            act.wait_ge(fin.rows_out, 16 * GROUPS)

        @block.vector
        def _(dve):
            v = nc.vector
            if layer == 0:
                v.memset(t.deg[:, :], 0.0).then_inc(way.cleared, 1)
                dve.wait_ge(way.cleared, 1)
            else:
                v.tensor_scalar(t.dinv[:, :], t.deg[:, :], 1.0, None, ALU.add).then_inc(root_ready, 1)
                dve.wait_ge(root_ready, 2)
                v.reciprocal(t.dinv[:, :], t.dinv[:, :]).then_inc(root_ready, 1)
                dve.wait_ge(root_ready, 3)
            with dve.Fori(0, GROUPS) as g:
                v.memset(fin.ZT[:, :, :], 0.0).then_inc(way.cleared, 1)
                dve.wait_ge(way.cleared, g + (2 if layer == 0 else 1))
                dve.sem_inc(way.dve_passed, 1)
                with dve.Fori(0, TILES) as tile:
                    n = g * TILES + tile
                    way.one_hot(dve, g, tile, n)
                    shape = [P, NB, P]
                    v.tensor_tensor(C[:, :, :], way.match[:, :].unsqueeze(1).to_broadcast(shape),
                                    t.coef[:, layer, bass.ds(tile, 1), :].rearrange("p a b -> p (a b)").unsqueeze(2).to_broadcast(shape),
                                    ALU.mult).then_inc(way.factor_ready, 1)
                    dve.wait_ge(way.done, n + 2)
                    for h in range(2):
                        z = flat(fin.ZT[:, h * HB:(h + 1) * HB, :])
                        v.tensor_tensor(z, z, ps_z[h][:, :], ALU.add)
                    if layer == 0:
                        d = t.deg[:, bass.ds(g, 1)]
                        v.tensor_tensor(d, d, ps_d[:, 0:1], ALU.add)
                v.tensor_scalar(fin.ZT[0:1, 0, 0:1], fin.ZT[0:1, 0, 0:1], 1.0, None, ALU.mult).then_inc(way.sum_ready, 1)
                if layer == 1:
                    fin.dve_out(dve, g)
                else:
                    dve.wait_ge(fin.out_done, g + 1)


def any_order_gcn(nc, t, layer, rows_in, rows_out, out):
    name = f"any_gcn{layer}"
    last = layer == 1
    with ExitStack() as ctx:
        z = ctx.enter_context(nc.sbuf_tensor(f"{name}_z", [P, P], F32))
        ps_g = ctx.enter_context(nc.psum_tensor(f"{name}_ps_g", [P, 512], F32))
        tail = DenseTail(nc, t, ctx, name, last)
        way = AnyOrder(nc, t, ctx, name, rows_in)
        chain, stored = ctx.enter_context(nc.semaphore(f"{name}_chain")), ctx.enter_context(nc.semaphore(f"{name}_stored"))
        block = ctx.enter_context(nc.Block())

        def groups(eng, body):
            with eng.Fori(0, GROUPS - 1) as g:
                body(g)
            body(GROUPS - 1)

        @block.gpsimd
        def _(pool):
            way.gather(pool)

        @block.tensor
        def _(pe):
            pe.sem_inc(way.done, 1)

            def group(g):
                with pe.Fori(0, TILES) as tile:
                    n = tile + g * TILES
                    pe.wait_ge(way.landed, (n + 1) * 16)
                    pe.wait_ge(way.match_ready, n + 1)
                    nc.tensor.matmul(ps_g[:, 0:P], way.match[:, :], way.rows[:, :], start=True, stop=True).then_inc(way.done, 1)
                if not last:
                    pe.wait_ge(tail.z_ready, g + 1)
                    nc.tensor.transpose(tail.ps_t[:, 0:P], z[:, :], t.ident[:, :]).then_inc(tail.turned, 1)
                    pe.wait_ge(tail.zT_ready, g + 1)
                    nc.tensor.matmul(tail.ps_o[:, 0:P], tail.zT[:, :], t.W[3][:, :], start=True, stop=True).then_inc(tail.w_done, 1)
            groups(pe, group)

        @block.scalar
        def _(act):
            def group(g):
                if last:
                    tail.store(act, g, z, out, stored)
                else:
                    tail.hold(act, tail.turned, g + 1)
                    nc.scalar.activation(tail.zT[:, :], tail.ps_t[:, 0:P], ACT.Relu).then_inc(tail.zT_ready, 1)
                    tail.hold(act, tail.parts_ready, g + 1)
                    nc.scalar.activation(one(t.HP[1], g), tail.hp[:, :], ACT.Copy).then_inc(tail.parts_kept, 1)
                    tail.hold(act, tail.parts_kept, g + 1)
                    act.dma_start(rows_out[bass.ds(g * P, P), :], one(t.HP[1], g)).then_inc(stored, 16)
            groups(act, group)
            act.wait_ge(stored, 16 * GROUPS)

        @block.vector
        def _(dve):
            v = nc.vector

            def group(g):
                v.memset(z[:, :], 0.0).then_inc(way.cleared, 1)
                dve.wait_ge(way.cleared, g + 1)
                dve.sem_inc(way.dve_passed, 1)
                with dve.Fori(0, TILES) as tile:
                    n = tile + g * TILES
                    way.one_hot(dve, g, tile, n)
                    dve.wait_ge(way.done, n + 2)
                    v.tensor_tensor(z[:, :], z[:, :], ps_g[:, 0:P], ALU.add).then_inc(way.sum_ready, 1)
                    dve.wait_ge(way.sum_ready, n + 1)
                tail.combine(dve, v, Chain(dve, chain, (2 if last else 1) * g), g, z)
                if last:
                    dve.wait_ge(stored, (g + 1) * 16)
                else:
                    dve.wait_ge(tail.w_done, g + 1)
                    v.tensor_scalar(tail.hp[:, :], tail.ps_o[:, 0:P], t.dinv[:, bass.ds(g, 1)], None, ALU.mult)\
                     .then_inc(tail.parts_ready, 1)
                    dve.wait_ge(tail.parts_kept, g + 1)
            groups(dve, group)


class Tensors:
    pass


def program(nc, io, out, force_slow=False):
    t = Tensors()
    with ExitStack() as ctx:
        sb = lambda n, s, d: ctx.enter_context(nc.sbuf_tensor(n, s, d))
        dram = lambda n, s, d: nc.dram_tensor(n, s, d, kind="Internal").ap()
        t.h1_dram, t.h2_dram = dram("h1_rows", (GROUPS * P, D), F32), dram("h2_rows", (GROUPS * P, D), F32)
        t.A_dram = dram("A_slabs", (GROUPS, P, SRC_BLOCKS * P), F16)
        t.X, t.H = sb("X", [P, GROUPS, D], F32), sb("H", [P, GROUPS, D], F32)
        t.V = [sb(f"V{i}", [P, NB, D], F32) for i in range(2)]
        t.W = [sb(f"W{i}", [P, D], F32) for i in range(4)]
        t.bias_row = [sb(f"bias_row{i}", [1, D], F32) for i in range(2)]
        t.bias_all = [sb(f"bias_all{i}", [P, D], F32) for i in range(2)]
        t.ident, t.ones, t.ones16 = sb("ident", [P, P], F32), sb("ones", [P, P], F32), sb("ones16", [P, 2], F16)
        t.idx = sb("idx_table", [P, TILES], I32)
        t.dst, t.norm = sb("dst_table", [P, TILES], F32), sb("norm_table", [P, TILES], F32)
        t.src_lo, t.key = sb("src_lo_table", [P, TILES], F32), sb("key_table", [P, TILES], F32)
        t.comp = sb("comp_parts", [RH, 3, 2, 2 * NB], BF16)
        t.neg_win, t.win512 = sb("neg_win", [P, WINDOWS], F32), sb("win512", [P, WINDOWS], F32)
        t.group_lo = sb("group_lo", [P, GROUPS], F32)
        t.iota16, t.iota400, t.iota128 = sb("iota16", [P, WIN], F32), sb("iota400", [P, AW], F16), sb("iota128", [P, P], F16)
        t.type_id = sb("type_id", [P, 2], F32)
        t.pos, t.first, t.slow = sb("pos", [1, WINDOWS, 8], I32), sb("first", [1, WINDOWS], I32), sb("slow", [1, 1], I32)
        t.deg, t.dinv = sb("deg", [P, GROUPS], F32), sb("dinv", [P, GROUPS], F32)

        prepare(nc, io, t)
        slow = nc.values_load(t.slow[0:1, 0:1], min_val=0, max_val=1)
        hp_rows = [dram(f"hp_rows{i}", (GROUPS * P, D), F32) for i in range(2)]
        right = lambda c, n, s, d: c.enter_context(nc.sbuf_tensor(n, s, d, side="right"))
        left = lambda c, n, s, d: c.enter_context(nc.sbuf_tensor(n, s, d))
        t.HP, t.S = [None, None], [None, None]
        with nc.If(slow == 0):
            with ExitStack() as parts:
                with ExitStack() as edges:
                    t.coef, t.ring = left(edges, "coef", [P, 2, TILES, NB], F32), left(edges, "ring", [P, RING, D], F32)
                    relational_layer(nc, io, t, 0, t.h1_dram, t.h2_dram)
                    t.HP[0] = right(parts, "hp0", [P, GROUPS, D], F32)
                    t.S[0] = right(parts, "hp0_parts", [P, GROUPS, 3, D], BF16)
                    relational_layer(nc, io, t, 1, t.h2_dram, None)
                t.HP[1] = right(parts, "hp1", [P, GROUPS, D], F32)
                t.S[1] = right(parts, "hp1_parts", [P, GROUPS, 3, D], BF16)
                dense_layer(nc, t, 0, out)
                dense_layer(nc, t, 1, out)
        with nc.Else():
            with ExitStack() as parts:
                t.coef = left(parts, "any_coef", [P, 2, TILES, NB], F32)
                t.HP = [left(parts, f"any_hp{i}", [P, GROUPS, D], F32) for i in range(2)]
                t.S = [left(parts, "any_parts", [P, GROUPS, 3, D], BF16), None]
                any_order_coefficients(nc, io, t)
                any_order_relational(nc, t, 0, t.h1_dram, t.h2_dram)
                any_order_relational(nc, t, 1, t.h2_dram, hp_rows[0])
                any_order_gcn(nc, t, 0, hp_rows[0], hp_rows[1], out)
                any_order_gcn(nc, t, 1, hp_rows[1], None, out)


_INS = ["x", "src", "dst", "edge_type_200", "edge_weight1", "L0_gnn_V1", "L0_gnn_comp1", "L0_gnn_loop1", "L0_gnn_bias1",
        "L0_gnn_V2", "L0_gnn_comp2", "L0_gnn_loop2", "L0_gnn_bias2", "L1_gnn_W1", "L1_gnn_b1", "L1_gnn_W2", "L1_gnn_b2"]


def kernel(**inputs):
    import numpy as _np
    import concourse.bacc as _bacc
    from concourse import mybir as _mybir
    from concourse.bass_utils import run_bass_kernel_spmd as _run

    nc = _bacc.Bacc("TRN2", target_bir_lowering=False, num_devices=1)
    arrays, io = {}, {}
    for name in _INS:
        a = _np.ascontiguousarray(inputs[name])
        arrays[f"in_{name}_dram"] = a
        io[name] = nc.dram_tensor(f"in_{name}_dram", a.shape, _mybir.dt.from_np(a.dtype), kind="ExternalInput").ap()
    out = nc.dram_tensor("out_0_dram", (N, D), _mybir.dt.float32, kind="ExternalOutput").ap()
    program(nc, io, out)
    r = _run(nc, [arrays], core_ids=[0])
    return r.results[0]["out_0_dram"]
```

```python
from contextlib import ExitStack

import concourse.bass as bass
import numpy as np
from concourse import mybir

ALU = mybir.AluOpType
ACT = mybir.ActivationFunctionType
AX = mybir.AxisListType
F32, F16, BF16, I32 = mybir.dt.float32, mybir.dt.float16, mybir.dt.bfloat16, mybir.dt.int32

P = 128
N, D, E, R, NB = 3125, 128, 100000, 200, 8
GROUPS = -(-N // P)
LAST_ROWS = N - (GROUPS - 1) * P
TILES = 784
RAW = 7
WIN = 16
WPG = P // WIN
WINDOWS = GROUPS * WPG
SPAN = 6
CHUNK = 16
RING = 4 * CHUNK
CHUNKS = TILES // CHUNK
SRC_BLOCKS = GROUPS
AW = SRC_BLOCKS * WIN
ET = 8
ET_CHUNKS = TILES // ET
RH = R // 2
PAD_DST = 4000
EPS = 1e-5


def after(eng, sem, value):
    if isinstance(value, int) and value <= 0:
        return
    eng.wait_ge(sem, value)


class Chain:

    def __init__(self, eng, sem, base=0):
        self.eng, self.sem, self.at, self.count = eng, sem, base, 0

    def link(self, ins):
        self.at, self.count = self.at + 1, self.count + 1
        ins.then_inc(self.sem, 1)
        self.eng.wait_ge(self.sem, self.at)


def flat(ap):
    return ap.rearrange("p a b -> p (a b)")


def one(ap, g):
    if isinstance(g, int):
        return ap[:, g, :]
    return ap[:, bass.ds(g, 1), :].rearrange("p a b -> p (a b)")


def prepare(nc, io, t):
    x, src, dst, norm = io["x"], io["src"], io["dst"], io["edge_weight1"]
    with ExitStack() as ctx:
        sb = lambda n, s, d: ctx.enter_context(nc.sbuf_tensor("pre_" + n, s, d))
        sem = lambda n: ctx.enter_context(nc.semaphore("pre_" + n))
        raw_src, raw_dst = sb("raw_src", [P, RAW, P], I32), sb("raw_dst", [P, RAW, P], I32)
        raw_norm = sb("raw_norm", [P, RAW, P], F32)
        src_f, dst_f = sb("src_f", [P, RAW, P], F32), sb("dst_f", [P, RAW, P], F32)
        stats, mv = sb("stats", [P, GROUPS, 6], F32), sb("mv", [P, GROUPS, 2], F32)
        rstd = sb("rstd", [P, GROUPS], F32)
        t_max, t_min, tile_id = sb("t_max", [P, RAW], F32), sb("t_min", [P, RAW], F32), sb("tile_id", [P, RAW], F32)
        win_lo, ring_lo = sb("win_lo", [P, WINDOWS], F32), sb("ring_lo", [P, WINDOWS], F32)
        kk = sb("kk", [P, 8], F32)
        before = sb("before", [P, RAW, WINDOWS], BF16)
        va, vb = sb("va", [P, RAW, WINDOWS], F32), sb("vb", [P, RAW, WINDOWS], F32)
        vc = sb("vc", [P, RAW, WINDOWS], F32)
        first = sb("first", [P, WINDOWS], F32)
        r1, r2 = sb("r1", [P, WINDOWS], F32), sb("r2", [P, WINDOWS], F32)
        bad, bad2 = sb("bad", [P, 1], F32), sb("bad2", [P, 1], F32)
        pos_f = sb("pos_f", [P, WINDOWS, 8], F32)
        ones_bf = sb("ones_bf", [P, P], BF16)
        ia, ib, dst_i = sb("ia", [P, TILES], I32), sb("ib", [P, TILES], I32), sb("dst_i", [P, TILES], I32)
        fa, fb = sb("fa", [P, TILES], F32), sb("fb", [P, TILES], F32)
        comp = sb("comp", [RH, 2, 2 * NB], F32)
        rest = sb("rest", [RH, 2, 2 * NB], F32)

        ps = lambda n: ctx.enter_context(nc.psum_tensor("pre_" + n, [P, 512], F32))
        ps_src, ps_dst, ps_norm = [ps("s0"), ps("s1")], [ps("d0"), ps("d1")], [ps("n0"), ps("n1")]
        ps_first, ps_bad = ps("ps_first"), ps("ps_bad")

        pads_set, consts_set = sem("pads_set"), sem("consts_set")
        x_in, src_in, dst_in, norm_in = sem("x_in"), sem("src_in"), sem("dst_in"), sem("norm_in")
        w_in, comp_in = sem("w_in"), sem("comp_in")
        ve, ve_ln = sem("vector_chain"), sem("centred")
        var_ready, sd_ready, h_ready, h_out = sem("var_ready"), sem("sd_ready"), sem("h_ready"), sem("h_out")
        srcf_ready, dstf_ready, src_t, dst_t, norm_t = (sem(n) for n in ("srcf", "dstf", "src_t", "dst_t", "norm_t"))
        before_ready, first_done, bad_ready, bad_done = (sem(n) for n in ("before", "first_done", "bad_ready", "bad_done"))
        full = (RAW - 1) * P * P
        rows = (E - full) // P
        tail = E - full - rows * P

        block = ctx.enter_context(nc.Block())

        def edge_loads(eng, raw, flat_dram, done):
            eng.dma_start(raw[:, 0:RAW - 1, :], flat_dram[0:full].rearrange("(c q e) -> q c e", q=P, e=P)).then_inc(done, 16)
            eng.dma_start(raw[0:rows, RAW - 1, :], flat_dram[full:full + rows * P].rearrange("(q e) -> q e", e=P)).then_inc(done, 16)
            eng.dma_start(raw[rows:rows + 1, RAW - 1, 0:tail], flat_dram[full + rows * P:E].rearrange("(q e) -> q e", q=1)).then_inc(done, 16)

        @block.sync
        def _(sp):
            sp.dma_start(t.X[:, 0:GROUPS - 1, :], x[0:(GROUPS - 1) * P, :].rearrange("(g p) d -> p g d", p=P)).then_inc(x_in, 16)
            sp.wait_ge(pads_set, 4)
            sp.dma_start(t.X[0:LAST_ROWS, GROUPS - 1, :], x[(GROUPS - 1) * P:N, :]).then_inc(x_in, 16)
            edge_loads(sp, raw_dst, dst, dst_in)
            edge_loads(sp, raw_norm, norm.rearrange("e a -> (e a)"), norm_in)
            for i, name in enumerate(("L0_gnn_V1", "L0_gnn_V2")):
                sp.dma_start(t.V[i][:, :, :], io[name].rearrange("b d o -> d b o")).then_inc(w_in, 16)
            for i, name in enumerate(("L0_gnn_loop1", "L0_gnn_loop2", "L1_gnn_W1", "L1_gnn_W2")):
                sp.dma_start(t.W[i][:, :], io[name]).then_inc(w_in, 16)
            for i, name in enumerate(("L0_gnn_bias1", "L0_gnn_bias2")):
                sp.dma_start(t.bias_row[i][:, :], io[name].rearrange("(a n) -> a n", a=1)).then_inc(w_in, 16)
            for i, name in enumerate(("L1_gnn_b1", "L1_gnn_b2")):
                sp.dma_start(t.bias_all[i][:, :], io[name].rearrange("(a n) -> a n", a=1).to_broadcast([P, D])).then_inc(w_in, 16)
            sp.wait_ge(h_ready, 1)
            sp.dma_start(t.h1_dram.rearrange("(g p) d -> p g d", p=P), t.H[:, :, :]).then_inc(h_out, 16)
            sp.wait_ge(w_in, 10 * 16)
            sp.wait_ge(h_out, 16)

        @block.scalar
        def _(act):
            for l, name in enumerate(("L0_gnn_comp1", "L0_gnn_comp2")):
                for h in range(2):
                    act.dma_start(comp[:, h, l * NB:(l + 1) * NB], io[name][h * RH:(h + 1) * RH, :]).then_inc(comp_in, 16)
            act.wait_ge(pads_set, 4)
            edge_loads(act, raw_src, src, src_in)
            act.wait_ge(var_ready, 1)
            nc.scalar.activation(rstd[:, :], rstd[:, :], ACT.Sqrt).then_inc(sd_ready, 1)
            act.wait_ge(ve_ln, 1)
            nc.scalar.activation(t.H[:, :, :], t.H[:, :, :], ACT.Relu).then_inc(h_ready, 1)

        @block.gpsimd
        def _(pool):
            g = nc.gpsimd
            g.memset(t.X[:, GROUPS - 1, :], 0.0).then_inc(pads_set, 1)
            g.memset(raw_src[:, RAW - 1, :], 0).then_inc(pads_set, 1)
            g.memset(raw_dst[:, RAW - 1, :], PAD_DST).then_inc(pads_set, 1)
            g.memset(raw_norm[:, RAW - 1, :], 0.0).then_inc(pads_set, 1)
            g.memset(t.ident[:, :], 0.0).then_inc(consts_set, 1)
            g.memset(t.ones[:, :], 1.0).then_inc(consts_set, 1)
            g.memset(ones_bf[:, :], 1.0).then_inc(consts_set, 1)
            g.memset(t.ones16[:, :], 1.0).then_inc(consts_set, 1)
            pool.wait_ge(consts_set, 4)
            g.affine_select(out=t.ident[:, :], in_=t.ident[:, :], compare_op=ALU.not_equal, fill=1.0, base=0,
                            pattern=[[-1, P]], channel_multiplier=1).then_inc(consts_set, 1)
            io_ = lambda out, pattern, base=0, cm=0: g.iota(out, pattern=pattern, base=base, channel_multiplier=cm,
                                                           allow_small_or_imprecise_dtypes=True).then_inc(consts_set, 1)
            io_(win_lo[:, :], [[WIN, WINDOWS]])
            io_(tile_id[:, :], [[P, RAW]], cm=1)
            io_(ring_lo[:, :], [[CHUNK, WINDOWS // 4], [0, 4]], base=-CHUNK)
            io_(kk[:, :], [[1, 8]])
            io_(t.neg_win[:, :], [[-WIN, WINDOWS]])
            io_(t.win512[:, :], [[512, WINDOWS]])
            io_(t.iota16[:, :], [[1, WIN]])
            io_(t.iota400[:, :], [[1, AW]])
            io_(t.iota128[:, :], [[1, P]])
            io_(t.type_id[:, :], [[RH, 2]], cm=1)
            io_(t.group_lo[:, :], [[P, GROUPS]])

        @block.tensor
        def _(pe):
            m = nc.tensor
            pe.wait_ge(before_ready, 1)
            for c in range(RAW):
                ins = m.matmul(ps_first[:, 0:WINDOWS], ones_bf[:, :], before[:, c, :], start=(c == 0), stop=(c == RAW - 1))
            ins.then_inc(first_done, 1)

            def turn(blocks, ps_pair, done):
                for c in range(RAW):
                    ins = m.transpose(ps_pair[c // 4][:, c % 4 * P:(c % 4 + 1) * P], blocks[:, c, :], t.ident[:, :])
                ins.then_inc(done, 1)

            pe.wait_ge(srcf_ready, 1)
            turn(src_f, ps_src, src_t)
            pe.wait_ge(dstf_ready, 1)
            turn(dst_f, ps_dst, dst_t)
            pe.wait_ge(norm_in, 48)
            turn(raw_norm, ps_norm, norm_t)
            pe.wait_ge(bad_ready, 1)
            m.matmul(ps_bad[:, 0:1], t.ones[:, :], bad[:, :], start=True, stop=True).then_inc(bad_done, 1)

        @block.vector
        def _(dve):
            v = nc.vector
            k = Chain(dve, ve)
            dve.wait_ge(x_in, 32)
            for g in range(GROUPS):
                ins = v.bn_stats(stats[:, g, :], t.X[:, g, :])
            k.link(ins)
            for g in range(GROUPS):
                ins = v.bn_aggr(mv[:, g, :], stats[:, g, :])
            k.link(ins)
            v.tensor_scalar(rstd[:, :], mv[:, :, 1], EPS, None, ALU.add).then_inc(var_ready, 1)
            dve.wait_ge(dst_in, 48)
            v.tensor_copy(dst_f[:, :, :], raw_dst[:, :, :]).then_inc(dstf_ready, 1)
            dve.wait_ge(sd_ready, 1)
            k.link(v.reciprocal(rstd[:, :], rstd[:, :]))
            for g in range(GROUPS):
                ins = v.tensor_scalar(t.H[:, g, :], t.X[:, g, :], mv[:, g, 0:1], rstd[:, g:g + 1], ALU.subtract, ALU.mult)
            ins.then_inc(ve_ln, 1)
            dve.wait_ge(src_in, 48)
            v.tensor_copy(src_f[:, :, :], raw_src[:, :, :]).then_inc(srcf_ready, 1)
            dve.wait_ge(dstf_ready, 1)
            v.tensor_reduce(t_max[:, :], dst_f[:, :, :], AX.X, ALU.max)
            k.link(v.tensor_reduce(t_min[:, :], dst_f[:, :, :], AX.X, ALU.min))
            dve.wait_ge(consts_set, 16)
            wide = [P, RAW, WINDOWS]
            v.tensor_tensor(before[:, :, :], t_max[:, :].unsqueeze(2).to_broadcast(wide),
                            win_lo[:, :].unsqueeze(1).to_broadcast(wide), ALU.is_lt).then_inc(before_ready, 1)
            k.link(v.scalar_tensor_tensor(out=va[:, :, :], in0=win_lo[:, :].unsqueeze(1).to_broadcast(wide), scalar=float(WIN),
                                          in1=t_min[:, :].unsqueeze(2).to_broadcast(wide), op0=ALU.add, op1=ALU.is_gt))
            dve.wait_ge(before_ready, 1)
            k.link(v.tensor_tensor(va[:, :, :], va[:, :, :], before[:, :, :], ALU.subtract))
            dve.wait_ge(first_done, 1)
            k.link(v.tensor_scalar(first[:, :], ps_first[:, 0:WINDOWS], float(TILES - SPAN), None, ALU.min))
            k.link(v.tensor_tensor(vb[:, :, :], first[:, :].unsqueeze(1).to_broadcast(wide),
                                   tile_id[:, :].unsqueeze(2).to_broadcast(wide), ALU.subtract))
            k.link(v.tensor_scalar(vc[:, :, :], vb[:, :, :], 0.0, None, ALU.is_gt))
            k.link(v.scalar_tensor_tensor(out=vc[:, :, :], in0=vb[:, :, :], scalar=float(1 - SPAN), in1=vc[:, :, :],
                                          op0=ALU.is_lt, op1=ALU.add))
            k.link(v.tensor_tensor(va[:, :, :], va[:, :, :], vc[:, :, :], ALU.mult))
            k.link(v.tensor_reduce(bad[:, :], va[:, :, :], AX.XY, ALU.add))
            k.link(v.tensor_tensor(r1[:, :], first[:, :], ring_lo[:, :], ALU.is_lt))
            k.link(v.scalar_tensor_tensor(out=r2[:, :], in0=first[:, :], scalar=float(SPAN - 3 * CHUNK), in1=ring_lo[:, :],
                                          op0=ALU.add, op1=ALU.is_gt))
            k.link(v.tensor_tensor(r1[:, :], r1[:, :], r2[:, :], ALU.add))
            k.link(v.tensor_reduce(bad2[:, :], r1[:, :], AX.X, ALU.add))
            v.tensor_tensor(bad[:, :], bad[:, :], bad2[:, :], ALU.add).then_inc(bad_ready, 1)
            k.link(v.tensor_tensor(pos_f[:, :, :], first[:, :].unsqueeze(2).to_broadcast([P, WINDOWS, 8]),
                                   kk[:, :].unsqueeze(1).to_broadcast([P, WINDOWS, 8]), ALU.add))
            k.link(v.tensor_copy(t.pos[:, :, :], pos_f[0:1, :, :]))
            k.link(v.tensor_single_scalar(t.pos[:, :, :], t.pos[:, :, :], RING - 1, ALU.bitwise_and))
            k.link(v.tensor_copy(t.first[:, :], first[0:1, :]))
            cut = 4 * P

            def column(out, pair):
                v.tensor_copy(out[:, 0:cut], pair[0][:, :])
                k.link(v.tensor_copy(out[:, cut:TILES], pair[1][:, 0:TILES - cut]))

            dve.wait_ge(src_t, 1)
            column(t.idx, ps_src)
            dve.wait_ge(dst_t, 1)
            column(t.dst, ps_dst)
            column(dst_i, ps_dst)
            dve.wait_ge(norm_t, 1)
            column(t.norm, ps_norm)
            k.link(v.tensor_single_scalar(ia[:, :], t.idx[:, :], P - 1, ALU.bitwise_and))
            k.link(v.tensor_copy(t.src_lo[:, :], ia[:, :]))
            k.link(v.tensor_single_scalar(ib[:, :], t.idx[:, :], 7, ALU.logical_shift_right))
            k.link(v.tensor_copy(fa[:, :], ib[:, :]))
            k.link(v.tensor_single_scalar(ia[:, :], dst_i[:, :], WIN - 1, ALU.bitwise_and))
            k.link(v.tensor_copy(fb[:, :], ia[:, :]))
            k.link(v.tensor_scalar(t.key[:, :], t.dst[:, :], 32.0, None, ALU.mult))
            k.link(v.scalar_tensor_tensor(out=t.key[:, :], in0=fa[:, :], scalar=16.0, in1=t.key[:, :], op0=ALU.mult, op1=ALU.add))
            k.link(v.scalar_tensor_tensor(out=t.key[:, :], in0=fb[:, :], scalar=-31.0, in1=t.key[:, :], op0=ALU.mult, op1=ALU.add))
            dve.wait_ge(comp_in, 64)
            k.link(v.tensor_copy(t.comp[:, 0, :, :], comp[:, :, :]))
            k.link(v.tensor_tensor(rest[:, :, :], comp[:, :, :], t.comp[:, 0, :, :], ALU.subtract))
            k.link(v.tensor_copy(t.comp[:, 1, :, :], rest[:, :, :]))
            k.link(v.tensor_tensor(rest[:, :, :], rest[:, :, :], t.comp[:, 1, :, :], ALU.subtract))
            k.link(v.tensor_copy(t.comp[:, 2, :, :], rest[:, :, :]))
            dve.wait_ge(bad_done, 1)
            k.link(v.tensor_scalar(t.slow[:, :], ps_bad[0:1, 0:1], 0.0, None, ALU.is_gt))


class Coefficients:

    def __init__(self, nc, io, t, ctx, name):
        self.nc, self.io, self.t = nc, io, t
        sem = lambda n: ctx.enter_context(nc.semaphore(f"{name}_{n}"))
        self.etype = ctx.enter_context(nc.sbuf_tensor(f"{name}_types", [RH, 2, ET * P], I32))
        self.onehot = ctx.enter_context(nc.sbuf_tensor(f"{name}_onehot", [RH, 2, 2, ET * P], BF16))
        self.ps = ctx.enter_context(nc.psum_tensor(f"{name}_ps", [P, 512], F32))
        self.etype_in = [sem("types_in0"), sem("types_in1")]
        self.onehot_ready, self.product_done, self.coef_ready = sem("onehot_ready"), sem("product_done"), sem("coef_ready")

    def load(self, eng, m, s):
        after(eng, self.onehot_ready, m - 1)
        count = ET * P if not isinstance(m, int) else min(ET * P, E - m * ET * P)
        rows = self.io["edge_type_200"].rearrange("(a n) -> a n", a=1)
        eng.dma_start(self.etype[:, s, 0:count], rows[:, bass.ds(m * ET * P, count)].to_broadcast([RH, count]))\
           .then_inc(self.etype_in[s], 16)

    def make_onehot(self, eng, m, half_m, s):
        after(eng, self.product_done, m - 1)
        eng.wait_ge(self.etype_in[s], (half_m + 1) * 16)
        for h in range(2):
            ins = self.nc.vector.tensor_scalar(self.onehot[:, s, h, :], self.etype[:, s, :], self.t.type_id[0:RH, h:h + 1],
                                               None, ALU.is_equal)
        ins.then_inc(self.onehot_ready, 1)

    def multiply(self, eng, m, s):
        after(eng, self.coef_ready, m)
        eng.wait_ge(self.onehot_ready, m + 1)
        for e in range(ET):
            for h in range(2):
                for part in range(3):
                    ins = self.nc.tensor.matmul(self.ps[:, e * 2 * NB:(e + 1) * 2 * NB], self.onehot[:, s, h, e * P:(e + 1) * P],
                                                self.t.comp[:, part, h, :], start=(h == 0 and part == 0),
                                                stop=(h == 1 and part == 2))
        ins.then_inc(self.product_done, 1)

    def scale(self, eng, m):
        eng.wait_ge(self.product_done, m + 1)
        for l in range(2):
            ins = self.nc.vector.tensor_tensor(self.t.coef[l][:, bass.ds(m * ET, ET), :],
                                               self.ps[:, 0:ET * 2 * NB].rearrange("p (e l b) -> p l e b", l=2, b=NB)[:, l, :, :],
                                               self.t.norm[:, bass.ds(m * ET, ET)].unsqueeze(2).to_broadcast([P, ET, NB]), ALU.mult)
        ins.then_inc(self.coef_ready, 1)


class Finish:

    def __init__(self, nc, t, ctx, name, layer):
        self.nc, self.t, self.layer = nc, t, layer
        sb = lambda n, s, d: ctx.enter_context(nc.sbuf_tensor(f"{name}_{n}", s, d))
        sem = lambda n: ctx.enter_context(nc.semaphore(f"{name}_{n}"))
        self.sem_passed = sem("passed")
        self.ZT = sb("ZT", [P, NB, P], F32)
        self.h_stage, self.hT = sb("h_stage", [P, P], F32), sb("hT", [P, P], F32)
        self.ps_h = ctx.enter_context(nc.psum_tensor(f"{name}_ps_h", [P, 512], F32))
        self.ps_o = ctx.enter_context(nc.psum_tensor(f"{name}_ps_o", [P, 512], F32))
        self.staged, self.turned, self.hT_ready = sem("staged"), sem("turned"), sem("hT_ready")
        self.out_done, self.h_new, self.rows_out = sem("out_done"), sem("h_new"), sem("rows_out")
        if layer == 1:
            self.xs, self.hn, self.r = sb("xs", [P, P], F32), sb("hn", [P, P], F32), sb("r", [P, P], F32)
            self.hp, self.parts, self.hnT = sb("hp", [P, P], F32), sb("parts", [P, 3, P], BF16), sb("hnT", [P, P], F32)
            self.stats, self.mv, self.roots = sb("stats", [P, 6], F32), sb("mv", [P, 2], F32), sb("roots", [P, 2], F32)
            self.xs_ready, self.xs_kept, self.var_ready, self.sd_ready = sem("xs_ready"), sem("xs_kept"), sem("var_ready"), sem("sd_ready")
            self.hn_ready, self.hn_turned, self.hnT_ready = sem("hn_ready"), sem("hn_turned"), sem("hnT_ready")
            self.w1_done, self.parts_ready, self.parts_kept = sem("w1_done"), sem("parts_ready"), sem("parts_kept")
            self.chain = sem("chain")

    def hold(self, act, sem, value):
        if isinstance(value, int) and value <= 0:
            return
        act.wait_ge(sem, value)
        act.sem_inc(self.sem_passed, 1)

    def act_stage(self, act, g):
        self.hold(act, self.turned, g)
        self.nc.scalar.activation(self.h_stage[:, :], one(self.t.H, g), ACT.Copy).then_inc(self.staged, 1)
        self.hold(act, self.out_done, g)
        self.hold(act, self.turned, g + 1)
        self.nc.scalar.activation(self.hT[:, :], self.ps_h[:, 0:P], ACT.Copy).then_inc(self.hT_ready, 1)

    def pe_turn(self, pe, g):
        after(pe, self.hT_ready, g)
        pe.wait_ge(self.staged, g + 1)
        self.nc.tensor.transpose(self.ps_h[:, 0:P], self.h_stage[:, :], self.t.ident[:, :]).then_inc(self.turned, 1)

    def pe_out(self, pe, g):
        t, m = self.t, self.nc.tensor
        after(pe, self.h_new if self.layer == 0 else self.parts_ready, g)
        pe.wait_ge(self.hT_ready, g + 1)
        for b in range(NB):
            m.matmul(self.ps_o[:, 0:P], self.ZT[:, b, :], t.V[self.layer][:, b, :], start=(b == 0), stop=False)
        m.matmul(self.ps_o[:, 0:P], self.hT[:, :], t.W[self.layer][:, :], start=False, stop=False)
        m.matmul(self.ps_o[:, 0:P], t.ones[0:1, :], t.bias_row[self.layer][:, :], start=False, stop=True)\
         .then_inc(self.out_done, 1)

    def pe_turn_new(self, pe, g):
        pe.wait_ge(self.hn_ready, g + 1)
        self.nc.tensor.transpose(self.ps_h[:, P:2 * P], self.hn[:, :], self.t.ident[:, :]).then_inc(self.hn_turned, 1)

    def pe_w1(self, pe, g):
        pe.wait_ge(self.hnT_ready, g + 1)
        self.nc.tensor.matmul(self.ps_o[:, P:2 * P], self.hnT[:, :], self.t.W[2][:, :], start=True, stop=True).then_inc(self.w1_done, 1)

    def act_relu(self, act, g, rows_dram):
        self.hold(act, self.out_done, g + 1)
        self.nc.scalar.activation(one(self.t.H, g), self.ps_o[:, 0:P], ACT.Relu).then_inc(self.h_new, 1)
        self.hold(act, self.h_new, g + 1)
        act.dma_start(rows_dram[bass.ds(g * P, P), :], one(self.t.H, g)).then_inc(self.rows_out, 16)

    def act_x(self, act, g):
        self.hold(act, self.xs_ready, g + 1)
        self.nc.scalar.activation(one(self.t.X, g), self.xs[:, :], ACT.Copy).then_inc(self.xs_kept, 1)
        self.hold(act, self.var_ready, g + 1)
        self.nc.scalar.activation(self.roots[:, :], self.roots[:, :], ACT.Sqrt).then_inc(self.sd_ready, 1)

    def act_hnT(self, act, g):
        self.hold(act, self.w1_done, g)
        self.hold(act, self.hn_turned, g + 1)
        self.nc.scalar.activation(self.hnT[:, :], self.ps_h[:, P:2 * P], ACT.Copy).then_inc(self.hnT_ready, 1)

    def act_parts(self, act, g, rows_dram=None):
        t, s = self.t, self.nc.scalar
        self.hold(act, self.parts_ready, g + 1)
        s.activation(one(t.HP[0], g), self.hp[:, :], ACT.Copy).then_inc(self.parts_kept, 1)
        out = t.S[0][:, bass.ds(g, 1), :, :].rearrange("p a b c -> p (a b) c")
        s.activation(out, self.parts[:, :, :], ACT.Copy).then_inc(self.parts_kept, 1)
        if rows_dram is not None:
            self.hold(act, self.parts_kept, 2 * (g + 1))
            act.dma_start(rows_dram[bass.ds(g * P, P), :], one(t.HP[0], g)).then_inc(self.rows_out, 16)

    def dve_x(self, dve, g):
        t, v = self.t, self.nc.vector
        self.k = Chain(dve, self.chain, 8 * g)
        after(dve, self.xs_kept, g)
        dve.wait_ge(self.out_done, g + 1)
        v.tensor_tensor(self.xs[:, :], self.ps_o[:, 0:P], one(t.X, g), ALU.add).then_inc(self.xs_ready, 1)
        dve.wait_ge(self.xs_ready, g + 1)
        self.k.link(v.bn_stats(self.stats[:, :], self.xs[:, :]))
        dve.sem_inc(self.sem_passed, 1)
        self.k.link(v.bn_aggr(self.mv[:, :], self.stats[:, :]))
        v.tensor_scalar(self.roots[:, 0:1], self.mv[:, 1:2], EPS, None, ALU.add)
        v.tensor_scalar(self.roots[:, 1:2], t.deg[:, bass.ds(g, 1)], 1.0, None, ALU.add).then_inc(self.var_ready, 1)

    def dve_norm(self, dve, g):
        t, v, k = self.t, self.nc.vector, self.k
        dve.wait_ge(self.sd_ready, g + 1)
        k.link(v.reciprocal(self.roots[:, :], self.roots[:, :]))
        v.tensor_scalar(t.dinv[:, bass.ds(g, 1)], self.roots[:, 1:2], 1.0, None, ALU.mult)
        k.link(v.tensor_scalar(self.r[:, :], self.xs[:, :], self.mv[:, 0:1], self.roots[:, 0:1], ALU.subtract, ALU.mult))
        v.tensor_scalar(self.hn[:, :], self.r[:, :], 0.0, None, ALU.max).then_inc(self.hn_ready, 1)

    def dve_parts(self, dve, g):
        t, v, k = self.t, self.nc.vector, self.k
        after(dve, self.parts_kept, 2 * g)
        dve.wait_ge(self.w1_done, g + 1)
        k.link(v.tensor_scalar(self.hp[:, :], self.ps_o[:, P:2 * P], self.roots[:, 1:2], None, ALU.mult))
        split(v, k, self.hp, self.r, self.parts, self.parts_ready)
        assert k.count == 8


def split(v, k, whole, r, parts, done):
    k.link(v.tensor_scalar(parts[:, 0, :], whole[:, :], 1.0, None, ALU.mult))
    k.link(v.tensor_tensor(r[:, :], whole[:, :], parts[:, 0, :], ALU.subtract))
    k.link(v.tensor_scalar(parts[:, 1, :], r[:, :], 1.0, None, ALU.mult))
    v.tensor_tensor(parts[:, 2, :], r[:, :], parts[:, 1, :], ALU.subtract).then_inc(done, 1)


def relational_layer(nc, io, t, layer, rows_in, rows_out):
    name = f"rel{layer}"
    with ExitStack() as ctx:
        sb = lambda n, s, d: ctx.enter_context(nc.sbuf_tensor(f"{name}_{n}", s, d))
        sem = lambda n: ctx.enter_context(nc.semaphore(f"{name}_{n}"))
        ps = lambda n: ctx.enter_context(nc.psum_tensor(f"{name}_{n}", [P, 512], F32))
        idx = [sb(f"idx{i}", [P, CHUNK], I32) for i in range(2)]
        match = [sb(f"match{i}", [P, SPAN, WIN], F32) for i in range(2)]
        C = [sb(f"C{i}", [P, SPAN, NB, WIN], F32) for i in range(2)]
        Z = [sb(f"Z{i}", [P, P], F32) for i in range(2)]
        fin = Finish(nc, t, ctx, name, layer)
        ps_z = [ps("ps_z0"), ps("ps_z1")]
        ps_t = ps("ps_t")
        idx_ready = sem("idx_ready")
        ring_even, ring_odd = sem("ring_even"), sem("ring_odd")
        z_done, t_done = sem("z_done"), sem("t_done")
        match_ready, c_ready, z_ready, zt_ready = sem("match_ready"), sem("c_ready"), sem("z_ready"), sem("zt_ready")
        passed = sem("waits_passed")
        ring = t.ring
        M = [sb(f"M{i}", [P, SPAN, AW], BF16) for i in range(2)]
        lo = [sb(f"lo{i}", [P, SPAN, P], BF16) for i in range(2)]
        A = sb("A", [P, SRC_BLOCKS, P], F16)
        ps_a = [ps("ps_a0"), ps("ps_a1")]
        m_ready, a_done, a_kept = sem("m_ready"), sem("a_done"), sem("a_kept")
        deg_done, deg_kept, a_out = sem("deg_done"), sem("deg_kept"), sem("a_out")
        co = Coefficients(nc, io, t, ctx, name) if layer == 0 else None
        block = ctx.enter_context(nc.Block())
        AHEAD = 12

        def hold(eng, s, value):
            if isinstance(value, int) and value <= 0:
                return
            eng.wait_ge(s, value)
            eng.sem_inc(passed, 1)

        def groups(eng, body):
            for parity in range(2):
                body(0, parity)
            with eng.Fori(1, 10) as pair:
                for parity in range(2):
                    body(pair, parity)
            for g in range(20, GROUPS):
                body(g // 2, g % 2)

        def builds(parity):
            return parity == layer

        def chunks_next(pair, parity):
            if layer or parity == 0:
                return 0
            if isinstance(pair, int):
                return min(8, max(0, ET_CHUNKS - AHEAD - 8 * pair))
            return 8

        @block.gpsimd
        def _(pool):
            g_ = nc.gpsimd

            def chunk(c, half_c, s):
                if not isinstance(c, int) or c >= 4:
                    hold(pool, z_done, (c - 2) * 4)
                landed = (ring_even, ring_odd)[s % 2]
                hold(pool, landed, CHUNK * 16 * half_c)
                g_.tensor_copy(idx[s % 2][:, :], t.idx[:, bass.ds(c * CHUNK, CHUNK)]).then_inc(idx_ready, 1)
                hold(pool, idx_ready, c + 1)
                for i in range(CHUNK):
                    g_.indirect_dma_start(ring[:, s * CHUNK + i, :], None, rows_in,
                                          bass.IndirectOffsetOnAxis(ap=idx[s % 2][:, i:i + 1], axis=0)).then_inc(landed, 16)

            for s in range(4):
                chunk(s, s // 2, s)
            with pool.Fori(1, CHUNKS // 4) as m:
                for s in range(4):
                    chunk(m * 4 + s, m * 2 + s // 2, s)
            chunk(CHUNKS - 1, (CHUNKS - 1) // 2, 0)

        if layer == 0:
            @block.sync
            def _(sp):
                for m in range(AHEAD):
                    co.load(sp, m, m % 2)

                def group(pair, parity):
                    for i in range(chunks_next(pair, parity)):
                        co.load(sp, pair * 8 + (AHEAD + i), i % 2)
                groups(sp, group)

        @block.vector
        def _(dve):
            v = nc.vector
            if layer == 0:
                for m in range(AHEAD):
                    co.make_onehot(dve, m, m // 2, m % 2)
                    if m:
                        co.scale(dve, m - 1)
                co.scale(dve, AHEAD - 1)
            regs = [dve.alloc_register(f"{name}_first{i}") for i in range(WPG)]

            def window(j, bj, i, start, build):
                s = i % 2
                tiles = bass.ds(start, SPAN)
                shape = [P, SPAN, WIN]
                v.scalar_tensor_tensor(out=match[s][:, :, :], in0=t.dst[:, tiles].unsqueeze(2).to_broadcast(shape),
                                       scalar=t.neg_win[:, bass.ds(j, 1)],
                                       in1=t.iota16[:, :].unsqueeze(1).to_broadcast(shape),
                                       op0=ALU.add, op1=ALU.is_equal).then_inc(match_ready, 1)
                if build:
                    after(dve, a_done, bj - 1)
                    for k in range(SPAN):
                        tile = bass.ds(start + k, 1)
                        v.tensor_scalar(M[s][:, k, :], t.iota400[:, :], t.win512[:, bass.ds(j, 1)], t.key[:, tile],
                                        ALU.add, ALU.is_equal)
                        ins = v.tensor_scalar(lo[s][:, k, :], t.iota128[:, :], t.src_lo[:, tile], None, ALU.is_equal)
                    ins.then_inc(m_ready, 1)
                after(dve, z_done, j - 1)
                dve.wait_ge(match_ready, j + 1)
                shape = [P, SPAN, NB, WIN]
                v.tensor_tensor(C[s][:, :, :, :], match[s][:, :, :].unsqueeze(2).to_broadcast(shape),
                                t.coef[layer][:, tiles, :].unsqueeze(3).to_broadcast(shape), ALU.mult).then_inc(c_ready, 1)

            def keep_deg(pair, g):
                dve.wait_ge(deg_done, pair + 1)
                v.tensor_scalar(t.deg[:, bass.ds(g, 1)], fin.ps_h[:, 2 * P:2 * P + 1], 1.0, None, ALU.mult).then_inc(deg_kept, 1)

            def finish(g, pair, parity, i):
                if layer == 0:
                    if i == 0 and parity == 0:
                        keep_deg(pair, g)
                elif i == 1:
                    if parity == 1:
                        keep_deg(pair, g)
                    fin.dve_x(dve, g)
                elif i == 3:
                    fin.dve_norm(dve, g)
                elif i == 7:
                    fin.dve_parts(dve, g)

            def group(pair, parity):
                g = pair * 2 + parity
                dve.load(regs, t.first[0:1, bass.ds(g * WPG, WPG)])
                starts = [dve.snap(r, min_val=0, max_val=TILES - SPAN) for r in regs]
                chunks = chunks_next(pair, parity)
                if layer == 0:
                    made = AHEAD + pair * 8
                    dve.wait_ge(co.coef_ready, min(made, ET_CHUNKS) if isinstance(made, int) else made)
                for i in range(WPG):
                    m = pair * 8 + (AHEAD + i)
                    if i < chunks:
                        co.make_onehot(dve, m, pair * 4 + (AHEAD + i) // 2, i % 2)
                    window(g * WPG + i, pair * WPG + i, i, starts[i], builds(parity))
                    if 0 < i <= chunks:
                        co.scale(dve, m - 1)
                    if not (isinstance(g, int) and g == 0):
                        finish(g - 1, pair - (1 - parity), 1 - parity, i)
                if chunks == WPG:
                    co.scale(dve, pair * 8 + (AHEAD + WPG - 1))
            groups(dve, group)
            for i in range(WPG):
                finish(GROUPS - 1, GROUPS // 2, 0, i)

        @block.tensor
        def _(pe):
            m_ = nc.tensor
            if layer == 0:
                for m in range(AHEAD):
                    co.multiply(pe, m, m % 2)
            regs = [pe.alloc_register(f"{name}_pos{i}") for i in range(SPAN)]

            def turn(g, i):
                j = g * WPG + i
                pe.wait_ge(z_ready, j + 1)
                after(pe, zt_ready, j)
                m_.transpose(ps_t[:, 0:P], Z[i % 2][:, :], t.ident[:, :]).then_inc(t_done, 1)

            def group(pair, parity):
                g = pair * 2 + parity
                is_last, is_first = (isinstance(g, int) and g == n for n in (GROUPS - 1, 0))
                after(pe, deg_kept, pair if layer == 1 or parity == 0 else pair + 1)
                fin.pe_turn(pe, g)
                for i in range(WPG):
                    j, s = g * WPG + i, i % 2
                    pe.load(regs, t.pos[0:1, bass.ds(j, 1), 0:SPAN].rearrange("p a b -> p (a b)"))
                    at = [pe.snap(r, min_val=0, max_val=RING - 1) for r in regs]
                    if i == 0:
                        pe.wait_ge(ring_even, (g + 1) * (16 * CHUNK))
                        pe.wait_ge(ring_odd, (g if is_last else g + 1) * (16 * CHUNK))
                    if i == WPG // 2 and not is_last:
                        pe.wait_ge(ring_even, (g + 2) * (16 * CHUNK))
                    after(pe, z_ready, j - 1)
                    pe.wait_ge(c_ready, j + 1)
                    for k in range(SPAN):
                        ins = m_.matmul(ps_z[s][:, 0:P], C[s][:, k, :, :].rearrange("p b w -> p (b w)"), one(ring, at[k]),
                                        start=(k == 0), stop=(k == SPAN - 1))
                    ins.then_inc(z_done, 1)
                    if builds(parity):
                        bj = pair * WPG + i
                        after(pe, a_kept, bj - 1)
                        pe.wait_ge(m_ready, bj + 1)
                        for k in range(SPAN):
                            ins = m_.matmul(ps_a[s][:, 0:AW], lo[s][:, k, :], M[s][:, k, :], start=(k == 0), stop=(k == SPAN - 1))
                        ins.then_inc(a_done, 1)
                    if i < chunks_next(pair, parity):
                        co.multiply(pe, pair * 8 + (AHEAD + i), i % 2)
                    if i:
                        turn(g, i - 1)
                    if layer == 1 and not is_first:
                        if i == 4:
                            pe.wait_ge(fin.hT_ready, g + 1)
                            fin.pe_turn_new(pe, g - 1)
                        if i == 6:
                            fin.pe_w1(pe, g - 1)
                turn(g, WPG - 1)
                pe.wait_ge(zt_ready, (g + 1) * WPG)
                fin.pe_out(pe, g)
                if builds(parity):
                    pe.wait_ge(a_kept, (pair + 1) * WPG)
                    for b in range(SRC_BLOCKS):
                        ins = m_.matmul(fin.ps_h[:, 2 * P:2 * P + 1], A[:, b, :], t.ones16[:, 0:1],
                                        start=(b == 0), stop=(b == SRC_BLOCKS - 1))
                    ins.then_inc(deg_done, 1)
            groups(pe, group)
            if layer == 1:
                fin.pe_turn_new(pe, GROUPS - 1)
                fin.pe_w1(pe, GROUPS - 1)

        @block.scalar
        def _(act):
            s_ = nc.scalar

            def keep_zt(g, i):
                j = g * WPG + i
                hold(act, t_done, j + 1)
                if i == 0:
                    hold(act, fin.out_done, g)
                s_.activation(fin.ZT[:, :, i * WIN:(i + 1) * WIN],
                              ps_t[:, 0:P].rearrange("p (b w) -> p b w", b=NB), ACT.Copy).then_inc(zt_ready, 1)

            def finish(g, i):
                if layer == 0 and i == 0:
                    fin.act_relu(act, g, rows_out)
                if layer == 1 and i == 1:
                    fin.act_x(act, g)
                if layer == 1 and i == 5:
                    fin.act_hnT(act, g)
                if layer == 1 and i == 7:
                    fin.act_parts(act, g)

            def group(pair, parity):
                g = pair * 2 + parity
                fin.act_stage(act, g)
                for i in range(WPG):
                    j, s = g * WPG + i, i % 2
                    hold(act, z_done, j + 1)
                    hold(act, t_done, j - 1)
                    s_.activation(Z[s][:, :], ps_z[s][:, 0:P], ACT.Copy).then_inc(z_ready, 1)
                    if builds(parity):
                        if i == 0:
                            hold(act, deg_done, pair)
                            hold(act, a_out, pair * 16)
                        bj = pair * WPG + i
                        hold(act, a_done, bj + 1)
                        s_.activation(A[:, :, i * WIN:(i + 1) * WIN],
                                      ps_a[s][:, 0:AW].rearrange("p (b w) -> p b w", w=WIN), ACT.Copy).then_inc(a_kept, 1)
                    if i:
                        keep_zt(g, i - 1)
                    if not (isinstance(g, int) and g == 0):
                        finish(g - 1, i)
                keep_zt(g, WPG - 1)
                if builds(parity):
                    hold(act, a_kept, (pair + 1) * WPG)
                    act.dma_start(t.A_dram[bass.ds(g, 1), :, :].rearrange("a p n -> (a p) n"),
                                  A[:, :, :].rearrange("p b n -> p (b n)")).then_inc(a_out, 16)
            groups(act, group)
            for i in range(WPG):
                finish(GROUPS - 1, i)
            act.wait_ge(a_out, 16 * (GROUPS // 2 + (1 - layer)))
            if layer == 0:
                act.wait_ge(fin.rows_out, 16 * GROUPS)


SLOTS = 5


def dense_layer(nc, t, layer, out):
    name = f"gcn{layer}"
    last = layer == 1
    with ExitStack() as ctx:
        sb = lambda n, s, d: ctx.enter_context(nc.sbuf_tensor(f"{name}_{n}", s, d))
        sem = lambda n: ctx.enter_context(nc.semaphore(f"{name}_{n}"))
        ps = lambda n: ctx.enter_context(nc.psum_tensor(f"{name}_{n}", [P, 512], F32))
        A = [sb(f"A{s}", [P, SRC_BLOCKS, P], F16) for s in range(SLOTS)]
        z = [sb(f"z{s}", [P, P], F32) for s in range(SLOTS)]
        ps_g = [ps(f"ps_g{s}") for s in range(SLOTS)]
        tail = DenseTail(nc, t, ctx, name, last)
        a_in = [sem(f"a_in{s}") for s in range(SLOTS)]
        agg_done = sem("agg_done")
        chain = sem("chain")
        z_out = [sem(f"z_out{s}") for s in range(SLOTS)]
        block = ctx.enter_context(nc.Block())

        def slots(eng, body):
            rounds = GROUPS // SLOTS
            for s in range(SLOTS):
                body(s, s, 0)
            with eng.Fori(1, rounds - 1) as m:
                for s in range(SLOTS):
                    body(m * SLOTS + s, s, m)
            for s in range(SLOTS):
                body((rounds - 1) * SLOTS + s, s, rounds - 1)

        @block.sync
        def _(sp):
            def load(g, s, m):
                after(sp, agg_done, g - (SLOTS - 1))
                sp.dma_start(A[s][:, :, :].rearrange("p b n -> p (b n)"),
                             t.A_dram[bass.ds(g, 1), :, :].rearrange("a p n -> (a p) n")).then_inc(a_in[s], 16)
            slots(sp, load)

        @block.tensor
        def _(pe):
            def group(g, s, m):
                pe.wait_ge(a_in[s], (m + 1) * 16)
                after(pe, tail.z_ready, g - (SLOTS - 1))
                for b in range(SRC_BLOCKS):
                    ins = nc.tensor.matmul(ps_g[s][:, 0:3 * P], A[s][:, b, :], t.S[layer][:, b, :, :].rearrange("p c n -> p (c n)"),
                                           start=(b == 0), stop=(b == SRC_BLOCKS - 1))
                ins.then_inc(agg_done, 1)
                if not last:
                    tail.pe_turn(pe, g - 1, z[(s - 1) % SLOTS])
                    tail.pe_multiply(pe, g - 2)
            slots(pe, group)
            if not last:
                tail.pe_turn(pe, GROUPS - 1, z[(GROUPS - 1) % SLOTS])
                tail.pe_multiply(pe, GROUPS - 2)
                tail.pe_multiply(pe, GROUPS - 1)

        @block.scalar
        def _(act):
            def group(g, s, m):
                if last:
                    tail.store(act, g, z[s], out, z_out[s])
                else:
                    tail.act(act, g)
            slots(act, group)
            if last:
                for s in range(SLOTS):
                    act.wait_ge(z_out[s], (GROUPS // SLOTS) * 16)

        @block.vector
        def _(dve):
            v = nc.vector

            def group(g, s, m):
                dve.wait_ge(agg_done, g + 1)
                if last:
                    after(dve, z_out[s], m * 16)
                k = Chain(dve, chain, 3 * g if last else 2 * g)
                k.link(v.tensor_reduce(z[s][:, :], ps_g[s][:, 0:3 * P].rearrange("p (c n) -> p n c", c=3), AX.X, ALU.add))
                tail.combine(dve, v, k, g, z[s])
                if not last:
                    tail.dve_split(dve, g - 2)
            slots(dve, group)
            if not last:
                tail.dve_split(dve, GROUPS - 2)
                tail.dve_split(dve, GROUPS - 1)



class DenseTail:

    def __init__(self, nc, t, ctx, name, last):
        self.nc, self.t, self.last = nc, t, last
        sem = lambda n: ctx.enter_context(nc.semaphore(f"{name}_{n}"))
        self.z_ready, self.passed = sem("z_ready"), sem("waits_passed")
        self.layer = 1 if last else 0
        if not last:
            sb = lambda n, s, d: ctx.enter_context(nc.sbuf_tensor(f"{name}_{n}", s, d))
            ps = lambda n: ctx.enter_context(nc.psum_tensor(f"{name}_{n}", [P, 512], F32))
            self.zT, self.hp, self.r = sb("zT", [P, P], F32), sb("hp", [P, P], F32), sb("r", [P, P], F32)
            self.parts = sb("parts", [P, 3, P], BF16)
            self.ps_t, self.ps_o = ps("ps_t"), ps("ps_o")
            self.turned, self.zT_ready, self.w_done = sem("turned"), sem("zT_ready"), sem("w_done")
            self.parts_ready, self.parts_kept, self.chain = sem("parts_ready"), sem("parts_kept"), sem("split_chain")

    def combine(self, dve, v, k, g, z):
        t = self.t
        k.link(v.tensor_tensor(z[:, :], z[:, :], one(t.HP[self.layer], g), ALU.add))
        ins = v.scalar_tensor_tensor(out=z[:, :], in0=z[:, :], scalar=t.dinv[:, bass.ds(g, 1)],
                                     in1=t.bias_all[self.layer][:, :], op0=ALU.mult, op1=ALU.add)
        if self.last:
            k.link(ins)
            v.tensor_tensor(z[:, :], z[:, :], one(t.X, g), ALU.add).then_inc(self.z_ready, 1)
        else:
            ins.then_inc(self.z_ready, 1)

    def pe_turn(self, pe, g, z):
        if isinstance(g, int) and g < 0:
            return
        after(pe, self.zT_ready, g)
        pe.wait_ge(self.z_ready, g + 1)
        self.nc.tensor.transpose(self.ps_t[:, 0:P], z[:, :], self.t.ident[:, :]).then_inc(self.turned, 1)

    def hold(self, act, sem, value):
        if isinstance(value, int) and value <= 0:
            return
        act.wait_ge(sem, value)
        act.sem_inc(self.passed, 1)

    def store(self, act, g, z, out, done):
        rows = LAST_ROWS if isinstance(g, int) and g == GROUPS - 1 else P
        self.hold(act, self.z_ready, g + 1)
        act.dma_start(out[bass.ds(g * P, rows), :], z[0:rows, :]).then_inc(done, 16)

    def act(self, act, g):
        hold = lambda sem, value: self.hold(act, sem, value)
        t, s = self.t, self.nc.scalar
        hold(self.w_done, g)
        hold(self.turned, g + 1)
        s.activation(self.zT[:, :], self.ps_t[:, 0:P], ACT.Relu).then_inc(self.zT_ready, 1)
        hold(self.parts_ready, g + 1)
        s.activation(one(t.HP[1], g), self.hp[:, :], ACT.Copy).then_inc(self.parts_kept, 1)
        out = t.S[1][:, bass.ds(g, 1), :, :].rearrange("p a b c -> p (a b) c")
        s.activation(out, self.parts[:, :, :], ACT.Copy).then_inc(self.parts_kept, 1)

    def pe_multiply(self, pe, g):
        if isinstance(g, int) and g < 0:
            return
        pe.wait_ge(self.zT_ready, g + 1)
        after(pe, self.parts_ready, g)
        self.nc.tensor.matmul(self.ps_o[:, 0:P], self.zT[:, :], self.t.W[3][:, :], start=True, stop=True).then_inc(self.w_done, 1)

    def dve_split(self, dve, g):
        if isinstance(g, int) and g < 0:
            return
        v = self.nc.vector
        after(dve, self.parts_kept, 2 * g)
        dve.wait_ge(self.w_done, g + 1)
        k = Chain(dve, self.chain, 4 * g)
        k.link(v.tensor_scalar(self.hp[:, :], self.ps_o[:, 0:P], self.t.dinv[:, bass.ds(g, 1)], None, ALU.mult))
        split(v, k, self.hp, self.r, self.parts, self.parts_ready)


def any_order_coefficients(nc, io, t):
    with ExitStack() as ctx:
        co = Coefficients(nc, io, t, ctx, "any_coef")
        block = ctx.enter_context(nc.Block())

        def chunks(eng, step):
            for m in range(2):
                step(m, 0, m)
            with eng.Fori(1, ET_CHUNKS // 2 - 1) as pair:
                for s in range(2):
                    step(pair * 2 + s, pair, s)
            for m in range(ET_CHUNKS - 2, ET_CHUNKS):
                step(m, m // 2, m % 2)

        @block.sync
        def _(sp):
            chunks(sp, lambda m, half_m, s: co.load(sp, m, s))

        @block.tensor
        def _(pe):
            chunks(pe, lambda m, half_m, s: co.multiply(pe, m, s))

        @block.vector
        def _(dve):
            def step(m, half_m, s):
                co.make_onehot(dve, m, half_m, s)
                co.scale(dve, m)
            chunks(dve, step)


class AnyOrder:

    def __init__(self, nc, t, ctx, name, rows_in):
        self.nc, self.t, self.rows_in, self.name = nc, t, rows_in, name
        sb = lambda n, s, d: ctx.enter_context(nc.sbuf_tensor(f"{name}_{n}", s, d))
        sem = lambda n: ctx.enter_context(nc.semaphore(f"{name}_{n}"))
        self.idx, self.rows = sb("idx", [P, 1], I32), sb("rows", [P, D], F32)
        self.match = sb("match", [P, P], F32)
        self.idx_ready, self.landed, self.done, self.passed = sem("idx_ready"), sem("landed"), sem("done"), sem("pool_waits_passed")
        self.match_ready, self.factor_ready, self.sum_ready = sem("match_ready"), sem("factor_ready"), sem("sum_ready")
        self.cleared, self.dve_passed = sem("cleared"), sem("dve_waits_passed")

    def gather(self, pool):
        with pool.Fori(0, GROUPS) as g:
            with pool.Fori(0, TILES) as tile:
                n = g * TILES + tile
                pool.wait_ge(self.done, n + 1)
                pool.sem_inc(self.passed, 1)
                self.nc.gpsimd.tensor_copy(self.idx[:, :], self.t.idx[:, bass.ds(tile, 1)]).then_inc(self.idx_ready, 1)
                pool.wait_ge(self.idx_ready, n + 1)
                pool.sem_inc(self.passed, 1)
                self.nc.gpsimd.indirect_dma_start(self.rows[:, :], None, self.rows_in,
                                                  bass.IndirectOffsetOnAxis(ap=self.idx[:, 0:1], axis=0)).then_inc(self.landed, 16)
            pool.wait_ge(self.done, (g + 1) * TILES + 1)
            pool.sem_inc(self.passed, 1)
            pool.inc_swdge_sem([self.landed], [TILES * 16], mode="sub")

    def wait_rows(self, pe, tile, n):
        pe.wait_ge(self.idx_ready, n + 1)
        pe.wait_ge(self.landed, (tile + 1) * 16)

    def one_hot(self, dve, g, tile, n):
        dve.wait_ge(self.done, n + 1)
        self.nc.vector.tensor_scalar(self.match[:, :], self.t.iota128[:, :], self.t.group_lo[:, bass.ds(g, 1)],
                                     self.t.dst[:, bass.ds(tile, 1)], ALU.add, ALU.is_equal).then_inc(self.match_ready, 1)
        dve.wait_ge(self.match_ready, n + 1)


def any_order_relational(nc, t, layer, rows_in, rows_out):
    name = f"any_rel{layer}"
    with ExitStack() as ctx:
        ps = lambda n: ctx.enter_context(nc.psum_tensor(f"{name}_{n}", [P, 512], F32))
        C = ctx.enter_context(nc.sbuf_tensor(f"{name}_C", [P, NB, P], F32))
        fin = Finish(nc, t, ctx, name, layer)
        way = AnyOrder(nc, t, ctx, name, rows_in)
        ps_z = [ps("ps_z0"), ps("ps_z1")]
        ps_d = ps("ps_d")
        block = ctx.enter_context(nc.Block())
        HB = NB // 2

        @block.gpsimd
        def _(pool):
            way.gather(pool)

        @block.tensor
        def _(pe):
            m_ = nc.tensor
            pe.sem_inc(way.done, 1)
            with pe.Fori(0, GROUPS) as g:
                pe.wait_ge(fin.staged, g + 1)
                m_.transpose(fin.ps_h[:, 0:P], fin.h_stage[:, :], t.ident[:, :]).then_inc(fin.turned, 1)
                with pe.Fori(0, TILES) as tile:
                    n = g * TILES + tile
                    way.wait_rows(pe, tile, n)
                    pe.wait_ge(way.factor_ready, n + 1)
                    if layer == 0:
                        m_.matmul(ps_d[:, 0:1], way.match[:, :], t.ones[:, 0:1], start=True, stop=True)
                    for h in range(2):
                        ins = m_.matmul(ps_z[h][:, :], way.rows[:, :], C[:, h * HB:(h + 1) * HB, :].rearrange("p b n -> p (b n)"),
                                        start=True, stop=True)
                    ins.then_inc(way.done, 1)
                pe.wait_ge(way.sum_ready, (g + 1) * TILES)
                fin.pe_out(pe, g)
                if layer == 1:
                    fin.pe_turn_new(pe, g)
                    fin.pe_w1(pe, g)

        @block.scalar
        def _(act):
            with act.Fori(0, GROUPS) as g:
                nc.scalar.activation(fin.h_stage[:, :], one(t.H, g), ACT.Copy).then_inc(fin.staged, 1)
                fin.hold(act, fin.turned, g + 1)
                nc.scalar.activation(fin.hT[:, :], fin.ps_h[:, 0:P], ACT.Copy).then_inc(fin.hT_ready, 1)
                if layer == 0:
                    fin.act_relu(act, g, rows_out)
                else:
                    fin.act_x(act, g)
                    fin.act_hnT(act, g)
                    fin.act_parts(act, g, rows_out)
            act.wait_ge(fin.rows_out, 16 * GROUPS)

        @block.vector
        def _(dve):
            v = nc.vector
            if layer == 0:
                v.memset(t.deg[:, :], 0.0).then_inc(way.cleared, 1)
                dve.wait_ge(way.cleared, 1)
            with dve.Fori(0, GROUPS) as g:
                v.memset(fin.ZT[:, :, :], 0.0).then_inc(way.cleared, 1)
                dve.wait_ge(way.cleared, g + (2 if layer == 0 else 1))
                dve.sem_inc(way.dve_passed, 1)
                with dve.Fori(0, TILES) as tile:
                    n = g * TILES + tile
                    way.one_hot(dve, g, tile, n)
                    shape = [P, NB, P]
                    v.tensor_tensor(C[:, :, :], way.match[:, :].unsqueeze(1).to_broadcast(shape),
                                    t.coef[layer][:, bass.ds(tile, 1), :].rearrange("p a b -> p (a b)").unsqueeze(2).to_broadcast(shape),
                                    ALU.mult).then_inc(way.factor_ready, 1)
                    dve.wait_ge(way.done, n + 2)
                    if layer == 0:
                        d = t.deg[:, bass.ds(g, 1)]
                        v.tensor_tensor(d, d, ps_d[:, 0:1], ALU.add)
                    for h in range(2):
                        z = flat(fin.ZT[:, h * HB:(h + 1) * HB, :])
                        ins = v.tensor_tensor(z, z, ps_z[h][:, :], ALU.add)
                    ins.then_inc(way.sum_ready, 1)
                if layer == 1:
                    fin.dve_x(dve, g)
                    fin.dve_norm(dve, g)
                    fin.dve_parts(dve, g)
                else:
                    dve.wait_ge(fin.out_done, g + 1)


def any_order_gcn(nc, t, layer, rows_in, rows_out, out):
    name = f"any_gcn{layer}"
    last = layer == 1
    with ExitStack() as ctx:
        z = ctx.enter_context(nc.sbuf_tensor(f"{name}_z", [P, P], F32))
        ps_g = ctx.enter_context(nc.psum_tensor(f"{name}_ps_g", [P, 512], F32))
        tail = DenseTail(nc, t, ctx, name, last)
        way = AnyOrder(nc, t, ctx, name, rows_in)
        chain, stored = ctx.enter_context(nc.semaphore(f"{name}_chain")), ctx.enter_context(nc.semaphore(f"{name}_stored"))
        block = ctx.enter_context(nc.Block())

        def groups(eng, body):
            with eng.Fori(0, GROUPS - 1) as g:
                body(g)
            body(GROUPS - 1)

        @block.gpsimd
        def _(pool):
            way.gather(pool)

        @block.tensor
        def _(pe):
            pe.sem_inc(way.done, 1)

            def group(g):
                with pe.Fori(0, TILES) as tile:
                    n = tile + g * TILES
                    way.wait_rows(pe, tile, n)
                    pe.wait_ge(way.match_ready, n + 1)
                    nc.tensor.matmul(ps_g[:, 0:P], way.match[:, :], way.rows[:, :], start=True, stop=True).then_inc(way.done, 1)
                if not last:
                    pe.wait_ge(tail.z_ready, g + 1)
                    nc.tensor.transpose(tail.ps_t[:, 0:P], z[:, :], t.ident[:, :]).then_inc(tail.turned, 1)
                    pe.wait_ge(tail.zT_ready, g + 1)
                    nc.tensor.matmul(tail.ps_o[:, 0:P], tail.zT[:, :], t.W[3][:, :], start=True, stop=True).then_inc(tail.w_done, 1)
            groups(pe, group)

        @block.scalar
        def _(act):
            def group(g):
                if last:
                    tail.store(act, g, z, out, stored)
                else:
                    tail.hold(act, tail.turned, g + 1)
                    nc.scalar.activation(tail.zT[:, :], tail.ps_t[:, 0:P], ACT.Relu).then_inc(tail.zT_ready, 1)
                    tail.hold(act, tail.parts_ready, g + 1)
                    nc.scalar.activation(one(t.HP[1], g), tail.hp[:, :], ACT.Copy).then_inc(tail.parts_kept, 1)
                    tail.hold(act, tail.parts_kept, g + 1)
                    act.dma_start(rows_out[bass.ds(g * P, P), :], one(t.HP[1], g)).then_inc(stored, 16)
            groups(act, group)
            act.wait_ge(stored, 16 * GROUPS)

        @block.vector
        def _(dve):
            v = nc.vector

            def group(g):
                v.memset(z[:, :], 0.0).then_inc(way.cleared, 1)
                dve.wait_ge(way.cleared, g + 1)
                dve.sem_inc(way.dve_passed, 1)
                with dve.Fori(0, TILES) as tile:
                    n = tile + g * TILES
                    way.one_hot(dve, g, tile, n)
                    dve.wait_ge(way.done, n + 2)
                    v.tensor_tensor(z[:, :], z[:, :], ps_g[:, 0:P], ALU.add).then_inc(way.sum_ready, 1)
                    dve.wait_ge(way.sum_ready, n + 1)
                tail.combine(dve, v, Chain(dve, chain, (2 if last else 1) * g), g, z)
                if last:
                    dve.wait_ge(stored, (g + 1) * 16)
                else:
                    dve.wait_ge(tail.w_done, g + 1)
                    v.tensor_scalar(tail.hp[:, :], tail.ps_o[:, 0:P], t.dinv[:, bass.ds(g, 1)], None, ALU.mult)\
                     .then_inc(tail.parts_ready, 1)
                    dve.wait_ge(tail.parts_kept, g + 1)
            groups(dve, group)


class Tensors:
    pass


def program(nc, io, out, force_slow=False):
    t = Tensors()
    with ExitStack() as ctx:
        sb = lambda n, s, d: ctx.enter_context(nc.sbuf_tensor(n, s, d))
        dram = lambda n, s, d: nc.dram_tensor(n, s, d, kind="Internal").ap()
        t.h1_dram, t.h2_dram = dram("h1_rows", (GROUPS * P, D), F32), dram("h2_rows", (GROUPS * P, D), F32)
        t.A_dram = dram("A_slabs", (GROUPS, P, SRC_BLOCKS * P), F16)
        t.X, t.H = sb("X", [P, GROUPS, D], F32), sb("H", [P, GROUPS, D], F32)
        t.V = [sb(f"V{i}", [P, NB, D], F32) for i in range(2)]
        t.W = [sb(f"W{i}", [P, D], F32) for i in range(4)]
        t.bias_row = [sb(f"bias_row{i}", [1, D], F32) for i in range(2)]
        t.bias_all = [sb(f"bias_all{i}", [P, D], F32) for i in range(2)]
        t.ident, t.ones, t.ones16 = sb("ident", [P, P], F32), sb("ones", [P, P], F32), sb("ones16", [P, 2], F16)
        t.idx = sb("idx_table", [P, TILES], I32)
        t.dst, t.norm = sb("dst_table", [P, TILES], F32), sb("norm_table", [P, TILES], F32)
        t.src_lo, t.key = sb("src_lo_table", [P, TILES], F32), sb("key_table", [P, TILES], F32)
        t.comp = sb("comp_parts", [RH, 3, 2, 2 * NB], BF16)
        t.neg_win, t.win512 = sb("neg_win", [P, WINDOWS], F32), sb("win512", [P, WINDOWS], F32)
        t.group_lo = sb("group_lo", [P, GROUPS], F32)
        t.iota16, t.iota400, t.iota128 = sb("iota16", [P, WIN], F32), sb("iota400", [P, AW], F16), sb("iota128", [P, P], F16)
        t.type_id = sb("type_id", [P, 2], F32)
        t.pos, t.first, t.slow = sb("pos", [1, WINDOWS, 8], I32), sb("first", [1, WINDOWS], I32), sb("slow", [1, 1], I32)
        t.deg, t.dinv = sb("deg", [P, GROUPS], F32), sb("dinv", [P, GROUPS], F32)

        prepare(nc, io, t)
        slow = nc.values_load(t.slow[0:1, 0:1], min_val=0, max_val=1)
        hp_rows = [dram(f"hp_rows{i}", (GROUPS * P, D), F32) for i in range(2)]
        right = lambda c, n, s, d: c.enter_context(nc.sbuf_tensor(n, s, d, side="right"))
        left = lambda c, n, s, d: c.enter_context(nc.sbuf_tensor(n, s, d))
        t.HP, t.S = [None, None], [None, None]
        with nc.If(slow == 0):
            with ExitStack() as parts:
                with ExitStack() as edges:
                    t.coef = [left(edges, f"coef{i}", [P, TILES, NB], F32) for i in range(2)]
                    t.ring = left(edges, "ring", [P, RING, D], F32)
                    relational_layer(nc, io, t, 0, t.h1_dram, t.h2_dram)
                    t.HP[0] = t.H
                    t.S[0] = right(parts, "hp0_parts", [P, GROUPS, 3, D], BF16)
                    relational_layer(nc, io, t, 1, t.h2_dram, None)
                t.HP[1] = right(parts, "hp1", [P, GROUPS, D], F32)
                t.S[1] = right(parts, "hp1_parts", [P, GROUPS, 3, D], BF16)
                dense_layer(nc, t, 0, out)
                dense_layer(nc, t, 1, out)
        with nc.Else():
            with ExitStack() as parts:
                t.coef = [left(parts, f"any_coef{i}", [P, TILES, NB], F32) for i in range(2)]
                t.HP = [left(parts, f"any_hp{i}", [P, GROUPS, D], F32) for i in range(2)]
                t.S = [left(parts, "any_parts", [P, GROUPS, 3, D], BF16), None]
                any_order_coefficients(nc, io, t)
                any_order_relational(nc, t, 0, t.h1_dram, t.h2_dram)
                any_order_relational(nc, t, 1, t.h2_dram, hp_rows[0])
                any_order_gcn(nc, t, 0, hp_rows[0], hp_rows[1], out)
                any_order_gcn(nc, t, 1, hp_rows[1], None, out)


_INS = ["x", "src", "dst", "edge_type_200", "edge_weight1", "L0_gnn_V1", "L0_gnn_comp1", "L0_gnn_loop1", "L0_gnn_bias1",
        "L0_gnn_V2", "L0_gnn_comp2", "L0_gnn_loop2", "L0_gnn_bias2", "L1_gnn_W1", "L1_gnn_b1", "L1_gnn_W2", "L1_gnn_b2"]


def kernel(**inputs):
    import numpy as _np
    import concourse.bacc as _bacc
    from concourse import mybir as _mybir
    from concourse.bass_utils import run_bass_kernel_spmd as _run

    nc = _bacc.Bacc("TRN2", target_bir_lowering=False, num_devices=1)
    arrays, io = {}, {}
    for name in _INS:
        a = _np.ascontiguousarray(inputs[name])
        arrays[f"in_{name}_dram"] = a
        io[name] = nc.dram_tensor(f"in_{name}_dram", a.shape, _mybir.dt.from_np(a.dtype), kind="ExternalInput").ap()
    out = nc.dram_tensor("out_0_dram", (N, D), _mybir.dt.float32, kind="ExternalOutput").ap()
    program(nc, io, out)
    r = _run(nc, [arrays], core_ids=[0])
    return r.results[0]["out_0_dram"]
```

```python
from contextlib import ExitStack

import concourse.bass as bass
from concourse import mybir

ALU = mybir.AluOpType
ACT = mybir.ActivationFunctionType
AX = mybir.AxisListType
F32, F16, BF16, I32 = mybir.dt.float32, mybir.dt.float16, mybir.dt.bfloat16, mybir.dt.int32

P = 128
N, D, E, R, NB = 3125, 128, 100000, 200, 8
GROUPS = -(-N // P)
LAST_ROWS = N - (GROUPS - 1) * P
TILES = 784
GATHERED = -(-E // P)
RAW = 7
WIN = 16
WPG = P // WIN
WINDOWS = GROUPS * WPG
XG = 5
LATE = 18
EARLY_BLOCKS = LATE - 1
EARLY_SLABS = 24
EARLY_PER_GROUP = 4
SLOTS = 5
FIRST_SLOTS = 3
CARRIED_SLABS, CARRIED_BLOCKS = 2, 20
PARTS_BIAS = SLOTS - 2
FIRST_TILES = 16
LAST_WINDOWS = -(-LAST_ROWS // WIN)
SPAN = 6
CHUNK = 8
SLOTS_RING = 8
RING = SLOTS_RING * CHUNK
CHUNKS = TILES // CHUNK
WPC = 2
SRC_BLOCKS = GROUPS
AW = SRC_BLOCKS * WIN
ET = 8
ET_CHUNKS = TILES // ET
RH = R // 2
PAD_DST = 4000
EPS = 1e-5


def after(eng, sem, value):
    if isinstance(value, int) and value <= 0:
        return
    eng.wait_ge(sem, value)


def begun_early(g):
    return not isinstance(g, int) or g < EARLY_SLABS


def is_group(g, number):
    return isinstance(g, int) and g == number


class Chain:

    def __init__(self, eng, sem, base=0):
        self.eng, self.sem, self.at, self.count = eng, sem, base, 0

    def link(self, ins):
        self.at, self.count = self.at + 1, self.count + 1
        ins.then_inc(self.sem, 1)
        self.eng.wait_ge(self.sem, self.at)


def semaphore(nc, t, ctx, name):
    if t.second_branch and t.numbers:
        return ctx.enter_context(nc.semaphore(name, num=t.numbers.pop()))
    made = ctx.enter_context(nc.semaphore(name))
    if t.first_branch:
        t.numbers.append(made.num)
    return made


def flat(ap):
    return ap.rearrange("p a b -> p (a b)")


def one(ap, g):
    if isinstance(g, int):
        return ap[:, g, :]
    return ap[:, bass.ds(g, 1), :].rearrange("p a b -> p (a b)")


def prepare(nc, io, t):
    x, src, dst, norm = io["x"], io["src"], io["dst"], io["edge_weight1"]
    with ExitStack() as ctx:
        sb = lambda n, s, d: ctx.enter_context(nc.sbuf_tensor("pre_" + n, s, d))
        sem = lambda n: ctx.enter_context(nc.semaphore("pre_" + n))
        raw_src, raw_dst = sb("raw_src", [P, RAW, P], I32), sb("raw_dst", [P, RAW, P], I32)
        raw_norm = sb("raw_norm", [P, RAW, P], F32)
        src_f, dst_f = sb("src_f", [P, RAW, P], F32), sb("dst_f", [P, RAW, P], F32)
        stats, mv = sb("stats", [P, GROUPS, 6], F32), sb("mv", [P, GROUPS, 2], F32)
        rstd, shift = sb("rstd", [P, GROUPS], F32), sb("shift", [P, GROUPS], F32)
        t_max, t_min = sb("t_max", [P, RAW], F32), sb("t_min", [P, RAW], F32)
        tile_lo, tile_hi = sb("tile_lo", [P, P], BF16), sb("tile_hi", [P, RAW, P], BF16)
        win_lo, ring_lo = sb("win_lo", [P, WINDOWS], F32), sb("ring_lo", [P, WINDOWS], F32)
        kk = sb("kk", [P, SPAN], F32)
        before, begun = sb("before", [P, RAW, WINDOWS], BF16), sb("begun", [P, RAW, WINDOWS], BF16)
        first, count = sb("first", [P, WINDOWS], F32), sb("count", [P, WINDOWS], F32)
        r1, r2, wrong = sb("r1", [P, WINDOWS], F32), sb("r2", [P, WINDOWS], F32), sb("wrong", [P, WINDOWS], F32)
        bad, pos_f = sb("bad", [P, 1], F32), sb("pos_f", [P, WINDOWS, SPAN], F32)
        ones_bf = sb("ones_bf", [P, P], BF16)
        ia, fa = sb("ia", [P, TILES], I32), sb("fa", [P, TILES], F32)
        comp = sb("comp", [RH, 2, 2 * NB], F32)
        rest = sb("rest", [RH, 2, 2 * NB], F32)

        ps = lambda n: ctx.enter_context(nc.psum_tensor("pre_" + n, [P, 512], F32))
        ps_src, ps_dst, ps_norm = [ps("s0"), ps("s1")], [ps("d0"), ps("d1")], [ps("n0"), ps("n1")]
        ps_before, ps_begun = ps("ps_before"), ps("ps_begun")

        pads_set, consts_set = sem("pads_set"), sem("consts_set")
        x_in = [sem(f"x_in{c}") for c in range(GROUPS // XG)]
        src_in, dst_in, norm_in = sem("src_in"), sem("dst_in"), sem("norm_in")
        w_in, comp_in = sem("w_in"), sem("comp_in")
        ve, scale_ready = sem("vector_chain"), sem("scale_ready")
        var_ready, sd_ready, h_ready, h_out = sem("var_ready"), sem("sd_ready"), sem("h_ready"), sem("h_out")
        srcf_ready, dstf_ready, src_t, dst_t, norm_t = (sem(n) for n in ("srcf", "dstf", "src_t", "dst_t", "norm_t"))
        before_ready, begun_ready, before_done, begun_done = (sem(n) for n in ("before", "begun", "before_done", "begun_done"))
        full = (RAW - 1) * P * P
        rows = (E - full) // P
        tail = E - full - rows * P

        idx_table_ready, columns_kept = sem("idx_table_ready"), sem("columns_kept")
        block = ctx.enter_context(nc.Block())

        def edge_loads(eng, raw, flat_dram, done):
            eng.dma_start(raw[:, 0:RAW - 1, :], flat_dram[0:full].rearrange("(c q e) -> q c e", q=P, e=P)).then_inc(done, 16)
            eng.dma_start(raw[0:rows, RAW - 1, :], flat_dram[full:full + rows * P].rearrange("(q e) -> q e", e=P)).then_inc(done, 16)
            eng.dma_start(raw[rows:rows + 1, RAW - 1, 0:tail], flat_dram[full + rows * P:E].rearrange("(q e) -> q e", q=1)).then_inc(done, 16)

        @block.sync
        def _(sp):
            for c in range(GROUPS // XG):
                g0, g1 = c * XG, min(c * XG + XG, GROUPS - 1)
                sp.dma_start(t.X[:, g0:g1, :], x[g0 * P:g1 * P, :].rearrange("(g p) d -> p g d", p=P)).then_inc(x_in[c], 16)
            sp.wait_ge(pads_set, 4)
            sp.dma_start(t.X[0:LAST_ROWS, GROUPS - 1, :], x[(GROUPS - 1) * P:N, :]).then_inc(x_in[-1], 16)
            edge_loads(sp, raw_dst, dst, dst_in)
            h_rows = t.h1_dram.rearrange("(g p) d -> p g d", p=P)
            for c in range(GROUPS // XG):
                sp.wait_ge(h_ready, c + 1)
                sp.dma_start(h_rows[:, c * XG:(c + 1) * XG, :], t.H[:, c * XG:(c + 1) * XG, :]).then_inc(h_out, 16)
            edge_loads(sp, raw_norm, norm.rearrange("e a -> (e a)"), norm_in)
            for l, name in enumerate(("L0_gnn_comp1", "L0_gnn_comp2")):
                for h in range(2):
                    sp.dma_start(comp[:, h, l * NB:(l + 1) * NB], io[name][h * RH:(h + 1) * RH, :]).then_inc(comp_in, 16)
            for i, name in enumerate(("L0_gnn_V1", "L0_gnn_V2")):
                sp.dma_start(t.V[i][:, :, :], io[name].rearrange("b d o -> d b o")).then_inc(w_in, 16)
            for i, name in enumerate(("L0_gnn_loop1", "L0_gnn_loop2", "L1_gnn_W1", "L1_gnn_W2")):
                sp.dma_start(t.W[i][:, :], io[name]).then_inc(w_in, 16)
            for i, name in enumerate(("L0_gnn_bias1", "L0_gnn_bias2")):
                sp.dma_start(t.bias_row[i][:, :], io[name].rearrange("(a n) -> a n", a=1)).then_inc(w_in, 16)
            for i, name in enumerate(("L1_gnn_b1", "L1_gnn_b2")):
                sp.dma_start(t.bias_all[i][:, :], io[name].rearrange("(a n) -> a n", a=1).to_broadcast([P, D])).then_inc(w_in, 16)
            sp.wait_ge(w_in, 10 * 16)
            sp.wait_ge(h_out, GROUPS // XG * 16)

        @block.scalar
        def _(act):
            act.wait_ge(pads_set, 4)
            edge_loads(act, raw_src, src, src_in)

            def relu(c):
                act.wait_ge(scale_ready, c + 1)
                for g in range(c * XG, (c + 1) * XG):
                    ins = nc.scalar.activation(t.H[:, g, :], t.X[:, g, :], ACT.Relu, bias=shift[:, g:g + 1],
                                               scale=rstd[:, g:g + 1])
                ins.then_inc(h_ready, 1)

            for c in range(GROUPS // XG):
                act.wait_ge(var_ready, c + 1)
                cols = rstd[:, c * XG:(c + 1) * XG]
                nc.scalar.activation(cols, cols, ACT.Sqrt).then_inc(sd_ready, 1)
                if c:
                    relu(c - 1)
            relu(GROUPS // XG - 1)
            for out, pair, done in ((t.dst, ps_dst, dst_t), (t.norm, ps_norm, norm_t)):
                act.wait_ge(done, 1)
                nc.scalar.activation(out[:, 0:4 * P], pair[0][:, :], ACT.Copy).then_inc(columns_kept, 1)
                nc.scalar.activation(out[:, 4 * P:TILES], pair[1][:, 0:TILES - 4 * P], ACT.Copy).then_inc(columns_kept, 1)

        @block.gpsimd
        def _(pool):
            g = nc.gpsimd
            g.memset(t.X[:, GROUPS - 1, :], 0.0).then_inc(pads_set, 1)
            g.memset(raw_src[:, RAW - 1, :], 0).then_inc(pads_set, 1)
            g.memset(raw_dst[:, RAW - 1, :], PAD_DST).then_inc(pads_set, 1)
            g.memset(raw_norm[:, RAW - 1, :], 0.0).then_inc(pads_set, 1)
            g.memset(t.ident[:, :], 0.0).then_inc(consts_set, 1)
            g.memset(t.ones[:, :], 1.0).then_inc(consts_set, 1)
            g.memset(ones_bf[:, :], 1.0).then_inc(consts_set, 1)
            g.memset(t.ones16[:, :], 1.0).then_inc(consts_set, 1)
            pool.wait_ge(consts_set, 4)
            g.affine_select(out=t.ident[:, :], in_=t.ident[:, :], compare_op=ALU.not_equal, fill=1.0, base=0,
                            pattern=[[-1, P]], channel_multiplier=1).then_inc(consts_set, 1)
            io_ = lambda out, pattern, base=0, cm=0: g.iota(out, pattern=pattern, base=base, channel_multiplier=cm,
                                                           allow_small_or_imprecise_dtypes=True).then_inc(consts_set, 1)
            io_(win_lo[:, :], [[WIN, WINDOWS]])
            io_(tile_lo[:, :], [[0, P]], cm=1)
            io_(tile_hi[:, :, :], [[P, RAW], [0, P]])
            io_(ring_lo[:, :], [[CHUNK, WINDOWS // WPC], [0, WPC]], base=-CHUNK)
            io_(kk[:, :], [[1, SPAN]])
            io_(t.neg_win[:, :], [[-WIN, WINDOWS]])
            io_(t.win512[:, :], [[512, WINDOWS]])
            io_(t.iota16[:, :], [[1, WIN]])
            io_(t.keys400[:, :], [[1, SRC_BLOCKS], [32, WIN]])
            io_(t.iota128[:, :], [[1, P]])
            io_(t.type_id[:, :], [[RH, 2]], cm=1)
            io_(t.group_lo[:, :], [[P, GROUPS]])
            pool.wait_ge(dst_in, 48)
            g.tensor_copy(dst_f[:, :, :], raw_dst[:, :, :]).then_inc(dstf_ready, 1)
            pool.wait_ge(src_in, 48)
            g.tensor_copy(src_f[:, :, :], raw_src[:, :, :]).then_inc(srcf_ready, 1)
            pool.wait_ge(h_out, GROUPS // XG * 16)
            pool.wait_ge(idx_table_ready, 1)
            for i in range(FIRST_TILES):
                g.indirect_dma_start(t.ring[:, i, :], None, t.h1_dram,
                                     bass.IndirectOffsetOnAxis(ap=t.idx[:, i:i + 1], axis=0)).then_inc(t.first_in[i // CHUNK % 2], 16)

        @block.tensor
        def _(pe):
            m = nc.tensor
            def turn(blocks, ps_pair, done):
                for c in range(RAW):
                    ins = m.transpose(ps_pair[c // 4][:, c % 4 * P:(c % 4 + 1) * P], blocks[:, c, :], t.ident[:, :])
                ins.then_inc(done, 1)

            pe.wait_ge(srcf_ready, 1)
            turn(src_f, ps_src, src_t)
            pe.wait_ge(dstf_ready, 1)
            turn(dst_f, ps_dst, dst_t)
            pe.wait_ge(norm_in, 48)
            turn(raw_norm, ps_norm, norm_t)
            for chosen, ready, out, done in ((before, before_ready, ps_before, before_done), (begun, begun_ready, ps_begun, begun_done)):
                pe.wait_ge(ready, 1)
                for c in range(RAW):
                    m.matmul(out[:, 0:WINDOWS], ones_bf[:, :], chosen[:, c, :], start=(c == 0), stop=(c == RAW - 1))
                for c in range(RAW):
                    m.matmul(out[:, 256:256 + WINDOWS], tile_lo[:, :], chosen[:, c, :], start=(c == 0), stop=False)
                    ins = m.matmul(out[:, 256:256 + WINDOWS], tile_hi[:, c, :], chosen[:, c, :], start=False, stop=(c == RAW - 1))
                ins.then_inc(done, 1)

        @block.vector
        def _(dve):
            v = nc.vector
            k = Chain(dve, ve)

            def finish_scale(c):
                cols = slice(c * XG, (c + 1) * XG)
                dve.wait_ge(sd_ready, c + 1)
                k.link(v.reciprocal(rstd[:, cols], rstd[:, cols]))
                v.scalar_tensor_tensor(out=shift[:, cols], in0=mv[:, cols, 0], scalar=-1.0, in1=rstd[:, cols],
                                       op0=ALU.mult, op1=ALU.mult).then_inc(scale_ready, 1)

            for c in range(GROUPS // XG):
                groups = range(c * XG, (c + 1) * XG)
                dve.wait_ge(x_in[c], 32 if c == GROUPS // XG - 1 else 16)
                for g in groups:
                    ins = v.bn_stats(stats[:, g, :], t.X[:, g, :])
                k.link(ins)
                for g in groups:
                    ins = v.bn_aggr(mv[:, g, :], stats[:, g, :])
                k.link(ins)
                v.tensor_scalar(rstd[:, c * XG:(c + 1) * XG], mv[:, c * XG:(c + 1) * XG, 1], EPS, None, ALU.add).then_inc(var_ready, 1)
                if c:
                    finish_scale(c - 1)
            finish_scale(GROUPS // XG - 1)
            dve.wait_ge(src_t, 1)
            v.tensor_copy(t.idx[:, 0:4 * P], ps_src[0][:, :])
            v.tensor_copy(t.idx[:, 4 * P:TILES], ps_src[1][:, 0:TILES - 4 * P]).then_inc(idx_table_ready, 1)
            dve.wait_ge(dstf_ready, 1)
            v.tensor_reduce(t_max[:, :], dst_f[:, :, :], AX.X, ALU.max)
            k.link(v.tensor_reduce(t_min[:, :], dst_f[:, :, :], AX.X, ALU.min))
            dve.wait_ge(consts_set, 17)
            wide = [P, RAW, WINDOWS]
            v.tensor_tensor(before[:, :, :], t_max[:, :].unsqueeze(2).to_broadcast(wide),
                            win_lo[:, :].unsqueeze(1).to_broadcast(wide), ALU.is_lt).then_inc(before_ready, 1)
            v.scalar_tensor_tensor(out=begun[:, :, :], in0=win_lo[:, :].unsqueeze(1).to_broadcast(wide), scalar=float(WIN),
                                   in1=t_min[:, :].unsqueeze(2).to_broadcast(wide), op0=ALU.add, op1=ALU.is_gt).then_inc(begun_ready, 1)
            dve.wait_ge(idx_table_ready, 1)
            k.link(v.tensor_single_scalar(ia[:, :], t.idx[:, :], 7, ALU.logical_shift_right))
            k.link(v.tensor_copy(fa[:, :], ia[:, :]))
            dve.wait_ge(columns_kept, 2)
            v.scalar_tensor_tensor(out=t.key[:, :], in0=t.dst[:, :], scalar=32.0, in1=fa[:, :], op0=ALU.mult, op1=ALU.add)
            k.link(v.tensor_single_scalar(ia[:, :], t.idx[:, :], P - 1, ALU.bitwise_and))
            k.link(v.tensor_copy(t.src_lo[:, :], ia[:, :]))
            dve.wait_ge(before_done, 1)
            k.link(v.tensor_scalar(first[:, :], ps_before[:, 0:WINDOWS], float(TILES - SPAN), None, ALU.min))
            k.link(v.tensor_tensor(pos_f[0:1, :, :], first[0:1, :].unsqueeze(2).to_broadcast([1, WINDOWS, SPAN]),
                                   kk[0:1, :].unsqueeze(1).to_broadcast([1, WINDOWS, SPAN]), ALU.add))
            k.link(v.tensor_copy(t.pos[:, :, :], pos_f[0:1, :, :]))
            k.link(v.tensor_single_scalar(t.pos[:, :, :], t.pos[:, :, :], RING - 1, ALU.bitwise_and))
            k.link(v.tensor_copy(t.first[:, :], first[0:1, :]))
            for which, out, done in ((0, ps_before, before_done), (1, ps_begun, begun_done)):
                dve.wait_ge(done, 1)
                k.link(v.tensor_copy(count[:, :], out[:, 0:WINDOWS]))
                k.link(v.scalar_tensor_tensor(out=r1[:, :], in0=count[:, :], scalar=-1.0, in1=count[:, :], op0=ALU.add, op1=ALU.mult))
                mismatch = wrong if which == 0 else r1
                k.link(v.scalar_tensor_tensor(out=mismatch[:, :], in0=out[:, 256:256 + WINDOWS], scalar=2.0, in1=r1[:, :],
                                              op0=ALU.mult, op1=ALU.not_equal))
            k.link(v.tensor_tensor(wrong[:, :], wrong[:, :], r1[:, :], ALU.add))
            k.link(v.scalar_tensor_tensor(out=r1[:, :], in0=first[:, :], scalar=float(SPAN), in1=count[:, :],
                                          op0=ALU.add, op1=ALU.is_lt))
            k.link(v.tensor_tensor(wrong[:, :], wrong[:, :], r1[:, :], ALU.add))
            used = slice(0, (GROUPS - 1) * WPG + LAST_WINDOWS)
            k.link(v.tensor_tensor(r1[:, used], first[:, used], ring_lo[:, used], ALU.is_lt))
            k.link(v.scalar_tensor_tensor(out=r2[:, used], in0=first[:, used], scalar=float(SPAN - 3 * CHUNK), in1=ring_lo[:, used],
                                          op0=ALU.add, op1=ALU.is_gt))
            k.link(v.tensor_tensor(r1[:, used], r1[:, used], r2[:, used], ALU.add))
            k.link(v.tensor_tensor(wrong[:, used], wrong[:, used], r1[:, used], ALU.add))
            k.link(v.tensor_reduce(bad[:, :], wrong[:, :], AX.X, ALU.add))
            k.link(v.tensor_scalar(t.slow[:, :], bad[0:1, 0:1], 0.0, None, ALU.is_gt))
            dve.wait_ge(comp_in, 64)
            k.link(v.tensor_copy(t.comp[:, 0, :, :], comp[:, :, :]))
            k.link(v.tensor_tensor(rest[:, :, :], comp[:, :, :], t.comp[:, 0, :, :], ALU.subtract))
            k.link(v.tensor_copy(t.comp[:, 1, :, :], rest[:, :, :]))
            k.link(v.tensor_tensor(rest[:, :, :], rest[:, :, :], t.comp[:, 1, :, :], ALU.subtract))
            k.link(v.tensor_copy(t.comp[:, 2, :, :], rest[:, :, :]))


class Coefficients:

    def __init__(self, nc, io, t, ctx, name):
        self.nc, self.io, self.t = nc, io, t
        sem = lambda n: semaphore(nc, t, ctx, f"{name}_{n}")
        self.etype = ctx.enter_context(nc.sbuf_tensor(f"{name}_types", [RH, 4, ET * P], I32))
        self.onehot = ctx.enter_context(nc.sbuf_tensor(f"{name}_onehot", [RH, 2, 2, ET * P], BF16))
        self.ps = ctx.enter_context(nc.psum_tensor(f"{name}_ps", [P, 512], F32))
        self.etype_in = [sem(f"types_in{s}") for s in range(4)]
        self.onehot_ready, self.product_done, self.coef_ready = sem("onehot_ready"), sem("product_done"), sem("coef_ready")

    def load(self, eng, m, s):
        after(eng, self.onehot_ready, m - 3)
        count = ET * P if not isinstance(m, int) else min(ET * P, E - m * ET * P)
        rows = self.io["edge_type_200"].rearrange("(a n) -> a n", a=1)
        eng.dma_start(self.etype[:, s, 0:count], rows[:, bass.ds(m * ET * P, count)].to_broadcast([RH, count]))\
           .then_inc(self.etype_in[s], 16)

    def make_onehot(self, eng, m, quarter_m, s):
        after(eng, self.product_done, m - 1)
        eng.wait_ge(self.etype_in[s], (quarter_m + 1) * 16)
        for h in range(2):
            ins = self.nc.vector.tensor_scalar(self.onehot[:, s % 2, h, :], self.etype[:, s, :], self.t.type_id[0:RH, h:h + 1],
                                               None, ALU.is_equal)
        ins.then_inc(self.onehot_ready, 1)

    def multiply(self, eng, m, s):
        after(eng, self.coef_ready, m)
        eng.wait_ge(self.onehot_ready, m + 1)
        for e in range(ET):
            for h in range(2):
                for part in range(3):
                    ins = self.nc.tensor.matmul(self.ps[:, e * 2 * NB:(e + 1) * 2 * NB], self.onehot[:, s, h, e * P:(e + 1) * P],
                                                self.t.comp[:, part, h, :], start=(h == 0 and part == 0),
                                                stop=(h == 1 and part == 2))
        ins.then_inc(self.product_done, 1)

    def scale(self, eng, m):
        eng.wait_ge(self.product_done, m + 1)
        for l in range(2):
            ins = self.nc.vector.tensor_tensor(self.t.coef[l][:, bass.ds(m * ET, ET), :],
                                               self.ps[:, 0:ET * 2 * NB].rearrange("p (e l b) -> p l e b", l=2, b=NB)[:, l, :, :],
                                               self.t.norm[:, bass.ds(m * ET, ET)].unsqueeze(2).to_broadcast([P, ET, NB]), ALU.mult)
        ins.then_inc(self.coef_ready, 1)


class Finish:

    def __init__(self, nc, t, ctx, name, layer):
        self.nc, self.t, self.layer = nc, t, layer
        sb = lambda n, s, d: ctx.enter_context(nc.sbuf_tensor(f"{name}_{n}", s, d))
        sem = lambda n: semaphore(nc, t, ctx, f"{name}_{n}")
        self.sem_passed = sem("passed")
        self.ZT = sb("ZT", [P, NB, P], F32)
        self.h_stage, self.hT = sb("h_stage", [P, P], F32), sb("hT", [P, P], F32)
        self.ps_h = ctx.enter_context(nc.psum_tensor(f"{name}_ps_h", [P, 512], F32))
        self.ps_o = ctx.enter_context(nc.psum_tensor(f"{name}_ps_o", [P, 512], F32))
        self.staged, self.turned, self.hT_ready = sem("staged"), sem("turned"), sem("hT_ready")
        self.out_done, self.h_new, self.rows_out = sem("out_done"), sem("h_new"), sem("rows_out")
        if layer == 1:
            self.xs, self.hn, self.r = sb("xs", [P, P], F32), sb("hn", [P, P], F32), sb("r", [P, P], F32)
            self.hp, self.parts, self.hnT = sb("hp", [P, P], F32), sb("parts", [P, 3, P], BF16), sb("hnT", [P, P], F32)
            self.stats, self.mv, self.roots = sb("stats", [P, 6], F32), sb("mv", [P, 2], F32), sb("roots", [P, 2], F32)
            self.xs_ready, self.xs_kept, self.var_ready, self.sd_ready = sem("xs_ready"), sem("xs_kept"), sem("var_ready"), sem("sd_ready")
            self.hn_ready, self.hn_turned, self.hnT_ready = sem("hn_ready"), sem("hn_turned"), sem("hnT_ready")
            self.w1_done, self.parts_ready, self.parts_kept = sem("w1_done"), sem("parts_ready"), sem("parts_kept")
            self.chain = sem("chain")

    def hold(self, act, sem, value):
        if isinstance(value, int) and value <= 0:
            return
        act.wait_ge(sem, value)
        act.sem_inc(self.sem_passed, 1)

    def act_stage(self, act, g):
        self.hold(act, self.turned, g)
        self.nc.scalar.activation(self.h_stage[:, :], one(self.t.H, g), ACT.Copy).then_inc(self.staged, 1)
        self.hold(act, self.out_done, g)
        self.hold(act, self.turned, g + 1)
        self.nc.scalar.activation(self.hT[:, :], self.ps_h[:, 0:P], ACT.Copy).then_inc(self.hT_ready, 1)

    def pe_turn(self, pe, g):
        after(pe, self.hT_ready, g)
        pe.wait_ge(self.staged, g + 1)
        self.nc.tensor.transpose(self.ps_h[:, 0:P], self.h_stage[:, :], self.t.ident[:, :]).then_inc(self.turned, 1)

    def pe_out(self, pe, g):
        t, m = self.t, self.nc.tensor
        after(pe, self.h_new if self.layer == 0 else self.parts_ready, g)
        pe.wait_ge(self.hT_ready, g + 1)
        for b in range(NB):
            m.matmul(self.ps_o[:, 0:P], self.ZT[:, b, :], t.V[self.layer][:, b, :], start=(b == 0), stop=False)
        m.matmul(self.ps_o[:, 0:P], self.hT[:, :], t.W[self.layer][:, :], start=False, stop=False)
        m.matmul(self.ps_o[:, 0:P], t.ones[0:1, :], t.bias_row[self.layer][:, :], start=False, stop=True)\
         .then_inc(self.out_done, 1)

    def pe_turn_new(self, pe, g):
        pe.wait_ge(self.hn_ready, g + 1)
        self.nc.tensor.transpose(self.ps_h[:, P:2 * P], self.hn[:, :], self.t.ident[:, :]).then_inc(self.hn_turned, 1)

    def pe_w1(self, pe, g):
        pe.wait_ge(self.hnT_ready, g + 1)
        self.nc.tensor.matmul(self.ps_o[:, P:2 * P], self.hnT[:, :], self.t.W[2][:, :], start=True, stop=True).then_inc(self.w1_done, 1)

    def act_relu(self, act, g, rows_dram):
        self.hold(act, self.out_done, g + 1)
        self.nc.scalar.activation(one(self.t.H, g), self.ps_o[:, 0:P], ACT.Relu).then_inc(self.h_new, 1)
        self.hold(act, self.h_new, g + 1)
        act.dma_start(rows_dram[bass.ds(g * P, P), :], one(self.t.H, g)).then_inc(self.rows_out, 16)

    def act_x(self, act, g):
        self.hold(act, self.xs_ready, g + 1)
        self.nc.scalar.activation(one(self.t.X, g), self.xs[:, :], ACT.Copy).then_inc(self.xs_kept, 1)
        self.hold(act, self.var_ready, g + 1)
        self.nc.scalar.activation(self.roots[:, :], self.roots[:, :], ACT.Sqrt).then_inc(self.sd_ready, 1)

    def act_hnT(self, act, g):
        self.hold(act, self.w1_done, g)
        self.hold(act, self.hn_turned, g + 1)
        self.nc.scalar.activation(self.hnT[:, :], self.ps_h[:, P:2 * P], ACT.Copy).then_inc(self.hnT_ready, 1)

    def act_parts(self, act, g, rows_dram=None):
        t, s = self.t, self.nc.scalar
        self.hold(act, self.parts_ready, g + 1)
        s.activation(one(t.HP[0], g), self.hp[:, :], ACT.Copy).then_inc(self.parts_kept, 1)
        out = t.S[0][:, bass.ds(g, 1), :, :].rearrange("p a b c -> p (a b) c")
        s.activation(out, self.parts[:, :, :], ACT.Copy).then_inc(self.parts_kept, 1)
        if rows_dram is not None:
            self.hold(act, self.parts_kept, 2 * (g + 1))
            act.dma_start(rows_dram[bass.ds(g * P, P), :], one(t.HP[0], g)).then_inc(self.rows_out, 16)

    def dve_x(self, dve, g):
        t, v = self.t, self.nc.vector
        self.k = Chain(dve, self.chain, 8 * g)
        after(dve, self.xs_kept, g)
        dve.wait_ge(self.out_done, g + 1)
        v.tensor_tensor(self.xs[:, :], self.ps_o[:, 0:P], one(t.X, g), ALU.add).then_inc(self.xs_ready, 1)
        dve.wait_ge(self.xs_ready, g + 1)
        self.k.link(v.bn_stats(self.stats[:, :], self.xs[:, :]))
        dve.sem_inc(self.sem_passed, 1)
        self.k.link(v.bn_aggr(self.mv[:, :], self.stats[:, :]))
        v.tensor_scalar(self.roots[:, 0:1], self.mv[:, 1:2], EPS, None, ALU.add)
        v.tensor_scalar(self.roots[:, 1:2], t.deg[:, bass.ds(g, 1)], 1.0, None, ALU.add).then_inc(self.var_ready, 1)

    def dve_norm(self, dve, g):
        t, v, k = self.t, self.nc.vector, self.k
        dve.wait_ge(self.sd_ready, g + 1)
        k.link(v.reciprocal(self.roots[:, :], self.roots[:, :]))
        v.tensor_scalar(t.dinv[:, bass.ds(g, 1)], self.roots[:, 1:2], 1.0, None, ALU.mult)
        k.link(v.tensor_scalar(self.r[:, :], self.xs[:, :], self.mv[:, 0:1], self.roots[:, 0:1], ALU.subtract, ALU.mult))
        v.tensor_scalar(self.hn[:, :], self.r[:, :], 0.0, None, ALU.max).then_inc(self.hn_ready, 1)

    def dve_parts(self, dve, g):
        t, v, k = self.t, self.nc.vector, self.k
        after(dve, self.parts_kept, 2 * g)
        dve.wait_ge(self.w1_done, g + 1)
        k.link(v.tensor_scalar(self.hp[:, :], self.ps_o[:, P:2 * P], self.roots[:, 1:2], None, ALU.mult))
        split(v, k, self.hp, self.r, self.parts, self.parts_ready)
        assert k.count == 8


def split(v, k, whole, r, parts, done):
    k.link(v.tensor_scalar(parts[:, 0, :], whole[:, :], 1.0, None, ALU.mult))
    k.link(v.tensor_tensor(r[:, :], whole[:, :], parts[:, 0, :], ALU.subtract))
    k.link(v.tensor_scalar(parts[:, 1, :], r[:, :], 1.0, None, ALU.mult))
    v.tensor_tensor(parts[:, 2, :], r[:, :], parts[:, 1, :], ALU.subtract).then_inc(done, 1)


def relational_layer(nc, io, t, layer, rows_in, rows_out):
    name = f"rel{layer}"
    with ExitStack() as ctx:
        sb = lambda n, s, d: ctx.enter_context(nc.sbuf_tensor(f"{name}_{n}", s, d))
        sem = lambda n: semaphore(nc, t, ctx, f"{name}_{n}")
        ps = lambda n: ctx.enter_context(nc.psum_tensor(f"{name}_{n}", [P, 512], F32))
        idx = [sb(f"idx{i}", [P, n * CHUNK], I32) for i, n in enumerate((2, 2, 4))]
        match = [sb(f"match{i}", [P, SPAN, WIN], F32) for i in range(2)]
        C = [sb(f"C{i}", [P, SPAN, NB, WIN], F32) for i in range(2)]
        Z = [sb(f"Z{i}", [P, P], F32) for i in range(2)]
        fin = Finish(nc, t, ctx, name, layer)
        ps_z = [ps("ps_z0"), ps("ps_z1")]
        ps_t = ps("ps_t")
        idx_ready = sem("idx_ready")
        ring_even, ring_odd = t.first_in if layer == 0 else (sem("ring_even"), sem("ring_odd"))
        z_done, t_done = sem("z_done"), sem("t_done")
        match_ready, c_ready, z_ready, zt_ready = sem("match_ready"), sem("c_ready"), sem("z_ready"), sem("zt_ready")
        passed = sem("waits_passed")
        ring = t.ring
        M = [sb(f"M{i}", [P, SPAN, AW], BF16) for i in range(2)]
        lo = [sb(f"lo{i}", [P, SPAN, P], BF16) for i in range(2)]
        A = sb("A", [P, SRC_BLOCKS, P], F16)
        ps_a = [ps("ps_a0"), ps("ps_a1")]
        m_ready, a_done, a_kept = sem("m_ready"), sem("a_done"), sem("a_kept")
        deg_done, deg_kept, a_out = sem("deg_done"), sem("deg_kept"), sem("a_out")
        co = Coefficients(nc, io, t, ctx, name) if layer == 0 else None
        if layer == 1:
            early_sum, ps_early = sb("early_sum", [P, P], F32), ps("ps_early")
            early_in = [sem(f"early_in{s}") for s in range(FIRST_SLOTS)]
            early_done, early_kept = sem("early_done"), sem("early_kept")
            early_summed = sem("early_summed")
        block = ctx.enter_context(nc.Block())
        AHEAD = 6

        def hold(eng, s, value):
            if isinstance(value, int) and value <= 0:
                return
            eng.wait_ge(s, value)
            eng.sem_inc(passed, 1)

        def groups(eng, body):
            for g in range(4):
                body(g // 2, g % 2)
            end = LATE if layer else 20
            with eng.Fori(2, end // 2) as pair:
                for parity in range(2):
                    body(pair, parity)
            for g in range(end, GROUPS):
                body(g // 2, g % 2)

        def early_slab(g, i):
            if layer == 1 and is_group(g, GROUPS - 1):
                return EARLY_SLABS - 2 if i == 6 else None
            if layer == 0 or not isinstance(g, int) or g < LATE or i not in range(0, 2 * EARLY_PER_GROUP, 2):
                return None
            n = (g - LATE) * EARLY_PER_GROUP + i // 2
            return n if n < EARLY_SLABS - 2 else None

        def slab(pair, parity):
            g = pair * 2 + parity
            if layer == 0:
                idle = is_group(pair, 0) or is_group(g, GROUPS - 1)
                return None if idle else (pair * 2 - 2, pair - 1, parity * WPG // 2, WPG // 2)
            if isinstance(g, int) and g < 4:
                return (GROUPS - 3, 1, GROUPS - 1, 3)[g], g, 0, WPG
            if isinstance(g, int) and g >= GROUPS - 7:
                if g > GROUPS - 3:
                    return None
                order = pair + 2 + parity
                if g == GROUPS - 7:
                    return g + 1, order, 0, WPG
                return 2 * order - 3, order, (1 - parity) * WPG // 2, WPG // 2
            return pair * 2 + 1, pair + 2, parity * WPG // 2, WPG // 2

        def window_built(built, i):
            if built is None or (built[3] < WPG and i % 2):
                return None
            return i if built[3] == WPG else built[2] + i // 2

        def completes(built):
            return built is not None and built[2] + built[3] == WPG

        def slabs_before(pair, parity):
            if is_group(pair, 0):
                return parity if layer else 0
            if layer == 0:
                return pair - 1
            g = pair * 2 + parity
            return 2 if is_group(g, 2) else pair + (2 + parity if isinstance(g, int) and g >= GROUPS - 7 else 2)

        def windows(g):
            return LAST_WINDOWS if is_group(g, GROUPS - 1) else WPG

        def chunks_next(pair, parity):
            if layer:
                return 0, 0
            if is_group(pair, 0) and parity == 0:
                return AHEAD, 6
            first = pair * 8 + (8 + 4 * parity)
            return first, max(0, min(4, ET_CHUNKS - first)) if isinstance(pair, int) else 4

        def chunk_made(count, i):
            n = i if count > 4 else i // 2 if i % 2 else count
            return n if n < count else None

        def quarter(pair, parity, m):
            return m // 4 if isinstance(m, int) else pair * 2 + (2 + parity)

        @block.gpsimd
        def _(pool):
            g_ = nc.gpsimd

            def stage(which, c):
                n = (2, 2, 4)[which] * CHUNK
                g_.tensor_copy(idx[which][:, :], t.idx[:, bass.ds(c * CHUNK, n)]).then_inc(idx_ready, 1)

            def chunk(m, s, is_end=False):
                c = m * SLOTS_RING + s
                hold(pool, z_done, (c - (SLOTS_RING - 2)) * WPC)
                landed = (ring_even, ring_odd)[s % 2]
                hold(pool, landed, (m * (SLOTS_RING // 2) + s // 2) * (CHUNK * 16))
                if s in (0, 2, 4):
                    hold(pool, idx_ready, m * 3 + (s // 2 - 2))
                if not is_end and s in (0, 2, 6):
                    stage({0: 1, 2: 2, 6: 0}[s], c + 2)
                which, start = (s // 2, s % 2) if s < 4 else (2, s - 4)
                for i in range(CHUNK):
                    if isinstance(c, int) and c * CHUNK + i >= GATHERED:
                        break
                    n = start * CHUNK + i
                    g_.indirect_dma_start(ring[:, s * CHUNK + i, :], None, rows_in,
                                          bass.IndirectOffsetOnAxis(ap=idx[which][:, n:n + 1], axis=0)).then_inc(landed, 16)

            for c in range(FIRST_TILES // CHUNK if layer == 0 else 0, SLOTS_RING):
                landed = (ring_even, ring_odd)[c % 2]
                hold(pool, landed, c // 2 * CHUNK * 16)
                if c == SLOTS_RING - 2:
                    stage(0, SLOTS_RING)
                for i in range(c * CHUNK, (c + 1) * CHUNK):
                    g_.indirect_dma_start(ring[:, i, :], None, rows_in, bass.IndirectOffsetOnAxis(ap=t.idx[:, i:i + 1], axis=0))\
                      .then_inc(landed, 16)
            with pool.Fori(1, CHUNKS // SLOTS_RING) as m:
                for s in range(SLOTS_RING):
                    chunk(m, s)
            for s in range(CHUNKS % SLOTS_RING):
                chunk(CHUNKS // SLOTS_RING, s, is_end=True)

        if layer == 0:
            @block.sync
            def _(sp):
                for m in range(AHEAD):
                    co.load(sp, m, m % 4)

                def group(pair, parity):
                    first, count = chunks_next(pair, parity)
                    for i in range(count):
                        co.load(sp, first + i, (first + i) % 4 if isinstance(first, int) else i)
                groups(sp, group)
        else:
            @block.sync
            def _(sp):
                for n in range(EARLY_SLABS):
                    if n % 2:
                        sp.wait_ge(a_out, (n if n < 4 else n // 2 + 2) * 16 + 16)
                    after(sp, early_done, n - (FIRST_SLOTS - 1))
                    sp.dma_start(flat(t.slots[n % FIRST_SLOTS][:, 0:EARLY_BLOCKS, :]), t.A_dram[n, :, 0:EARLY_BLOCKS * P]).then_inc(early_in[n % FIRST_SLOTS], 16)
                sp.wait_ge(early_done, EARLY_SLABS)
                for s in range(FIRST_SLOTS):
                    sp.dma_start(flat(t.slots[s][:, EARLY_BLOCKS:, :]), t.A_dram[s, :, EARLY_BLOCKS * P:]).then_inc(t.a_in[s], 16)

        @block.vector
        def _(dve):
            v = nc.vector
            if layer == 0:
                for m in range(AHEAD):
                    co.make_onehot(dve, m, m // 4, m % 4)
                    if m:
                        co.scale(dve, m - 1)
                co.scale(dve, AHEAD - 1)
            regs = [dve.alloc_register(f"{name}_first{i}") for i in range(WPG)]
            slab_regs = [dve.alloc_register(f"{name}_slab_first{i}") for i in range(WPG)]

            def build_factors(j, bj, i, start):
                s = i % 2
                after(dve, a_done, bj - 1)
                for k in range(SPAN):
                    tile = bass.ds(start + k, 1)
                    v.tensor_scalar(M[s][:, k, :], t.keys400[:, :], t.win512[:, bass.ds(j, 1)], t.key[:, tile],
                                    ALU.add, ALU.is_equal)
                    ins = v.tensor_scalar(lo[s][:, k, :], t.iota128[:, :], t.src_lo[:, tile], None, ALU.is_equal)
                ins.then_inc(m_ready, 1)

            def match_nodes(j, i, start):
                s = i % 2
                tiles = bass.ds(start, SPAN)
                shape = [P, SPAN, WIN]
                v.scalar_tensor_tensor(out=match[s][:, :, :], in0=t.dst[:, tiles].unsqueeze(2).to_broadcast(shape),
                                       scalar=t.neg_win[:, bass.ds(j, 1)],
                                       in1=t.iota16[:, :].unsqueeze(1).to_broadcast(shape),
                                       op0=ALU.add, op1=ALU.is_equal).then_inc(match_ready, 1)

            def weigh(j, i, start):
                s, tiles = i % 2, bass.ds(start, SPAN)
                after(dve, z_done, j - 1)
                dve.wait_ge(match_ready, j + 1)
                shape = [P, SPAN, NB, WIN]
                v.tensor_tensor(C[s][:, :, :, :], match[s][:, :, :].unsqueeze(2).to_broadcast(shape),
                                t.coef[layer][:, tiles, :].unsqueeze(3).to_broadcast(shape), ALU.mult).then_inc(c_ready, 1)

            def keep_early(g, n):
                dve.wait_ge(early_done, n + 1)
                v.tensor_reduce(early_sum[:, :], ps_early[:, 0:3 * P].rearrange("p (c n) -> p n c", c=3), AX.X, ALU.add)\
                 .then_inc(early_summed, 1)
                dve.wait_ge(fin.parts_kept, 2 * (g - 1))
                dve.wait_ge(early_summed, 2 * n + 1)
                v.tensor_tensor(early_sum[:, :], early_sum[:, :], t.HP[0][:, n, :], ALU.add).then_inc(early_summed, 1)
                dve.wait_ge(early_summed, 2 * n + 2)
                v.scalar_tensor_tensor(out=t.HP[1][:, n, :], in0=early_sum[:, :], scalar=t.dinv[:, n:n + 1],
                                       in1=t.bias_all[0][:, :], op0=ALU.mult, op1=ALU.add).then_inc(early_kept, 1)

            def keep_deg(g, order):
                dve.wait_ge(deg_done, order + 1)
                v.tensor_scalar(t.deg[:, bass.ds(g, 1)], fin.ps_h[:, 2 * P:2 * P + 1], 1.0, None, ALU.mult).then_inc(deg_kept, 1)

            def finish(g, pair, parity, i):
                built = slab(pair, parity)
                if i == layer and completes(built):
                    keep_deg(built[0], built[1])
                if layer == 0:
                    return
                if i == 1:
                    fin.dve_x(dve, g)
                elif i == 3:
                    fin.dve_norm(dve, g)
                elif i == 7:
                    fin.dve_parts(dve, g)

            def group(pair, parity):
                g = pair * 2 + parity
                dve.load(regs, t.first[0:1, bass.ds(g * WPG, WPG)])
                starts = [dve.snap(r, min_val=0, max_val=TILES - SPAN) for r in regs]
                built = slab(pair, parity)
                if built:
                    dve.load(slab_regs[0:built[3]], t.first[0:1, bass.ds(built[0] * WPG + built[2], built[3])])
                    slab_starts = [dve.snap(r, min_val=0, max_val=TILES - SPAN) for r in slab_regs[0:built[3]]]
                made, chunks = chunks_next(pair, parity)
                if layer == 0:
                    dve.wait_ge(co.coef_ready, min(made, ET_CHUNKS) if isinstance(made, int) else made)
                for i in range(WPG):
                    n = chunk_made(chunks, i)
                    if n is not None:
                        m = made + n
                        co.make_onehot(dve, m, quarter(pair, parity, m), m % 4 if isinstance(m, int) else n % 4)
                    if i < windows(g):
                        match_nodes(g * WPG + i, i, starts[i])
                    w = window_built(built, i)
                    if w is not None:
                        build_factors(built[0] * WPG + w, built[1] * WPG + w, w, slab_starts[w - built[2]])
                    if i < windows(g):
                        weigh(g * WPG + i, i, starts[i])
                    if i and chunk_made(chunks, i - 1) is not None:
                        co.scale(dve, made + chunk_made(chunks, i - 1))
                    if not (isinstance(g, int) and g == 0):
                        finish(g - 1, pair - (1 - parity), 1 - parity, i)
                    begun = early_slab(g, i - 2) if i >= 2 else early_slab(g - 1, i + 6)
                    if begun is not None:
                        keep_early(g, begun)
                if early_slab(g, WPG - 2) == EARLY_SLABS - 2:
                    keep_early(g, EARLY_SLABS - 2)
                if chunk_made(chunks, WPG - 1) is not None:
                    co.scale(dve, made + chunk_made(chunks, WPG - 1))
            groups(dve, group)
            for i in range(WPG):
                finish(GROUPS - 1, GROUPS // 2, 0, i)
                if layer == 1 and i == 3:
                    keep_early(GROUPS, EARLY_SLABS - 1)

        @block.tensor
        def _(pe):
            m_ = nc.tensor
            if layer == 0:
                for m in range(AHEAD):
                    co.multiply(pe, m, m % 2)
            regs = [pe.alloc_register(f"{name}_pos{i}") for i in range(SPAN)]

            def early(n):
                pe.wait_ge(fin.parts_kept, 2 * EARLY_BLOCKS)
                pe.wait_ge(early_in[n % FIRST_SLOTS], (n // FIRST_SLOTS + 1) * 16)
                after(pe, early_kept, n)
                for b in range(EARLY_BLOCKS):
                    ins = m_.matmul(ps_early[:, 0:3 * P], t.slots[n % FIRST_SLOTS][:, b, :],
                                    t.S[0][:, b, :, :].rearrange("p c n -> p (c n)"), start=(b == 0), stop=(b == EARLY_BLOCKS - 1))
                ins.then_inc(early_done, 1)

            def turn(g, i):
                j = g * WPG + i
                pe.wait_ge(z_ready, j + 1)
                after(pe, zt_ready, j)
                m_.transpose(ps_t[:, 0:P], Z[i % 2][:, :], t.ident[:, :]).then_inc(t_done, 1)

            def group(pair, parity):
                g = pair * 2 + parity
                is_last, is_first, built = is_group(g, GROUPS - 1), is_group(g, 0), slab(pair, parity)
                after(pe, deg_kept, slabs_before(pair, parity))
                fin.pe_turn(pe, g)
                for i in range(WPG):
                    if i < windows(g):
                        j, s = g * WPG + i, i % 2
                        pe.load(regs, t.pos[0:1, bass.ds(j, 1), 0:SPAN].rearrange("p a b -> p (a b)"))
                        at = [pe.snap(r, min_val=0, max_val=RING - 1) for r in regs]
                        if i % WPC == 0:
                            n = WPG // WPC * g + (i // WPC + 1)
                            landed = (ring_even, ring_odd)[(i // WPC + 1) % 2]
                            if is_first and i == 0:
                                pe.wait_ge(ring_even, 16 * CHUNK)
                            if not (isinstance(n, int) and n >= CHUNKS):
                                rounds = g * (WPG // WPC // 2) + (i // WPC + 1) // 2 + 1
                                absent = TILES - GATHERED if is_group(n, CHUNKS - 1) else 0
                                pe.wait_ge(landed, rounds * (16 * CHUNK) - 16 * absent)
                        after(pe, z_ready, j - 1)
                        pe.wait_ge(c_ready, j + 1)
                        for k in range(SPAN):
                            ins = m_.matmul(ps_z[s][:, 0:P], C[s][:, k, :, :].rearrange("p b w -> p (b w)"), one(ring, at[k]),
                                            start=(k == 0), stop=(k == SPAN - 1))
                        ins.then_inc(z_done, 1)
                    w = window_built(built, i)
                    if w is not None:
                        bj, s = built[1] * WPG + w, w % 2
                        after(pe, a_kept, bj - 1)
                        pe.wait_ge(m_ready, bj + 1)
                        for k in range(SPAN):
                            ins = m_.matmul(ps_a[s][:, 0:AW], lo[s][:, k, :], M[s][:, k, :], start=(k == 0), stop=(k == SPAN - 1))
                        ins.then_inc(a_done, 1)
                    made, chunks = chunks_next(pair, parity)
                    n = chunk_made(chunks, i)
                    if n is not None:
                        co.multiply(pe, made + n, n % 2)
                    if 0 < i <= windows(g):
                        turn(g, i - 1)
                    if layer == 1 and not is_first:
                        if i == 4:
                            pe.wait_ge(fin.hT_ready, g + 1)
                            fin.pe_turn_new(pe, g - 1)
                        if i == 6:
                            fin.pe_w1(pe, g - 1)
                    if early_slab(g, i) is not None:
                        early(early_slab(g, i))
                if windows(g) == WPG:
                    turn(g, WPG - 1)
                pe.wait_ge(zt_ready, g * WPG + windows(g))
                fin.pe_out(pe, g)
                if completes(built):
                    pe.wait_ge(a_kept, (built[1] + 1) * WPG)
                    for b in range(SRC_BLOCKS):
                        ins = m_.matmul(fin.ps_h[:, 2 * P:2 * P + 1], A[:, b, :], t.ones16[:, 0:1],
                                        start=(b == 0), stop=(b == SRC_BLOCKS - 1))
                    ins.then_inc(deg_done, 1)
            groups(pe, group)
            if layer == 1:
                early(EARLY_SLABS - 1)
                fin.pe_turn_new(pe, GROUPS - 1)
                fin.pe_w1(pe, GROUPS - 1)

        @block.scalar
        def _(act):
            s_ = nc.scalar

            def keep_zt(g, i):
                j = g * WPG + i
                hold(act, t_done, j + 1)
                if i == 0:
                    hold(act, fin.out_done, g)
                s_.activation(fin.ZT[:, :, i * WIN:(i + 1) * WIN],
                              ps_t[:, 0:P].rearrange("p (b w) -> p b w", b=NB), ACT.Copy).then_inc(zt_ready, 1)

            def finish(g, i):
                if layer == 0 and i == 0:
                    fin.act_relu(act, g, rows_out)
                if layer == 1 and i == 1:
                    fin.act_x(act, g)
                if layer == 1 and i == 5:
                    fin.act_hnT(act, g)
                if layer == 1 and i == 7:
                    fin.act_parts(act, g)

            def group(pair, parity):
                g = pair * 2 + parity
                built = slab(pair, parity)
                fin.act_stage(act, g)
                for i in range(WPG):
                    j, s = g * WPG + i, i % 2
                    if i < windows(g):
                        hold(act, z_done, j + 1)
                        hold(act, t_done, j - 1)
                        s_.activation(Z[s][:, :], ps_z[s][:, 0:P], ACT.Copy).then_inc(z_ready, 1)
                    w = window_built(built, i)
                    if w is not None:
                        if w == 0:
                            hold(act, deg_done, built[1])
                            hold(act, a_out, built[1] * 16)
                        hold(act, a_done, built[1] * WPG + (w + 1))
                        s_.activation(A[:, :, w * WIN:(w + 1) * WIN],
                                      ps_a[w % 2][:, 0:AW].rearrange("p (b w) -> p b w", w=WIN), ACT.Copy).then_inc(a_kept, 1)
                    if 0 < i <= windows(g):
                        keep_zt(g, i - 1)
                    if not (isinstance(g, int) and g == 0):
                        finish(g - 1, i)
                if windows(g) == WPG:
                    keep_zt(g, WPG - 1)
                if completes(built):
                    hold(act, a_kept, (built[1] + 1) * WPG)
                    act.dma_start(t.A_dram[bass.ds(built[0], 1), :, :].rearrange("a p n -> (a p) n"),
                                  A[:, :, :].rearrange("p b n -> p (b n)")).then_inc(a_out, 16)
            groups(act, group)
            for i in range(WPG):
                finish(GROUPS - 1, i)
            act.wait_ge(a_out, 16 * (14 if layer else 11))
            if layer == 0:
                act.wait_ge(fin.rows_out, 16 * GROUPS)


def dense_layer(nc, t, layer, out):
    name = f"gcn{layer}"
    last = layer == 1
    with ExitStack() as ctx:
        sb = lambda n, s, d: ctx.enter_context(nc.sbuf_tensor(f"{name}_{n}", s, d))
        sem = lambda n: semaphore(nc, t, ctx, f"{name}_{n}")
        ps = lambda n: ctx.enter_context(nc.psum_tensor(f"{name}_{n}", [P, 512], F32))
        A = t.slots
        z = [sb(f"z{s}", [P, P], F32) for s in range(SLOTS)]
        ps_g = t.ps_g
        tail = DenseTail(nc, t, ctx, name, last)
        a_in, ahead = t.a_in, layer * (GROUPS // SLOTS)
        agg_done = sem("agg_done")
        chain = sem("chain")
        z_out = [sem(f"z_out{s}") for s in range(SLOTS)]
        block = ctx.enter_context(nc.Block())

        def slots(eng, body):
            rounds = GROUPS // SLOTS
            for s in range(SLOTS):
                body(s, s, 0)
            with eng.Fori(1, rounds - 1) as m:
                for s in range(SLOTS):
                    body(m * SLOTS + s, s, m)
            for s in range(SLOTS):
                body((rounds - 1) * SLOTS + s, s, rounds - 1)

        @block.sync
        def _(sp):
            def load(g, s, m):
                if isinstance(m, int) and m == 0 and (last or s < FIRST_SLOTS):
                    return
                after(sp, agg_done, g - (SLOTS - 1))
                b0 = EARLY_BLOCKS if not last and begun_early(g) else 0
                sp.dma_start(A[s][:, b0:, :].rearrange("p b n -> p (b n)"),
                             t.A_dram[bass.ds(g, 1), :, b0 * P:].rearrange("a p n -> (a p) n")).then_inc(a_in[s], 16)
            slots(sp, load)
            for s in range(0 if last else SLOTS):
                sp.wait_ge(agg_done, GROUPS - SLOTS + s + 1)
                sp.dma_start(flat(A[s][:, :, :]), t.A_dram[s, :, :]).then_inc(a_in[s], 16)

        @block.tensor
        def _(pe):
            def group(g, s, m):
                pe.wait_ge(a_in[s], (m + (1 + ahead)) * 16)
                after(pe, tail.z_ready, g - (SLOTS - 1))
                carried = CARRIED_BLOCKS if last and isinstance(g, int) and g < CARRIED_SLABS else 0
                b0 = EARLY_BLOCKS if not last and begun_early(g) else carried
                for b in range(b0, SRC_BLOCKS):
                    ins = nc.tensor.matmul(ps_g[s][:, 0:3 * P], A[s][:, b, :], t.S[layer][:, b, :, :].rearrange("p c n -> p (c n)"),
                                           start=(b == b0 and not carried), stop=(b == SRC_BLOCKS - 1))
                ins.then_inc(agg_done, 1)
                if not last:
                    tail.pe_multiply(pe, g - 2)
                    tail.pe_turn(pe, g - 1, z[(s - 1) % SLOTS])
            slots(pe, group)
            if not last:
                def begin_next(s, b0, b1):
                    pe.wait_ge(a_in[s], (1 + GROUPS // SLOTS) * 16)
                    pe.wait_ge(tail.z_ready, GROUPS - SLOTS + s + 1)
                    pe.wait_ge(tail.parts_kept, CARRIED_BLOCKS + PARTS_BIAS)
                    for b in range(b0, b1):
                        nc.tensor.matmul(ps_g[s][:, 0:3 * P], A[s][:, b, :], t.S[1][:, b, :, :].rearrange("p c n -> p (c n)"),
                                         start=(b == 0), stop=False)

                tail.pe_multiply(pe, GROUPS - 2)
                begin_next(0, 0, CARRIED_BLOCKS // 2)
                tail.pe_turn(pe, GROUPS - 1, z[(GROUPS - 1) % SLOTS])
                begin_next(0, CARRIED_BLOCKS // 2, CARRIED_BLOCKS)
                tail.pe_multiply(pe, GROUPS - 1)
                begin_next(1, 0, CARRIED_BLOCKS)

        @block.scalar
        def _(act):
            def group(g, s, m):
                if last:
                    tail.store(act, g, z[s], out, z_out[s])
                else:
                    tail.act(act, g, s)
            if not last:
                act.sem_inc(tail.parts_kept, PARTS_BIAS)
            slots(act, group)
            if not last:
                for g in range(GROUPS, GROUPS + 4):
                    tail.act(act, g, g % SLOTS)
            if last:
                for s in range(SLOTS):
                    act.wait_ge(z_out[s], (GROUPS // SLOTS) * 16)

        @block.vector
        def _(dve):
            v = nc.vector

            def group(g, s, m):
                dve.wait_ge(agg_done, g + 1)
                if last:
                    after(dve, z_out[s], m * 16)
                reduced = v.tensor_reduce(z[s][:, :], ps_g[s][:, 0:3 * P].rearrange("p (c n) -> p n c", c=3), AX.X, ALU.add)
                if last:
                    k = Chain(dve, chain, 3 * g)
                    k.link(reduced)
                    tail.combine(dve, v, k, g, z[s])
                    return
                old = None if isinstance(g, int) and g < 3 else g - 3
                reduced.then_inc(chain, 1)
                if old is not None:
                    tail.split_begin(dve, old, (s - 3) % SLOTS)
                dve.wait_ge(chain, g + 1)
                dve.sem_inc(tail.passed, 1)
                if begun_early(g):
                    tail.scale_add(v, g, z[s], one(t.HP[1], g)).then_inc(tail.z_ready, 1)
                else:
                    v.tensor_tensor(z[s][:, :], z[s][:, :], one(t.HP[0], g), ALU.add).then_inc(chain, 1)
                    dve.wait_ge(chain, g + 2)
                    tail.scale_add(v, g, z[s], t.bias_all[0][:, :]).then_inc(tail.z_ready, 1)
                if old is not None:
                    tail.split_rest(dve, old, (s - 3) % SLOTS)
                    tail.split_second(dve, old, (s - 3) % SLOTS)
                    tail.split_third(dve, old, (s - 3) % SLOTS)
            slots(dve, group)
            if not last:
                for g in range(GROUPS - 3, GROUPS):
                    tail.split_begin(dve, g, g % SLOTS)
                    tail.split_rest(dve, g, g % SLOTS)
                    tail.split_second(dve, g, g % SLOTS)
                    tail.split_third(dve, g, g % SLOTS)


class DenseTail:

    def __init__(self, nc, t, ctx, name, last):
        self.nc, self.t, self.last = nc, t, last
        sem = lambda n: semaphore(nc, t, ctx, f"{name}_{n}")
        self.z_ready, self.passed = sem("z_ready"), sem("waits_passed")
        self.layer = 1 if last else 0
        if not last:
            sb = lambda n, s, d: ctx.enter_context(nc.sbuf_tensor(f"{name}_{n}", s, d))
            ps = lambda n: ctx.enter_context(nc.psum_tensor(f"{name}_{n}", [P, 512], F32))
            self.zT, self.hp, self.r = sb("zT", [P, P], F32), sb("hp", [P, P], F32), sb("r", [P, P], F32)
            self.parts = [sb(f"parts{s}", [P, 3, P], BF16) for s in range(SLOTS)]
            self.ps_t, self.ps_o = ps("ps_t"), ps("ps_o")
            self.turned, self.zT_ready, self.w_done = sem("turned"), sem("zT_ready"), sem("w_done")
            self.parts_ready, self.parts_kept, self.chain = sem("parts_ready"), sem("parts_kept"), sem("split_chain")
            self.hp_kept = sem("hp_kept")

    def scale_add(self, v, g, z, rest):
        return v.scalar_tensor_tensor(out=z[:, :], in0=z[:, :], scalar=self.t.dinv[:, bass.ds(g, 1)], in1=rest,
                                      op0=ALU.mult, op1=ALU.add)

    def combine(self, dve, v, k, g, z):
        t = self.t
        k.link(v.tensor_tensor(z[:, :], z[:, :], one(t.HP[self.layer], g), ALU.add))
        ins = self.scale_add(v, g, z, t.bias_all[self.layer][:, :])
        if self.last:
            k.link(ins)
            v.tensor_tensor(z[:, :], z[:, :], one(t.X, g), ALU.add).then_inc(self.z_ready, 1)
        else:
            ins.then_inc(self.z_ready, 1)

    def pe_turn(self, pe, g, z):
        if isinstance(g, int) and g < 0:
            return
        after(pe, self.zT_ready, g)
        pe.wait_ge(self.z_ready, g + 1)
        self.nc.tensor.transpose(self.ps_t[:, 0:P], z[:, :], self.t.ident[:, :]).then_inc(self.turned, 1)

    def hold(self, act, sem, value):
        if isinstance(value, int) and value <= 0:
            return
        act.wait_ge(sem, value)
        act.sem_inc(self.passed, 1)

    def store(self, act, g, z, out, done):
        rows = LAST_ROWS if isinstance(g, int) and g == GROUPS - 1 else P
        self.hold(act, self.z_ready, g + 1)
        act.dma_start(out[bass.ds(g * P, rows), :], z[0:rows, :]).then_inc(done, 16)

    def act(self, act, g, slot):
        hold = lambda sem, value: self.hold(act, sem, value)
        t, s = self.t, self.nc.scalar
        exists = lambda g: not isinstance(g, int) or 0 <= g < GROUPS
        if exists(g - 2):
            hold(self.w_done, g - 1)
            s.activation(one(t.HP[1], g - 2), self.ps_o[:, 0:P], ACT.Copy, scale=t.dinv[:, bass.ds(g - 2, 1)]).then_inc(self.hp_kept, 1)
        if exists(g - 1):
            hold(self.w_done, g - 1)
            hold(self.turned, g)
            s.activation(self.zT[:, :], self.ps_t[:, 0:P], ACT.Relu).then_inc(self.zT_ready, 1)
        if exists(g - 4):
            hold(self.parts_ready, g - 3)
            out = t.S[1][:, bass.ds(g - 4, 1), :, :].rearrange("p a b c -> p (a b) c")
            s.activation(out, self.parts[(slot - 4) % SLOTS][:, :, :], ACT.Copy).then_inc(self.parts_kept, 1)

    def pe_multiply(self, pe, g):
        if isinstance(g, int) and g < 0:
            return
        pe.wait_ge(self.zT_ready, g + 1)
        after(pe, self.hp_kept, g)
        self.nc.tensor.matmul(self.ps_o[:, 0:P], self.zT[:, :], self.t.W[3][:, :], start=True, stop=True).then_inc(self.w_done, 1)

    def split_begin(self, dve, g, s):
        after(dve, self.parts_kept, g - (SLOTS - 1) + PARTS_BIAS)
        dve.wait_ge(self.hp_kept, g + 1)
        dve.sem_inc(self.passed, 1)
        self.nc.vector.tensor_scalar(self.parts[s][:, 0, :], one(self.t.HP[1], g), 1.0, None, ALU.mult).then_inc(self.chain, 1)

    def split_rest(self, dve, g, s):
        dve.wait_ge(self.chain, 3 * g + 1)
        dve.sem_inc(self.passed, 1)
        self.nc.vector.tensor_tensor(self.r[:, :], one(self.t.HP[1], g), self.parts[s][:, 0, :], ALU.subtract).then_inc(self.chain, 1)

    def split_second(self, dve, g, s):
        dve.wait_ge(self.chain, 3 * g + 2)
        self.nc.vector.tensor_scalar(self.parts[s][:, 1, :], self.r[:, :], 1.0, None, ALU.mult).then_inc(self.chain, 1)

    def split_third(self, dve, g, s):
        dve.wait_ge(self.chain, 3 * g + 3)
        self.nc.vector.tensor_tensor(self.parts[s][:, 2, :], self.r[:, :], self.parts[s][:, 1, :], ALU.subtract).then_inc(self.parts_ready, 1)


def any_order_coefficients(nc, io, t):
    with ExitStack() as ctx:
        co = Coefficients(nc, io, t, ctx, "any_coef")
        block = ctx.enter_context(nc.Block())

        def chunks(eng, step):
            for m in range(4):
                step(m, 0, m)
            with eng.Fori(1, ET_CHUNKS // 4) as four:
                for s in range(4):
                    step(four * 4 + s, four, s)
            for m in range(ET_CHUNKS // 4 * 4, ET_CHUNKS):
                step(m, m // 4, m % 4)

        @block.sync
        def _(sp):
            chunks(sp, lambda m, quarter_m, s: co.load(sp, m, s))

        @block.tensor
        def _(pe):
            chunks(pe, lambda m, quarter_m, s: co.multiply(pe, m, s % 2))

        @block.vector
        def _(dve):
            def step(m, quarter_m, s):
                co.make_onehot(dve, m, quarter_m, s)
                co.scale(dve, m)
            chunks(dve, step)


class AnyOrder:

    def __init__(self, nc, t, ctx, name, rows_in):
        self.nc, self.t, self.rows_in, self.name = nc, t, rows_in, name
        sb = lambda n, s, d: ctx.enter_context(nc.sbuf_tensor(f"{name}_{n}", s, d))
        sem = lambda n: semaphore(nc, t, ctx, f"{name}_{n}")
        self.idx, self.rows = sb("idx", [P, 1], I32), sb("rows", [P, D], F32)
        self.match = sb("match", [P, P], F32)
        self.idx_ready, self.landed, self.done, self.passed = sem("idx_ready"), sem("landed"), sem("done"), sem("pool_waits_passed")
        self.match_ready, self.factor_ready, self.sum_ready = sem("match_ready"), sem("factor_ready"), sem("sum_ready")
        self.cleared, self.dve_passed = sem("cleared"), sem("dve_waits_passed")

    def gather(self, pool):
        with pool.Fori(0, GROUPS) as g:
            with pool.Fori(0, TILES) as tile:
                n = g * TILES + tile
                pool.wait_ge(self.done, n + 1)
                pool.sem_inc(self.passed, 1)
                self.nc.gpsimd.tensor_copy(self.idx[:, :], self.t.idx[:, bass.ds(tile, 1)]).then_inc(self.idx_ready, 1)
                pool.wait_ge(self.idx_ready, n + 1)
                pool.sem_inc(self.passed, 1)
                self.nc.gpsimd.indirect_dma_start(self.rows[:, :], None, self.rows_in,
                                                  bass.IndirectOffsetOnAxis(ap=self.idx[:, 0:1], axis=0)).then_inc(self.landed, 16)
            pool.wait_ge(self.done, (g + 1) * TILES + 1)
            pool.sem_inc(self.passed, 1)
            pool.inc_swdge_sem([self.landed], [TILES * 16], mode="sub")

    def wait_rows(self, pe, tile, n):
        pe.wait_ge(self.idx_ready, n + 1)
        pe.wait_ge(self.landed, (tile + 1) * 16)

    def one_hot(self, dve, g, tile, n):
        dve.wait_ge(self.done, n + 1)
        self.nc.vector.tensor_scalar(self.match[:, :], self.t.iota128[:, :], self.t.group_lo[:, bass.ds(g, 1)],
                                     self.t.dst[:, bass.ds(tile, 1)], ALU.add, ALU.is_equal).then_inc(self.match_ready, 1)
        dve.wait_ge(self.match_ready, n + 1)


def any_order_relational(nc, t, layer, rows_in, rows_out):
    name = f"any_rel{layer}"
    with ExitStack() as ctx:
        ps = lambda n: ctx.enter_context(nc.psum_tensor(f"{name}_{n}", [P, 512], F32))
        C = ctx.enter_context(nc.sbuf_tensor(f"{name}_C", [P, NB, P], F32))
        fin = Finish(nc, t, ctx, name, layer)
        way = AnyOrder(nc, t, ctx, name, rows_in)
        ps_z = [ps("ps_z0"), ps("ps_z1")]
        ps_d = ps("ps_d")
        block = ctx.enter_context(nc.Block())
        HB = NB // 2

        @block.gpsimd
        def _(pool):
            way.gather(pool)

        @block.tensor
        def _(pe):
            m_ = nc.tensor
            pe.sem_inc(way.done, 1)
            with pe.Fori(0, GROUPS) as g:
                pe.wait_ge(fin.staged, g + 1)
                m_.transpose(fin.ps_h[:, 0:P], fin.h_stage[:, :], t.ident[:, :]).then_inc(fin.turned, 1)
                with pe.Fori(0, TILES) as tile:
                    n = g * TILES + tile
                    way.wait_rows(pe, tile, n)
                    pe.wait_ge(way.factor_ready, n + 1)
                    if layer == 0:
                        m_.matmul(ps_d[:, 0:1], way.match[:, :], t.ones[:, 0:1], start=True, stop=True)
                    for h in range(2):
                        ins = m_.matmul(ps_z[h][:, :], way.rows[:, :], C[:, h * HB:(h + 1) * HB, :].rearrange("p b n -> p (b n)"),
                                        start=True, stop=True)
                    ins.then_inc(way.done, 1)
                pe.wait_ge(way.sum_ready, (g + 1) * TILES)
                fin.pe_out(pe, g)
                if layer == 1:
                    fin.pe_turn_new(pe, g)
                    fin.pe_w1(pe, g)

        @block.scalar
        def _(act):
            with act.Fori(0, GROUPS) as g:
                nc.scalar.activation(fin.h_stage[:, :], one(t.H, g), ACT.Copy).then_inc(fin.staged, 1)
                fin.hold(act, fin.turned, g + 1)
                nc.scalar.activation(fin.hT[:, :], fin.ps_h[:, 0:P], ACT.Copy).then_inc(fin.hT_ready, 1)
                if layer == 0:
                    fin.act_relu(act, g, rows_out)
                else:
                    fin.act_x(act, g)
                    fin.act_hnT(act, g)
                    fin.act_parts(act, g, rows_out)
            act.wait_ge(fin.rows_out, 16 * GROUPS)

        @block.vector
        def _(dve):
            v = nc.vector
            if layer == 0:
                v.memset(t.deg[:, :], 0.0).then_inc(way.cleared, 1)
                dve.wait_ge(way.cleared, 1)
            with dve.Fori(0, GROUPS) as g:
                v.memset(fin.ZT[:, :, :], 0.0).then_inc(way.cleared, 1)
                dve.wait_ge(way.cleared, g + (2 if layer == 0 else 1))
                dve.sem_inc(way.dve_passed, 1)
                with dve.Fori(0, TILES) as tile:
                    n = g * TILES + tile
                    way.one_hot(dve, g, tile, n)
                    shape = [P, NB, P]
                    v.tensor_tensor(C[:, :, :], way.match[:, :].unsqueeze(1).to_broadcast(shape),
                                    t.coef[layer][:, bass.ds(tile, 1), :].rearrange("p a b -> p (a b)").unsqueeze(2).to_broadcast(shape),
                                    ALU.mult).then_inc(way.factor_ready, 1)
                    dve.wait_ge(way.done, n + 2)
                    if layer == 0:
                        d = t.deg[:, bass.ds(g, 1)]
                        v.tensor_tensor(d, d, ps_d[:, 0:1], ALU.add)
                    for h in range(2):
                        z = flat(fin.ZT[:, h * HB:(h + 1) * HB, :])
                        ins = v.tensor_tensor(z, z, ps_z[h][:, :], ALU.add)
                    ins.then_inc(way.sum_ready, 1)
                if layer == 1:
                    fin.dve_x(dve, g)
                    fin.dve_norm(dve, g)
                    fin.dve_parts(dve, g)
                else:
                    dve.wait_ge(fin.out_done, g + 1)


def any_order_gcn(nc, t, layer, rows_in, rows_out, out):
    name = f"any_gcn{layer}"
    last = layer == 1
    with ExitStack() as ctx:
        z = ctx.enter_context(nc.sbuf_tensor(f"{name}_z", [P, P], F32))
        ps_g = ctx.enter_context(nc.psum_tensor(f"{name}_ps_g", [P, 512], F32))
        tail = DenseTail(nc, t, ctx, name, last)
        way = AnyOrder(nc, t, ctx, name, rows_in)
        chain, stored = semaphore(nc, t, ctx, f"{name}_chain"), semaphore(nc, t, ctx, f"{name}_stored")
        block = ctx.enter_context(nc.Block())

        def groups(eng, body):
            with eng.Fori(0, GROUPS - 1) as g:
                body(g)
            body(GROUPS - 1)

        @block.gpsimd
        def _(pool):
            way.gather(pool)

        @block.tensor
        def _(pe):
            pe.sem_inc(way.done, 1)

            def group(g):
                with pe.Fori(0, TILES) as tile:
                    n = tile + g * TILES
                    way.wait_rows(pe, tile, n)
                    pe.wait_ge(way.match_ready, n + 1)
                    nc.tensor.matmul(ps_g[:, 0:P], way.match[:, :], way.rows[:, :], start=True, stop=True).then_inc(way.done, 1)
                if not last:
                    pe.wait_ge(tail.z_ready, g + 1)
                    nc.tensor.transpose(tail.ps_t[:, 0:P], z[:, :], t.ident[:, :]).then_inc(tail.turned, 1)
                    pe.wait_ge(tail.zT_ready, g + 1)
                    nc.tensor.matmul(tail.ps_o[:, 0:P], tail.zT[:, :], t.W[3][:, :], start=True, stop=True).then_inc(tail.w_done, 1)
            groups(pe, group)

        @block.scalar
        def _(act):
            def group(g):
                if last:
                    tail.store(act, g, z, out, stored)
                else:
                    tail.hold(act, tail.turned, g + 1)
                    nc.scalar.activation(tail.zT[:, :], tail.ps_t[:, 0:P], ACT.Relu).then_inc(tail.zT_ready, 1)
                    tail.hold(act, tail.parts_ready, g + 1)
                    nc.scalar.activation(one(t.HP[1], g), tail.hp[:, :], ACT.Copy).then_inc(tail.parts_kept, 1)
                    tail.hold(act, tail.parts_kept, g + 1)
                    act.dma_start(rows_out[bass.ds(g * P, P), :], one(t.HP[1], g)).then_inc(stored, 16)
            groups(act, group)
            act.wait_ge(stored, 16 * GROUPS)

        @block.vector
        def _(dve):
            v = nc.vector

            def group(g):
                v.memset(z[:, :], 0.0).then_inc(way.cleared, 1)
                dve.wait_ge(way.cleared, g + 1)
                dve.sem_inc(way.dve_passed, 1)
                with dve.Fori(0, TILES) as tile:
                    n = tile + g * TILES
                    way.one_hot(dve, g, tile, n)
                    dve.wait_ge(way.done, n + 2)
                    v.tensor_tensor(z[:, :], z[:, :], ps_g[:, 0:P], ALU.add).then_inc(way.sum_ready, 1)
                    dve.wait_ge(way.sum_ready, n + 1)
                tail.combine(dve, v, Chain(dve, chain, (2 if last else 1) * g), g, z)
                if last:
                    dve.wait_ge(stored, (g + 1) * 16)
                else:
                    dve.wait_ge(tail.w_done, g + 1)
                    v.tensor_scalar(tail.hp[:, :], tail.ps_o[:, 0:P], t.dinv[:, bass.ds(g, 1)], None, ALU.mult)\
                     .then_inc(tail.parts_ready, 1)
                    dve.wait_ge(tail.parts_kept, g + 1)
            groups(dve, group)


class Tensors:
    pass


def program(nc, io, out, force_slow=False):
    t = Tensors()
    t.numbers, t.first_branch, t.second_branch = [], False, False
    with ExitStack() as ctx:
        sb = lambda n, s, d: ctx.enter_context(nc.sbuf_tensor(n, s, d))
        dram = lambda n, s, d: nc.dram_tensor(n, s, d, kind="Internal").ap()
        t.h1_dram, t.h2_dram = dram("h1_rows", (GROUPS * P, D), F32), dram("h2_rows", (GROUPS * P, D), F32)
        t.A_dram = dram("A_slabs", (GROUPS, P, SRC_BLOCKS * P), F16)
        t.X, t.H = sb("X", [P, GROUPS, D], F32), sb("H", [P, GROUPS, D], F32)
        t.V = [sb(f"V{i}", [P, NB, D], F32) for i in range(2)]
        t.W = [sb(f"W{i}", [P, D], F32) for i in range(4)]
        t.bias_row = [sb(f"bias_row{i}", [1, D], F32) for i in range(2)]
        t.bias_all = [sb(f"bias_all{i}", [P, D], F32) for i in range(2)]
        t.ident, t.ones, t.ones16 = sb("ident", [P, P], F32), sb("ones", [P, P], F32), sb("ones16", [P, 2], F16)
        t.idx = sb("idx_table", [P, TILES], I32)
        t.dst, t.norm = sb("dst_table", [P, TILES], F32), sb("norm_table", [P, TILES], F32)
        t.src_lo, t.key = sb("src_lo_table", [P, TILES], F32), sb("key_table", [P, TILES], F32)
        t.comp = sb("comp_parts", [RH, 3, 2, 2 * NB], BF16)
        t.neg_win, t.win512 = sb("neg_win", [P, WINDOWS], F32), sb("win512", [P, WINDOWS], F32)
        t.group_lo = sb("group_lo", [P, GROUPS], F32)
        t.iota16, t.keys400, t.iota128 = sb("iota16", [P, WIN], F32), sb("keys400", [P, AW], F16), sb("iota128", [P, P], F16)
        t.type_id = sb("type_id", [P, 2], F32)
        t.pos, t.first, t.slow = sb("pos", [1, WINDOWS, SPAN], I32), sb("first", [1, WINDOWS], I32), sb("slow", [1, 1], I32)
        t.deg, t.dinv = sb("deg", [P, GROUPS], F32), sb("dinv", [P, GROUPS], F32)
        t.ring = sb("ring", [P, RING, D], F32)
        t.first_in = [ctx.enter_context(nc.semaphore(n)) for n in ("ring_even", "ring_odd")]

        prepare(nc, io, t)
        slow = nc.values_load(t.slow[0:1, 0:1], min_val=0, max_val=1)
        hp_rows = [dram(f"hp_rows{i}", (GROUPS * P, D), F32) for i in range(2)]
        right = lambda c, n, s, d: c.enter_context(nc.sbuf_tensor(n, s, d, side="right"))
        left = lambda c, n, s, d: c.enter_context(nc.sbuf_tensor(n, s, d))
        t.HP, t.S = [None, None], [None, None]
        t.first_branch = True
        with nc.If(slow == 0):
            with ExitStack() as parts:
                t.a_in = [semaphore(nc, t, parts, f"slab_in{s}") for s in range(SLOTS)]
                with ExitStack() as edges:
                    t.coef = [None, left(edges, "coef1", [P, TILES, NB], F32)]
                    with ExitStack() as first_layer:
                        t.coef[0] = left(first_layer, "coef0", [P, TILES, NB], F32)
                        relational_layer(nc, io, t, 0, t.h1_dram, t.h2_dram)
                    t.HP = [t.H, right(parts, "hp1", [P, GROUPS, D], F32)]
                    t.S[0] = right(parts, "hp0_parts", [P, GROUPS, 3, D], BF16)
                    t.slots = [right(parts, f"A_slot{s}", [P, SRC_BLOCKS, P], F16) for s in range(FIRST_SLOTS)]
                    relational_layer(nc, io, t, 1, t.h2_dram, None)
                t.slots += [right(parts, f"A_slot{s}", [P, SRC_BLOCKS, P], F16) for s in range(FIRST_SLOTS, SLOTS)]
                t.S[1] = right(parts, "hp1_parts", [P, GROUPS, 3, D], BF16)
                t.ps_g = [parts.enter_context(nc.psum_tensor(f"ps_g{s}", [P, 512], F32)) for s in range(SLOTS)]
                dense_layer(nc, t, 0, out)
                dense_layer(nc, t, 1, out)
        t.first_branch, t.second_branch = False, True
        with nc.Else():
            with ExitStack() as parts:
                t.coef = [left(parts, f"any_coef{i}", [P, TILES, NB], F32) for i in range(2)]
                any_order_coefficients(nc, io, t)
                any_order_relational(nc, t, 0, t.h1_dram, t.h2_dram)
                t.HP = [left(parts, f"any_hp{i}", [P, GROUPS, D], F32) for i in range(2)]
                t.S = [left(parts, "any_parts", [P, GROUPS, 3, D], BF16), None]
                any_order_relational(nc, t, 1, t.h2_dram, hp_rows[0])
                any_order_gcn(nc, t, 0, hp_rows[0], hp_rows[1], out)
                any_order_gcn(nc, t, 1, hp_rows[1], None, out)


_INS = ["x", "src", "dst", "edge_type_200", "edge_weight1", "L0_gnn_V1", "L0_gnn_comp1", "L0_gnn_loop1", "L0_gnn_bias1",
        "L0_gnn_V2", "L0_gnn_comp2", "L0_gnn_loop2", "L0_gnn_bias2", "L1_gnn_W1", "L1_gnn_b1", "L1_gnn_W2", "L1_gnn_b2"]


def kernel(**inputs):
    import numpy as _np
    import concourse.bacc as _bacc
    from concourse import mybir as _mybir
    from concourse.bass_utils import run_bass_kernel_spmd as _run

    nc = _bacc.Bacc("TRN2", target_bir_lowering=False, num_devices=1)
    arrays, io = {}, {}
    for name in _INS:
        a = _np.ascontiguousarray(inputs[name])
        arrays[f"in_{name}_dram"] = a
        io[name] = nc.dram_tensor(f"in_{name}_dram", a.shape, _mybir.dt.from_np(a.dtype), kind="ExternalInput").ap()
    out = nc.dram_tensor("out_0_dram", (N, D), _mybir.dt.float32, kind="ExternalOutput").ap()
    program(nc, io, out)
    r = _run(nc, [arrays], core_ids=[0])
    return r.results[0]["out_0_dram"]
```
